# Optimizing a Trainium2 kernel written in Bass

```python
import numpy as np
import jax
import jax.numpy as jnp

def _softmax(x, axis=-1):
    return jax.nn.softmax(x, axis=axis)

def _gelu(x):
    return jax.nn.gelu(x, approximate=True)

def _silu(x):
    return jax.nn.silu(x)

def _sigmoid(x):
    return jax.nn.sigmoid(x)

def _layernorm(x, axis=-1, eps=1e-05):
    m = jnp.mean(x, axis=axis, keepdims=True)
    v = jnp.var(x, axis=axis, keepdims=True)
    return (x - m) / jnp.sqrt(v + eps)

def _scatter_add(tgt, idx, src, axis=0):
    return tgt.at[idx].add(src)

def _segment_sum(src, seg, n):
    return jax.ops.segment_sum(src, seg, n)
kernel_name = 'mk_early_fusion_d1_tok_img256_r4_9ddec7'

def setup_inputs(seed: int=0):
    np.random.seed(seed)
    _w = jnp.asarray

    def _rec_inputs():
        import jax
        import jax.numpy as jnp
        _rk = jax.random.key(seed)
        x = -0.00040386 + 0.999972 * jax.random.normal(jax.random.fold_in(_rk, 1), (8, 3, 64, 64), jnp.float32)
        txt = -0.0054313 + 0.191732 * jax.random.normal(jax.random.fold_in(_rk, 2), (8, 77, 64), jnp.float32)
        return (x, txt)
    x, txt = _rec_inputs()

    def _L0_tok_setup():
        import jax, jax.numpy as jnp
        import numpy as np
        EPS = 1e-05
        P = 8
        DIM = 64
        NUM_TOKENS = 64
        PATCH_DIM = 3 * P * P

        def layernorm(x, g, b):
            mu = jnp.mean(x, axis=-1, keepdims=True)
            var = jnp.mean(jnp.square(x - mu), axis=-1, keepdims=True)
            return (x - mu) * jax.lax.rsqrt(var + EPS) * g + b
        key = jax.random.key(seed)
        ks = jax.random.split(key, 8)
        b, c, h, w = (16, 3, 128, 128)
        x = jax.random.normal(ks[0], (b, c, h, w), dtype=jnp.float32)
        ln1_g = jnp.ones((PATCH_DIM,), jnp.float32)
        ln1_b = jnp.zeros((PATCH_DIM,), jnp.float32)
        W1 = jax.random.normal(ks[1], (PATCH_DIM, DIM), jnp.float32) * 0.02
        b1 = jnp.zeros((DIM,), jnp.float32)
        ln2_g = jnp.ones((DIM,), jnp.float32)
        ln2_b = jnp.zeros((DIM,), jnp.float32)
        Wp1 = jax.random.normal(ks[2], (DIM, DIM), jnp.float32) * 0.02
        bp1 = jnp.zeros((DIM,), jnp.float32)
        lnp_g = jnp.ones((DIM,), jnp.float32)
        lnp_b = jnp.zeros((DIM,), jnp.float32)
        Wp2 = jax.random.normal(ks[3], (DIM, NUM_TOKENS), jnp.float32) * 0.02
        bp2 = jnp.zeros((NUM_TOKENS,), jnp.float32)
        return {'x': x, 'ln1_g': ln1_g, 'ln1_b': ln1_b, 'W1': W1, 'b1': b1, 'ln2_g': ln2_g, 'ln2_b': ln2_b, 'Wp1': Wp1, 'bp1': bp1, 'lnp_g': lnp_g, 'lnp_b': lnp_b, 'Wp2': Wp2, 'bp2': bp2}
    _L0_tok_all = _L0_tok_setup()
    _L0_tok_in = {k: v for k, v in _L0_tok_all.items() if k in ('ln1_g', 'ln1_b', 'W1', 'b1', 'ln2_g', 'ln2_b', 'Wp1', 'bp1', 'lnp_g', 'lnp_b', 'Wp2', 'bp2')}
    del _L0_tok_all

    def _L0_attn_setup():
        import jax, jax.numpy as jnp
        import numpy as np
        B, T, D = (4, 512, 64)
        W_LORA, A_LORA, G_LORA = (64, 64, 128)
        DECAY_SCALE = -0.6065306597126334
        EPS = D * 1e-05

        def _forward(x, x_mix, W_r, W_k, W_v, W_o, A_w, B_w, b_w, A_a, B_a, b_a, A_g, B_g, k_k, k_a, r_k, gn_w, gn_b):
            b, t, d = x.shape
            shifted = jnp.pad(x, ((0, 0), (1, 0), (0, 0)))[:, :-1]
            delta = shifted - x
            xr, xw, xk, xv, xa, xg = [x + delta * x_mix[i] for i in range(6)]
            r = xr @ W_r
            w = DECAY_SCALE * jax.nn.sigmoid(jnp.tanh(xw @ A_w) @ B_w + b_w)
            k = xk @ W_k
            v = xv @ W_v
            a = jax.nn.sigmoid(xa @ A_a @ B_a + b_a)
            g = jax.nn.sigmoid(xg @ A_g) @ B_g
            kk = k * k_k
            kk = kk / jnp.maximum(jnp.linalg.norm(kk, axis=-1, keepdims=True), 1e-12)
            k = k * (1.0 + (a - 1.0) * k_a)
            decay = jnp.exp(w)

            def step(S, inp):
                r_t, dec_t, k_t, v_t, kk_t, a_t = inp
                b_t = kk_t * a_t
                sa = jnp.einsum('bvk,bk->bv', S, -kk_t)
                S = S * dec_t[:, None, :] + sa[:, :, None] * b_t[:, None, :] + v_t[:, :, None] * k_t[:, None, :]
                o_t = jnp.einsum('bvk,bk->bv', S, r_t)
                return (S, o_t)
            tm = lambda z: jnp.swapaxes(z, 0, 1)
            S0 = jnp.zeros((b, d, d), x.dtype)
            _, o = jax.lax.scan(step, S0, (tm(r), tm(decay), tm(k), tm(v), tm(kk), tm(a)))
            o = jnp.swapaxes(o, 0, 1)
            mu = jnp.mean(o, axis=-1, keepdims=True)
            var = jnp.var(o, axis=-1, keepdims=True)
            o = (o - mu) * jax.lax.rsqrt(var + EPS) * gn_w + gn_b
            o = o + jnp.sum(r * k * r_k, axis=-1, keepdims=True) * v
            return o * g @ W_o
        key = jax.random.key(seed)
        ks = jax.random.split(key, 20)
        n = jax.random.normal
        p = {}
        p['x'] = n(ks[0], (B, T, D), jnp.float32)
        p['x_mix'] = n(ks[1], (6, D), jnp.float32) * 0.1
        s = 1.0 / np.sqrt(D).astype(np.float32)
        p['W_r'] = n(ks[2], (D, D), jnp.float32) * s
        p['W_k'] = n(ks[3], (D, D), jnp.float32) * s
        p['W_v'] = n(ks[4], (D, D), jnp.float32) * s
        p['W_o'] = n(ks[5], (D, D), jnp.float32) * s
        p['A_w'] = n(ks[6], (D, W_LORA), jnp.float32) * s
        p['B_w'] = n(ks[7], (W_LORA, D), jnp.float32) / np.sqrt(W_LORA).astype(np.float32)
        p['b_w'] = n(ks[8], (D,), jnp.float32) * 0.5
        p['A_a'] = n(ks[9], (D, A_LORA), jnp.float32) * s
        p['B_a'] = n(ks[10], (A_LORA, D), jnp.float32) / np.sqrt(A_LORA).astype(np.float32)
        p['b_a'] = n(ks[11], (D,), jnp.float32) * 0.1
        p['A_g'] = n(ks[12], (D, G_LORA), jnp.float32) * s
        p['B_g'] = n(ks[13], (G_LORA, D), jnp.float32) / np.sqrt(G_LORA).astype(np.float32)
        p['k_k'] = n(ks[14], (D,), jnp.float32) * 0.5 + 0.85
        p['k_a'] = n(ks[15], (D,), jnp.float32) * 0.1 + 1.0
        p['r_k'] = n(ks[16], (D,), jnp.float32) * 0.1
        p['gn_w'] = jnp.ones((D,), jnp.float32)
        p['gn_b'] = jnp.zeros((D,), jnp.float32)
        return p
    _L0_attn_all = _L0_attn_setup()
    _L0_attn_in = {k: v for k, v in _L0_attn_all.items() if k in ('x_mix', 'W_r', 'W_k', 'W_v', 'W_o', 'A_w', 'B_w', 'b_w', 'A_a', 'B_a', 'b_a', 'A_g', 'B_g', 'k_k', 'k_a', 'r_k', 'gn_w', 'gn_b')}
    del _L0_attn_all

    def _L0_ffn_setup():
        import jax, jax.numpy as jnp
        import numpy as np
        D_MODEL = 64
        EXPERT_DIM = 128
        NUM_EXPERTS = 8
        TOP_K = 2
        SEQ_LEN = 512
        BATCH = 2
        key = jax.random.key(seed)
        ks = jax.random.split(key, 8)
        s = 0.02
        x = jax.random.normal(ks[0], (SEQ_LEN, BATCH, D_MODEL), dtype=jnp.float32)
        Wg = jax.random.normal(ks[1], (D_MODEL, NUM_EXPERTS), dtype=jnp.float32) * s
        bg = jax.random.normal(ks[2], (NUM_EXPERTS,), dtype=jnp.float32) * s
        bias = jnp.zeros((NUM_EXPERTS,), dtype=jnp.float32)
        W1 = jax.random.normal(ks[3], (NUM_EXPERTS, D_MODEL, EXPERT_DIM), dtype=jnp.float32) * s
        b1 = jax.random.normal(ks[4], (NUM_EXPERTS, EXPERT_DIM), dtype=jnp.float32) * s
        W2 = jax.random.normal(ks[5], (NUM_EXPERTS, EXPERT_DIM, D_MODEL), dtype=jnp.float32) * s
        b2 = jax.random.normal(ks[6], (NUM_EXPERTS, D_MODEL), dtype=jnp.float32) * s
        return {'x': x, 'Wg': Wg, 'bg': bg, 'bias': bias, 'W1': W1, 'b1': b1, 'W2': W2, 'b2': b2}
    _L0_ffn_all = _L0_ffn_setup()
    _L0_ffn_in = {k: v for k, v in _L0_ffn_all.items() if k in ('Wg', 'bg', 'bias', 'W1', 'b1', 'W2', 'b2')}
    del _L0_ffn_all
    return {'x': x, 'txt': txt, 'L0_tok_ln1_g': _L0_tok_in['ln1_g'], 'L0_tok_ln1_b': _L0_tok_in['ln1_b'], 'L0_tok_W1': _L0_tok_in['W1'], 'L0_tok_b1': _L0_tok_in['b1'], 'L0_tok_ln2_g': _L0_tok_in['ln2_g'], 'L0_tok_ln2_b': _L0_tok_in['ln2_b'], 'L0_tok_Wp1': _L0_tok_in['Wp1'], 'L0_tok_bp1': _L0_tok_in['bp1'], 'L0_tok_lnp_g': _L0_tok_in['lnp_g'], 'L0_tok_lnp_b': _L0_tok_in['lnp_b'], 'L0_tok_Wp2': _L0_tok_in['Wp2'], 'L0_tok_bp2': _L0_tok_in['bp2'], 'L0_attn_x_mix': _L0_attn_in['x_mix'], 'L0_attn_W_r': _L0_attn_in['W_r'], 'L0_attn_W_k': _L0_attn_in['W_k'], 'L0_attn_W_v': _L0_attn_in['W_v'], 'L0_attn_W_o': _L0_attn_in['W_o'], 'L0_attn_A_w': _L0_attn_in['A_w'], 'L0_attn_B_w': _L0_attn_in['B_w'], 'L0_attn_b_w': _L0_attn_in['b_w'], 'L0_attn_A_a': _L0_attn_in['A_a'], 'L0_attn_B_a': _L0_attn_in['B_a'], 'L0_attn_b_a': _L0_attn_in['b_a'], 'L0_attn_A_g': _L0_attn_in['A_g'], 'L0_attn_B_g': _L0_attn_in['B_g'], 'L0_attn_k_k': _L0_attn_in['k_k'], 'L0_attn_k_a': _L0_attn_in['k_a'], 'L0_attn_r_k': _L0_attn_in['r_k'], 'L0_attn_gn_w': _L0_attn_in['gn_w'], 'L0_attn_gn_b': _L0_attn_in['gn_b'], 'L0_ffn_Wg': _L0_ffn_in['Wg'], 'L0_ffn_bg': _L0_ffn_in['bg'], 'L0_ffn_bias': _L0_ffn_in['bias'], 'L0_ffn_W1': _L0_ffn_in['W1'], 'L0_ffn_b1': _L0_ffn_in['b1'], 'L0_ffn_W2': _L0_ffn_in['W2'], 'L0_ffn_b2': _L0_ffn_in['b2']}

def reference(x, txt, L0_tok_ln1_g, L0_tok_ln1_b, L0_tok_W1, L0_tok_b1, L0_tok_ln2_g, L0_tok_ln2_b, L0_tok_Wp1, L0_tok_bp1, L0_tok_lnp_g, L0_tok_lnp_b, L0_tok_Wp2, L0_tok_bp2, L0_attn_x_mix, L0_attn_W_r, L0_attn_W_k, L0_attn_W_v, L0_attn_W_o, L0_attn_A_w, L0_attn_B_w, L0_attn_b_w, L0_attn_A_a, L0_attn_B_a, L0_attn_b_a, L0_attn_A_g, L0_attn_B_g, L0_attn_k_k, L0_attn_k_a, L0_attn_r_k, L0_attn_gn_w, L0_attn_gn_b, L0_ffn_Wg, L0_ffn_bg, L0_ffn_bias, L0_ffn_W1, L0_ffn_b1, L0_ffn_W2, L0_ffn_b2):
    import jax
    import jax.numpy as jnp

    def _L0_tok_ref(x, ln1_g, ln1_b, W1, b1, ln2_g, ln2_b, Wp1, bp1, lnp_g, lnp_b, Wp2, bp2):
        import jax, jax.numpy as jnp
        import numpy as np
        EPS = 1e-05
        P = 8
        DIM = 64
        NUM_TOKENS = 64
        PATCH_DIM = 3 * P * P

        def layernorm(x, g, b):
            mu = jnp.mean(x, axis=-1, keepdims=True)
            var = jnp.mean(jnp.square(x - mu), axis=-1, keepdims=True)
            return (x - mu) * jax.lax.rsqrt(var + EPS) * g + b
        b, c, H, W = x.shape
        hp, wp = (H // P, W // P)
        patches = x.reshape(b, c, hp, P, wp, P)
        patches = jnp.transpose(patches, (0, 2, 4, 3, 5, 1))
        patches = patches.reshape(b, hp * wp, P * P * c)
        tokens = layernorm(patches, ln1_g, ln1_b)
        tokens = tokens @ W1 + b1
        tokens = layernorm(tokens, ln2_g, ln2_b)
        q = tokens
        k = tokens
        tokens = jnp.concatenate([q, k, tokens], axis=1)
        h1 = layernorm(tokens @ Wp1 + bp1, lnp_g, lnp_b)
        h1 = jax.nn.silu(h1)
        return h1 @ Wp2 + bp2

    def _L0_attn_ref(x, x_mix, W_r, W_k, W_v, W_o, A_w, B_w, b_w, A_a, B_a, b_a, A_g, B_g, k_k, k_a, r_k, gn_w, gn_b):
        import jax, jax.numpy as jnp
        import numpy as np
        B, T, D = (4, 512, 64)
        W_LORA, A_LORA, G_LORA = (64, 64, 128)
        DECAY_SCALE = -0.6065306597126334
        EPS = D * 1e-05

        def _forward(x, x_mix, W_r, W_k, W_v, W_o, A_w, B_w, b_w, A_a, B_a, b_a, A_g, B_g, k_k, k_a, r_k, gn_w, gn_b):
            b, t, d = x.shape
            shifted = jnp.pad(x, ((0, 0), (1, 0), (0, 0)))[:, :-1]
            delta = shifted - x
            xr, xw, xk, xv, xa, xg = [x + delta * x_mix[i] for i in range(6)]
            r = xr @ W_r
            w = DECAY_SCALE * jax.nn.sigmoid(jnp.tanh(xw @ A_w) @ B_w + b_w)
            k = xk @ W_k
            v = xv @ W_v
            a = jax.nn.sigmoid(xa @ A_a @ B_a + b_a)
            g = jax.nn.sigmoid(xg @ A_g) @ B_g
            kk = k * k_k
            kk = kk / jnp.maximum(jnp.linalg.norm(kk, axis=-1, keepdims=True), 1e-12)
            k = k * (1.0 + (a - 1.0) * k_a)
            decay = jnp.exp(w)

            def step(S, inp):
                r_t, dec_t, k_t, v_t, kk_t, a_t = inp
                b_t = kk_t * a_t
                sa = jnp.einsum('bvk,bk->bv', S, -kk_t)
                S = S * dec_t[:, None, :] + sa[:, :, None] * b_t[:, None, :] + v_t[:, :, None] * k_t[:, None, :]
                o_t = jnp.einsum('bvk,bk->bv', S, r_t)
                return (S, o_t)
            tm = lambda z: jnp.swapaxes(z, 0, 1)
            S0 = jnp.zeros((b, d, d), x.dtype)
            _, o = jax.lax.scan(step, S0, (tm(r), tm(decay), tm(k), tm(v), tm(kk), tm(a)))
            o = jnp.swapaxes(o, 0, 1)
            mu = jnp.mean(o, axis=-1, keepdims=True)
            var = jnp.var(o, axis=-1, keepdims=True)
            o = (o - mu) * jax.lax.rsqrt(var + EPS) * gn_w + gn_b
            o = o + jnp.sum(r * k * r_k, axis=-1, keepdims=True) * v
            return o * g @ W_o
        return _forward(x, x_mix, W_r, W_k, W_v, W_o, A_w, B_w, b_w, A_a, B_a, b_a, A_g, B_g, k_k, k_a, r_k, gn_w, gn_b)

    def _L0_ffn_ref(x, Wg, bg, bias, W1, b1, W2, b2):
        import jax, jax.numpy as jnp
        import numpy as np
        D_MODEL = 64
        EXPERT_DIM = 128
        NUM_EXPERTS = 8
        TOP_K = 2
        SEQ_LEN = 512
        BATCH = 2
        x_flat = x.reshape(-1, D_MODEL)
        gate_logits = x_flat @ Wg + bg + bias
        topk_vals, topk_idx = jax.lax.top_k(gate_logits, TOP_K)
        topk_w = jax.nn.softmax(topk_vals, axis=-1)
        combine = (jax.nn.one_hot(topk_idx, NUM_EXPERTS, dtype=x.dtype) * topk_w[..., None]).sum(axis=1)
        h = jax.nn.relu(jnp.einsum('td,edh->teh', x_flat, W1) + b1)
        y = jnp.einsum('teh,ehd->ted', h, W2) + b2
        out = jnp.einsum('ted,te->td', y, combine)
        return out.reshape(x.shape)
    h = _L0_tok_ref(x, L0_tok_ln1_g, L0_tok_ln1_b, L0_tok_W1, L0_tok_b1, L0_tok_ln2_g, L0_tok_ln2_b, L0_tok_Wp1, L0_tok_bp1, L0_tok_lnp_g, L0_tok_lnp_b, L0_tok_Wp2, L0_tok_bp2)
    h = jnp.concatenate([h, txt], axis=1)
    h = h + _L0_attn_ref(_layernorm(h, axis=-1), L0_attn_x_mix, L0_attn_W_r, L0_attn_W_k, L0_attn_W_v, L0_attn_W_o, L0_attn_A_w, L0_attn_B_w, L0_attn_b_w, L0_attn_A_a, L0_attn_B_a, L0_attn_b_a, L0_attn_A_g, L0_attn_B_g, L0_attn_k_k, L0_attn_k_a, L0_attn_r_k, L0_attn_gn_w, L0_attn_gn_b)
    h = h + _L0_ffn_ref(_layernorm(h, axis=-1), L0_ffn_Wg, L0_ffn_bg, L0_ffn_bias, L0_ffn_W1, L0_ffn_b1, L0_ffn_W2, L0_ffn_b2)
    return h

_drawn_inputs = setup_inputs


def setup_inputs(seed=0):
    import zlib

    import numpy as np

    out = dict(_drawn_inputs(seed))
    spreads = {'L0_tok_ln1_g': (1.0, 0.2),
     'L0_tok_ln1_b': (0.0, 0.1),
     'L0_tok_b1': (0.0, 0.1),
     'L0_tok_ln2_g': (1.0, 0.2),
     'L0_tok_ln2_b': (0.0, 0.1),
     'L0_tok_bp1': (0.0, 0.1),
     'L0_tok_lnp_g': (1.0, 0.2),
     'L0_tok_lnp_b': (0.0, 0.1),
     'L0_tok_bp2': (0.0, 0.1),
     'L0_attn_gn_w': (1.0, 0.2),
     'L0_attn_gn_b': (0.0, 0.1),
     'L0_ffn_bias': (0.0, 0.1)}
    factors = {'L0_ffn_bg': 6.493, 'L0_ffn_b1': 8.0}
    for name, (base, spread) in spreads.items():
        noise = np.random.default_rng([zlib.crc32(name.encode()), seed]).standard_normal(out[name].shape)
        drawn = base * np.exp(spread * noise) if base else spread * noise
        out[name] = jnp.asarray(drawn.astype(out[name].dtype))
    for name, factor in factors.items():
        out[name] = (out[name] * factor).astype(out[name].dtype)
    return out
```

```python
from contextlib import ExitStack

import numpy as np
import concourse.bass as bass
from concourse import mybir

F32 = mybir.dt.float32
F32R = mybir.dt.float32r
BF16 = mybir.dt.bfloat16
ALU = mybir.AluOpType
ACT = mybir.ActivationFunctionType
AX = mybir.AxisListType

P = 128
D = 64
BATCH = 8
G = 2
J = 4
C = 32
IMG = 64
TXT = 77
SEQ = 3 * IMG + TXT
PATCH = 192
PH = PATCH // 2
NIMG = IMG // C
NTXT = -(-TXT // C)
NCH = 3 * NIMG + NTXT
NU = 1 + NIMG + NTXT
ROUNDS = NU // 2
E = 8
EH = 128
PAIRS = -(-NCH // 2)
LEVELS = (2, 4, 8, 16)
EPS = 1e-5
GN_EPS = D * 1e-5
DECAY = -0.6065306597126334


def columns(*widths):
    at, out = 0, {}
    for name, width in widths:
        out[name] = slice(at, at + width)
        at += width
    return out, at


CONST, NCONST = columns(("ident", P), ("masks", 4 * P), ("suffix", P), ("m1", 2 * P),
                        *((f"m{l}", 2 * P) for l in LEVELS), ("ident2", 2 * P), ("seq", J), ("block", J * D),
                        ("tri", 2 * E * E), ("fold", D), ("half", 16))
ROWS, NROWS = columns(("b1", D), ("bp1", D), ("bp2", D), ("k_k", D), ("k_a", D), ("r_k", D), ("gn_w", D),
                      ("gn_b", D), ("b_a", D), ("bg", E), ("bias", E))
COLS, NCOLS = columns(("ln1_g", 2), ("ln1_b", 2), ("ln2_g", 1), ("ln2_b", 1), ("lnp_g", 1), ("lnp_b", 1),
                      ("mix", 6), ("b1e", E))
TOKW, NTOKW = columns(("W1", 2 * D), ("Wp1", D), ("Wp2", D))
ATTW, NATTW = columns(("rkv", 3 * D), ("A_w", D), ("A_g", P), ("A_aT", P), ("B_a", D), ("B_w", D), ("B_g", D),
                      ("W_o", 2 * D), ("Wg", E), ("b2", P))
ARC, NARC = columns(("U", P), ("Wf", P), ("OV", P), ("H", 2 * P), ("GW", P), ("GB", P), ("Bp", P),
                    ("LrbT", 2 * P), ("Rf", P), ("E", J))


def constants():
    i = np.arange(P)
    same = (i[:, None] // C) == (i[None, :] // C)
    su = (same & (i[:, None] < i[None, :])).astype(np.float32)
    iu = (same & (i[:, None] <= i[None, :])).astype(np.float32)
    t = np.zeros((P, NCONST), np.float32)
    t[:, CONST["ident"]] = np.eye(P)
    t[:, CONST["masks"]] = np.concatenate([su, iu, su, iu], 1)
    t[:, CONST["suffix"]] = su.T
    def merged(l):
        return ((i[:, None] // (2 * l) == i[None, :] // (2 * l)) & (i[:, None] % (2 * l) >= l)
                & (i[None, :] % (2 * l) < l)).astype(np.float32)
    t[:, CONST["m1"]] = np.concatenate([merged(1).T] * 2, 1)
    for l in LEVELS:
        t[:, CONST[f"m{l}"]] = np.concatenate([merged(l)] * 2, 1)
    t[:, CONST["ident2"]] = np.concatenate([np.eye(P)] * 2, 1)
    seq = (i[:, None] // C == np.arange(J)[None, :]).astype(np.float32)
    t[:, CONST["seq"]] = seq
    t[:, CONST["block"]] = np.repeat(seq, D, 1)
    e = np.arange(E)
    t[:, CONST["tri"]] = np.tile((e[None, :] < e[:, None]).reshape(1, -1), (P, 2))
    t[:, CONST["fold"]] = np.tile(np.eye(D), (2, 1))
    t[:, CONST["half"]] = -0.5
    return t


def picks():
    pick = np.zeros((3, E, E, P), np.float32)
    for e in range(E):
        pick[:, e, e] = 1.0
    return pick.reshape(3 * E, E * P)


def build(nc, patches, text, consts, pick, rows, cols, tokw, attw, w1, w2, out):
    ctx = ExitStack()
    with ctx:
        def sb(name, shape, dt=F32):
            return ctx.enter_context(nc.sbuf_tensor(name, shape, dt))

        def sem(name):
            return ctx.enter_context(nc.semaphore(name))

        PT = sb("PT", [P, 4, PATCH])
        KC = sb("KC", [P, NCONST])
        RW = sb("RW", [P, NROWS])
        CL = sb("CL", [P, NCOLS])
        TW = sb("TW", [P, NTOKW])
        AW = sb("AW", [P, NATTW])
        W2 = sb("W2", [P, E * D])

        def const(name):
            return KC[:, CONST[name]]

        def row(name, n=2):
            v = RW[:, ROWS[name]]
            return v.unsqueeze(1).to_broadcast([P, n, v.shape[1]])

        def pairs(ap):
            return ap.rearrange("p (g d) -> p g d", g=2)

        ident = const("ident")
        Wproj = sb("Wproj", [P, 4 * D])
        Wlora = sb("Wlora", [P, D + P])
        mix = sb("mix", [P, 6])
        kaH = sb("kaH", [P, D])
        gbias = sb("gbias", [P, E])
        lnpH = sb("lnpH", [P, 2])
        pickB = sb("pickB", [24, E * P], BF16)
        W1h = sb("W1h", [P, E * EH], F32R)
        W1l = sb("W1l", [P, E * EH], F32R)

        st0 = sb("st0", [P, 10, 6])
        mv0 = sb("mv0", [P, 10, 2])
        rs0 = sb("rs0", [P, 10, 1])
        xh0 = sb("xh0", [P, 4, PATCH])
        xT0 = sb("xT0", [P, 2, 4 * P])
        t0 = sb("t0", [P, 4, D])
        n0 = sb("n0", [P, 4, D])
        nT0 = sb("nT0", [P, 2, P])
        th0 = sb("th0", [P, 2, P])
        HT = sb("HT", [P, 10, D])
        XHD = sb("XHD", [P, 10, 2, D])
        XT = sb("XT", [P, NU + 2, G, J, C])

        def two(name, shape, dt=F32):
            return [sb(f"{name}{s}", shape, dt) for s in range(2)]

        XS = two("XS", [P, G * P])
        RK = two("RK", [P, G, 4, D])
        TH = two("TH", [D + 1, G * P])
        SG = two("SG", [P, G * P])
        ZA = two("ZA", [P, G, D])
        TA = two("TA", [P, G, D])
        TWd = two("TWd", [P, G, D])
        LW = two("LW", [P, G, D])
        KK = two("KK", [P, G, D])
        SQ = two("SQ", [P, G, D])
        SS = two("SS", [P, G, 1])
        RN = two("RN", [P, G, 1])
        KN = two("KN", [P, G, D])
        RR = two("RR", [P, G, D])
        T1 = two("T1", [P, G, D])
        K2 = two("K2", [P, G, D])
        B2 = two("B2", [P, G, D])
        MM = SQ
        BON = two("BON", [P, G, 1])
        VBN = T1
        EX = two("EX", [P, 3, G, D])
        NN = two("NN", [P, G, D])
        HAT = two("HAT", [P, 4, G, D])
        KP = two("KP", [P, G, D])
        FT = two("FT", [P, 4, P])
        AT = two("AT", [P, G, P])
        LKT = two("LKT", [P, G, 2, P])
        VB = two("VB", [P, G, J, D])
        QT = two("QT", [P, G, P])
        PI = two("PI", [P, G, P])
        YI = two("YI", [P, G, P])
        QA = YI
        LV = two("LV", [P, G, D])
        ARCH = sb("ARCH", [P, NU, NARC])
        W1raw = ARCH[:, 0, 0:E * EH]
        pickraw = ARCH[0:24, 1, 0:E * P]

        STG = two("STG", [P, NARC])
        STH = two("STH", [P, G, D])
        ST = two("ST", [P, J * D])
        ES = sb("ES", [P, J * D])
        EHs = sb("EHs", [P, J * D])
        SA = sb("SA", [P, G, D])
        SAB = sb("SAB", [P, G, J, D])
        OO = sb("OO", [P, G, D])
        st2 = sb("st2", [P, G, 6])
        mv2 = sb("mv2", [P, G, 2])
        rs2 = sb("rs2", [P, G, 1])
        ve2 = sb("ve2", [P, G, 1])
        X1 = sb("X1", [P, G, D])
        OG = sb("OG", [P, G, D])
        OGT = sb("OGT", [P, P])
        H1 = sb("H1", [P, 2 * PAIRS, G * D])
        st3 = sb("st3", [P, G, 6])
        mv3 = sb("mv3", [P, G, 2])
        rs3 = sb("rs3", [P, G, 1])
        ve3 = sb("ve3", [P, G, 1])
        XN = sb("XN", [P, G, D])
        XD = sb("XD", [P, G, 2, D], F32R)
        X2S = sb("X2S", [P, G * P])
        XHL = sb("XHL", [P, 2 * PAIRS, G * P], F32R)
        LG = sb("LG", [P, G, E])
        M1 = sb("M1", [P, G, 1])
        LS = sb("LS", [P, G, E])
        PX = sb("PX", [P, G, E])
        DD = sb("DD", [P, G, E, E])
        D1 = sb("D1", [P, G * E * E])
        D2 = sb("D2", [P, G, E, E])
        RKs = sb("RKs", [P, G, E])
        PM = sb("PM", [P, G, E])
        SM = sb("SM", [P, G, 1])
        RC = sb("RC", [P, G, 1])
        CF = sb("CF", [P, G, E])
        CB = sb("CB", [P, G, E], BF16)
        C2 = sb("C2", [P, G, E])
        C2B = sb("C2B", [P, G, E], BF16)
        CP = sb("CP", [P, G, 3, E])
        CTF = sb("CTF", [24, 2 * PAIRS, G * P])
        CTB = sb("CTB", [24, 2 * PAIRS, G * P], BF16)
        RL = [xh0[:, :, :].rearrange("p q d -> p (q d)")[:, 0:4 * P], sb("RL1", [P, 4 * P])]
        HC = [xT0[:, 0, :], xT0[:, 1, :]]
        YS = PT[:, :, :].rearrange("p q d -> p (q d)")[:, 0:4 * P]

        PS = ctx.enter_context(nc.psum_tensor("PS", [P, 8, 512], F32))

        def sems(names):
            return [sem(n) for n in names.split()]

        l_patch, l_text, l_const, l_pick, l_rows, l_cols, l_tokw, l_attw, l_w1, l_w2 = sems(
            "l_patch l_text l_const l_pick l_rows l_cols l_tokw l_attw l_w1 l_w2")
        var_ready, rs_ready, xh_ready, tr_ready, nt_ready, mm_ready, zh_ready, zt_ready = sems(
            "var_ready rs_ready xh_ready tr_ready nt_ready mm_ready zh_ready zt_ready")
        dve0, pool0 = sems("dve0 pool0")
        memsets, xt_dve, xt_act, w_rounded, w_rest, pick_ready, mix_ready, aab_ready = sems(
            "memsets xt_dve xt_act w_rounded w_rest pick_ready mix_ready aab_ready")
        (x_staged, proj_ready, hid_ready, rk_ready, th_ready, sgt_ready, sg_ready, za_ready, ta_ready, wg_ready,
         tw_ready, w_ready, cum_ready, ex_ready, ss_ready, rn_ready, hat_ready, kp_ready, ft_ready, ftc_ready,
         l_ready, p1t_ready, p1_ready) = sems(
             "x_staged proj_ready hid_ready rk_ready th_ready sgt_ready sg_ready za_ready ta_ready wg_ready "
             "tw_ready w_ready cum_ready ex_ready ss_ready rn_ready hat_ready kp_ready ft_ready ftc_ready "
             "l_ready p1t_ready p1_ready")
        (y_ready, ysb_ready, pp_ready, pu_ready, qq_ready, q_ready, lvov_ready, lv_ready, uw_ready, vb_ready,
         arch_act, arch_dve, dve1, pool1) = sems(
             "y_ready ysb_ready pp_ready pu_ready qq_ready q_ready lvov_ready lv_ready uw_ready vb_ready "
             "arch_act arch_dve dve1 pool1")
        stg = sems("stg_loaded0 stg_loaded1")
        (s_ready, sap_ready, sa_ready, sab_ready, ops_ready, sps_ready, eh_ready, oo_ready, mv2_ready, rs2_ready,
         og_ready, ogt_ready, ogtc_ready, att_ready, h1_ready, mv3_ready, rs3_ready, xn_ready, xr_ready, xd_ready,
         x2t_ready, x2s_ready, xhl_ready, lg_ready, ls_ready, pex_ready, cf_ready, cp_ready, ct_ready,
         ctc_ready) = sems(
             "s_ready sap_ready sa_ready sab_ready ops_ready sps_ready eh_ready oo_ready mv2_ready rs2_ready "
             "og_ready ogt_ready ogtc_ready att_ready h1_ready mv3_ready rs3_ready xn_ready xr_ready xd_ready "
             "x2t_ready x2s_ready xhl_ready lg_ready ls_ready pex_ready cf_ready cp_ready ct_ready ctc_ready")
        z_ready, c_ready, relu_done, hc_done, y_done, y_sum, ys_ready, fin_ready, fin_done, stored = sems(
            "z_ready c_ready relu_done hc_done y_done y_sum ys_ready fin_ready fin_done stored")
        dve2, pool2, passed = sems("dve2 pool2 passed")

        block = ctx.enter_context(nc.Block())

        class Chain:

            def __init__(self, eng, s, per=0):
                self.eng, self.s, self.per, self.n = eng, s, per, 0

            def mark(self, ins):
                self.n += 1
                ins.then_inc(self.s, 1)
                return self.n

            def wait(self, n, r=0):
                self.eng.wait_ge(self.s, r * self.per + n)

            def link(self, ins, r=0):
                self.wait(self.mark(ins), r)

        def alone(eng, s, value):
            eng.wait_ge(s, value)
            if not isinstance(value, int):
                eng.sem_inc(passed, 1)

        SLOT = [0, 1, 2, 1, 2, 1] + list(range(NU - NTXT, NU))
        HQ = [2 * (k % NIMG) for k in range(3 * NIMG)] + [2 * NIMG + 2 * t for t in range(NTXT)]

        def at(k, n=1):
            return slice(k, k + n) if isinstance(k, int) else bass.ds(k, n)

        def loaded(k, b):
            return 16 * (k - b) + 32

        def level(it, li, s, levels):
            return it * (2 * levels) + (2 * li + s + 1)

        def phase2(eng, chunk, expert, finish):
            def beside(p, c):
                return lambda i: expert(p, 4 * c + i, 2)
            for k in range(2):
                chunk(k, k, lambda i: None)
            with eng.Fori(0, PAIRS - 2) as p:
                for b in range(2):
                    chunk(2 * p + (2 + b), b, beside(p, b))
                finish(p, 2)
            p = PAIRS - 2
            chunk(2 * p + 2, 0, beside(p, 0))
            for e in range(4, E):
                expert(p, e, 2)
            finish(p, 2)
            for e in range(E):
                expert(p + 1, e, 1)
            finish(p + 1, 1)

        @block.sync
        def _(sp):
            sp.dma_start(PT[:, :, :], patches).then_inc(l_patch, 16)
            sp.dma_start(KC[:, :], consts).then_inc(l_const, 16)
            sp.dma_start(AW[:, :], attw).then_inc(l_attw, 16)
            sp.dma_start(W1raw, w1).then_inc(l_w1, 16)
            sp.dma_start(W2[:, :], w2).then_inc(l_w2, 16)

            def load(k):
                b, u = k % 2, SLOT[k]
                sp.wait_ge(arch_act, u + 1)
                sp.wait_ge(arch_dve, u + 1)
                if k >= 2:
                    sp.wait_ge(h1_ready, k - 1)
                sp.dma_start(STG[b][:, :], ARCH[:, u, :]).then_inc(stg[b], 16)
                sp.dma_start(STH[b][:, :, :], HT[:, HQ[k]:HQ[k] + 2, :]).then_inc(stg[b], 16)

            def store(p, n):
                sp.wait_ge(fin_done, p + 2)
                sp.dma_start(out[:, 2 * p * G * D:(2 * p + n) * G * D],
                             H1[:, 2 * p:2 * p + n, :].rearrange("p k d -> p (k d)")).then_inc(stored, 16)

            for k in range(NCH):
                load(k)
                if k >= 5 and k % 2:
                    store((k - 5) // 2, 2)
            for p in range((NCH - 6) // 2 + 1, PAIRS):
                store(p, min(2, NCH - 2 * p))
            sp.wait_ge(stored, 16 * PAIRS)

        @block.gpsimd
        def _(pool):
            half = KC[:, CONST["half"]]

            c0 = Chain(pool, pool0)
            c0.link(nc.gpsimd.memset(XT[:, NU:, :, :, :], 0.0))
            c0.link(nc.gpsimd.memset(XT[D:P, 0, :, :, 0:1], 0.0))
            for s in range(2):
                c0.link(nc.gpsimd.memset(TH[s][D:D + 1, :], 1.0))
            nc.gpsimd.memset(ST[0][:, :], 0.0).then_inc(memsets, 1)
            pool.wait_ge(memsets, 1)
            pool.wait_ge(l_const, 16)
            for i, (a, b) in enumerate(((0, 4), (4, 10), (0, 4), (0, 4), (0, 4))):
                pool.wait_ge(var_ready, i + 1)
                c0.link(nc.gpsimd.tensor_scalar(rs0[:, a:b, :], mv0[:, a:b, 1:2], EPS, None, ALU.add))
                nc.gpsimd.tensor_tensor(rs0[:, a:b, :], rs0[:, a:b, :], half[:, 0:b - a].unsqueeze(2), ALU.pow)\
                    .then_inc(rs_ready, 1)
                if i == 1:
                    pool.wait_ge(w_rounded, 1)
                    nc.gpsimd.tensor_tensor(W1l[:, :], W1raw, W1h[:, :].bitcast(F32), ALU.subtract)\
                        .then_inc(w_rest, 1)

            def stage(n, s):
                nc.gpsimd.tensor_copy(XS[s][:, :].unsqueeze(1),
                                      XT[:, at(n), :, :, :].rearrange("p u g j c -> p u (g j c)"))\
                    .then_inc(x_staged, 1)

            pool.wait_ge(xt_dve, 1)
            pool.wait_ge(xt_act, 1)
            pool.wait_ge(memsets, 1)
            for s in range(2):
                stage(s, s)

            c1 = Chain(pool, pool1, 2)
            with pool.Fori(0, ROUNDS) as it:
                for s in range(2):
                    alone(pool, sgt_ready, 2 * it + (s + 1))
                    nc.gpsimd.tensor_scalar(SG[s][:, :], SG[s][:, :], 0.5, 0.5, ALU.mult, ALU.add)\
                        .then_inc(sg_ready, 1)
                for s in range(2):
                    alone(pool, ss_ready, 2 * it + (s + 1))
                    c1.link(nc.gpsimd.tensor_scalar(RN[s][:, :, :], SS[s][:, :, :], 1e-24, None, ALU.max), it)
                    nc.gpsimd.tensor_tensor(RN[s][:, :, :], RN[s][:, :, :], half[:, 0:G].unsqueeze(2), ALU.pow)\
                        .then_inc(rn_ready, 1)
                for s in range(2):
                    alone(pool, hid_ready, 2 * it + (s + 1))
                    stage(2 * it + (s + 2), s)
                for s in range(2):
                    pool.wait_ge(rk_ready, 2 * it + (s + 1))
                    for g in range(G):
                        last = nc.gpsimd.tensor_tensor(
                            VB[s][:, g, :, :], RK[s][:, g, 2:3, :].to_broadcast([P, J, D]),
                            const("block").rearrange("p (j d) -> p j d", j=J), ALU.mult)
                    last.then_inc(vb_ready, 1)
            assert c1.n == c1.per

            PER = 8

            def chunk(k, b, step):
                if isinstance(k, int) and k == 0:
                    pool.wait_ge(memsets, 1)
                else:
                    pool.wait_ge(s_ready, k)
                pool.wait_ge(stg[b], loaded(k, b))
                nc.gpsimd.tensor_tensor(ES[:, :].rearrange("p (j d) -> p j d", j=J),
                                        ST[b][:, :].rearrange("p (j d) -> p j d", j=J),
                                        STG[b][:, ARC["E"]].unsqueeze(2).to_broadcast([P, J, D]), ALU.mult)\
                    .then_inc(pool2, 1)
                pool.wait_ge(pool2, PER * k + 1)
                nc.gpsimd.tensor_tensor(EHs[:, :], ES[:, :], STG[b][:, ARC["H"]], ALU.add).then_inc(eh_ready, 1)
                for i, (mv, ve, rs, ready, done, eps) in enumerate(((mv2, ve2, rs2, mv2_ready, rs2_ready, GN_EPS),
                                                                    (mv3, ve3, rs3, mv3_ready, rs3_ready, EPS))):
                    alone(pool, ready, k + 1)
                    nc.gpsimd.tensor_scalar(ve[:, :, :], mv[:, :, 1:2], eps, None, ALU.add).then_inc(pool2, 1)
                    pool.wait_ge(pool2, PER * k + (2 + i))
                    nc.gpsimd.tensor_tensor(rs[:, :, :], ve[:, :, :], half[:, 0:G].unsqueeze(2), ALU.pow)\
                        .then_inc(done, 1)
                alone(pool, x2s_ready, k + 1)
                nc.gpsimd.tensor_copy(XHL[:, at(k), :], X2S[:, :].unsqueeze(1)).then_inc(xhl_ready, 1)
                alone(pool, cf_ready, k + 1)
                nc.gpsimd.tensor_copy(CB[:, :, :], CF[:, :, :]).then_inc(pool2, 1)
                pool.wait_ge(pool2, PER * k + 4)
                nc.gpsimd.tensor_tensor(C2[:, :, :], CF[:, :, :], CB[:, :, :], ALU.subtract).then_inc(pool2, 1)
                alone(pool, pool2, PER * k + 5)
                nc.gpsimd.tensor_copy(C2B[:, :, :], C2[:, :, :]).then_inc(pool2, 1)
                nc.gpsimd.tensor_copy(CP[:, :, 0, :], CB[:, :, :]).then_inc(pool2, 1)
                alone(pool, pool2, PER * k + 7)
                nc.gpsimd.tensor_copy(CP[:, :, 1, :], C2B[:, :, :]).then_inc(pool2, 1)
                pool.wait_ge(pool2, PER * k + 8)
                nc.gpsimd.tensor_tensor(CP[:, :, 2, :], C2[:, :, :], C2B[:, :, :], ALU.subtract)\
                    .then_inc(cp_ready, 1)

            for k in range(2):
                chunk(k, k, None)
            with pool.Fori(0, PAIRS - 2) as p:
                for b in range(2):
                    chunk(2 * p + (2 + b), b, None)
            chunk(NCH - 1, 0, None)

        @block.scalar
        def _(act):
            copy = nc.scalar.copy
            act.dma_start(CL[:, :], cols).then_inc(l_cols, 16)
            act.dma_start(RW[:, :], rows.partition_broadcast(P)).then_inc(l_rows, 16)
            act.dma_start(TW[:, :], tokw).then_inc(l_tokw, 16)
            act.dma_start(HT[:, 4:10, :], text).then_inc(l_text, 16)
            act.dma_start(pickraw, pick).then_inc(l_pick, 16)
            act.wait_ge(l_pick, 16)
            copy(pickB[:, :], pickraw).then_inc(pick_ready, 1)
            act.wait_ge(l_w1, 16)
            copy(W1h[:, :], W1raw).then_inc(w_rounded, 1)
            act.wait_ge(zh_ready, 1)
            nc.scalar.activation(th0[:, :, :], nT0[:, :, :], ACT.Tanh).then_inc(zt_ready, 1)
            act.wait_ge(tr_ready, 4)
            src = PS[:, 5:8, :].rearrange("p b n -> p (b n)").rearrange("p (q j c) -> p q j c", j=J, c=C)
            for u, q in ((0, 0), (1, 2), (2, 0), (3, 4), (4, 6), (5, 8)):
                copy(XT[D:P, u, :, :, 1:C], src[D:P, q:q + 2, :, 0:C - 1])
            for u, q in ((1, 0), (2, 2), (3, 2), (4, 4), (5, 6)):
                last = copy(XT[D:P, u, :, :, 0:1], src[D:P, q:q + 2, :, C - 1:C])
            last.then_inc(xt_act, 1)

            with act.Fori(0, ROUNDS) as it:
                def bank(s, i):
                    return PS[:, 4 * s + i, :]

                for s in range(2):
                    n = 2 * it + s
                    act.wait_ge(proj_ready, 2 * it + (s + 1))
                    copy(RK[s][:, :, :, :].rearrange("p g w d -> p (g w d)"), bank(s, 0)).then_inc(rk_ready, 1)
                    act.wait_ge(hid_ready, 2 * it + (s + 1))
                    nc.scalar.activation(TH[s][0:D, :], bank(s, 1)[0:D, 0:G * P], ACT.Tanh).then_inc(th_ready, 1)
                    nc.scalar.activation(SG[s][:, :], bank(s, 1)[:, G * P:2 * G * P], ACT.Tanh, scale=0.5)\
                        .then_inc(sgt_ready, 1)
                for s in range(2):
                    act.wait_ge(za_ready, 2 * it + (s + 1))
                    nc.scalar.activation(TA[s][:, :, :], ZA[s][:, :, :], ACT.Tanh, scale=0.5).then_inc(ta_ready, 1)
                for s in range(2):
                    act.wait_ge(wg_ready, 2 * it + (s + 1))
                    nc.scalar.activation(TWd[s][:, :, :], bank(s, 1)[:, 0:2 * G * D].rearrange(
                        "p (g w d) -> p g w d", g=G, w=2)[:, :, 0, :], ACT.Tanh, scale=0.5).then_inc(tw_ready, 1)
                for s in range(2):
                    n = 2 * it + s
                    act.wait_ge(cum_ready, 2 * it + (s + 1))
                    nc.scalar.activation(EX[s][:, :, :, :].rearrange("p w g d -> p (w g d)"),
                                         bank(s, 2)[:, 0:3 * P], ACT.Exp)
                    nc.scalar.activation(ARCH[:, at(n), ARC["E"]], bank(s, 2)[:, 3 * P:3 * P + J].unsqueeze(1),
                                         ACT.Exp)
                    nc.scalar.activation(NN[s][:, :, :].rearrange("p g d -> p (g d)"), bank(s, 2)[:, 0:P],
                                         ACT.Exp, scale=-1.0).then_inc(ex_ready, 1)
                for s in range(2):
                    n = 2 * it + s
                    act.wait_ge(ft_ready, 2 * it + (s + 1))
                    copy(ARCH[:, at(n), ARC["Rf"]], bank(s, 0)[:, P:2 * P].unsqueeze(1))
                    copy(FT[s][:, :, :].rearrange("p w t -> p (w t)"), bank(s, 0)).then_inc(ftc_ready, 1)
                for s in range(2):
                    act.wait_ge(p1t_ready, 2 * it + (s + 1))
                    copy(PI[s][:, :, :].rearrange("p g t -> p (g t)"), bank(s, 3)[:, 0:G * P]).then_inc(p1_ready, 1)
                for s in range(2):
                    n = 2 * it + s
                    act.wait_ge(lvov_ready, 2 * it + (s + 1))
                    copy(ARCH[:, at(n), ARC["OV"].start:ARC["H"].stop], bank(s, 1)[:, P:4 * P].unsqueeze(1))
                    copy(LV[s][:, :, :].rearrange("p g d -> p (g d)"), bank(s, 1)[:, 0:P]).then_inc(lv_ready, 1)
                for s in range(2):
                    n = 2 * it + s
                    act.wait_ge(uw_ready, 2 * it + (s + 1))
                    copy(ARCH[:, at(n), ARC["U"].start:ARC["Wf"].stop], bank(s, 2)[:, 0:2 * P].unsqueeze(1))\
                        .then_inc(arch_act, 1)

            act.sem_inc(relu_done, 2)

            def expert(p, e, n):
                x = E * p + e
                act.wait_ge(z_ready, E * p + (e + 1))
                act.wait_ge(hc_done, E * p + (e + 1))
                nc.scalar.activation(RL[e % 2][:, 0:n * G * P], PS[:, 4 + e % 2, 0:n * G * P], ACT.Relu,
                                     bias=CL[:, COLS["b1e"]][:, e:e + 1]).then_inc(relu_done, 1)

            def chunk(k, b, step):
                step(0)
                step(1)
                act.wait_ge(ogt_ready, k + 1)
                copy(OGT[:, :], PS[:, 2, 0:P]).then_inc(ogtc_ready, 1)
                step(2)
                act.wait_ge(xn_ready, k + 1)
                copy(XD[:, :, 0, :], XN[:, :, :]).then_inc(xr_ready, 1)
                step(3)
                act.wait_ge(x2t_ready, k + 1)
                copy(X2S[:, :], PS[:, 2, 2 * P:4 * P]).then_inc(x2s_ready, 1)
                act.wait_ge(ls_ready, k + 1)
                nc.scalar.activation(PX[:, :, :], LS[:, :, :], ACT.Exp).then_inc(pex_ready, 1)
                act.wait_ge(ct_ready, k + 1)
                copy(CTF[:, at(k), :], PS[0:24, 2, P:3 * P].unsqueeze(1))
                copy(CTB[:, at(k), :], PS[0:24, 2, P:3 * P].unsqueeze(1)).then_inc(ctc_ready, 1)

            def finish(p, n):
                act.wait_ge(y_sum, p + 1)
                copy(YS[:, 0:n * G * P], PS[:, 7, 0:n * G * P]).then_inc(ys_ready, 1)

            phase2(act, chunk, expert, finish)

        @block.vector
        def _(dve):
            V = nc.vector
            TT, TS, STT = V.tensor_tensor, V.tensor_scalar, V.scalar_tensor_tensor
            c0 = Chain(dve, dve0)

            def variances(src, tiles):
                for q in tiles:
                    last = V.bn_stats(st0[:, q, :], src(q))
                c0.link(last)
                for q in tiles:
                    last = V.bn_aggr(mv0[:, q, :], st0[:, q, :])
                last.then_inc(var_ready, 1)

            def normalised(dst, src, tiles, count):
                dve.wait_ge(var_ready, count)
                dve.wait_ge(rs_ready, count)
                for q in tiles:
                    last = TS(dst(q), src(q), mv0[:, q, 0:1], rs0[:, q, 0:1], ALU.subtract, ALU.mult)
                return last

            four = range(4)
            dve.wait_ge(l_patch, 16)
            variances(lambda q: PT[:, q, :], four)
            dve.wait_ge(l_text, 16)
            variances(lambda q: HT[:, q, :], range(4, 10))
            normalised(lambda q: xh0[:, q, :], lambda q: PT[:, q, :], four, 1).then_inc(xh_ready, 1)
            normalised(lambda q: XHD[:, q, 0, :], lambda q: HT[:, q, :], range(4, 10), 2)
            normalised(lambda q: XHD[:, q, 1, :], lambda q: HT[:, q, :], range(4, 10), 2)

            def col(name):
                return CL[:, COLS[name]]

            dve.wait_ge(l_cols, 16)
            dve.wait_ge(l_rows, 16)
            TS(mix[0:D, :], col("mix")[0:D, :], -1.0, 1.0, ALU.mult, ALU.add)
            V.tensor_copy(mix[D:P, :], col("mix")[D:P, :])
            TS(kaH[:, :], RW[:, ROWS["k_a"]], 0.5, None, ALU.mult)
            TT(gbias[:, :], RW[:, ROWS["bg"]], RW[:, ROWS["bias"]], ALU.add)
            c0.link(TS(lnpH[:, :], CL[:, COLS["lnp_g"].start:COLS["lnp_b"].stop], 0.5, None, ALU.mult))
            dve.wait_ge(tr_ready, 1)
            for h in range(2):
                last = TS(xT0[0:PH, h, :], PS[0:PH, h, :], col("ln1_g")[0:PH, h:h + 1], col("ln1_b")[0:PH, h:h + 1],
                          ALU.mult, ALU.add)
            last.then_inc(nt_ready, 1)
            dve.wait_ge(l_attw, 16)
            for i, m in ((0, 0), (1, 2), (2, 3)):
                TS(Wproj[:, i * D:(i + 1) * D], AW[:, ATTW["rkv"]][:, i * D:(i + 1) * D], mix[:, m:m + 1], None,
                   ALU.mult)
            TS(Wlora[:, 0:D], AW[:, ATTW["A_w"]], mix[:, 1:2], None, ALU.mult)
            TS(Wlora[:, D:D + P], AW[:, ATTW["A_g"]], mix[:, 5:6], None, ALU.mult)
            dve.wait_ge(aab_ready, 1)
            TS(Wproj[:, 3 * D:4 * D], PS[:, 7, 0:D], mix[:, 4:5], None, ALU.mult).then_inc(mix_ready, 1)

            dve.wait_ge(mm_ready, 1)
            c0.link(TT(t0[:, :, :], PS[:, 2, 0:4 * D].rearrange("p (q d) -> p q d", q=4), row("b1", 4), ALU.add))
            variances(lambda q: t0[:, q, :], four)
            normalised(lambda q: n0[:, q, :], lambda q: t0[:, q, :], four, 3).then_inc(xh_ready, 1)
            dve.wait_ge(tr_ready, 2)
            TS(nT0[:, :, :], PS[:, 0, 0:2 * P].rearrange("p (c t) -> p c t", c=2), col("ln2_g"), col("ln2_b"),
               ALU.mult, ALU.add).then_inc(nt_ready, 1)

            def by_group(ap):
                return ap.rearrange("p (c g) d -> p g c d", g=G)

            def two_banks(b):
                return PS[:, b:b + 2, 0:2 * D].rearrange("p g (c d) -> p g c d", c=2)

            def row4(name):
                return RW[:, ROWS[name]].unsqueeze(1).unsqueeze(1).to_broadcast([P, G, 2, D])

            dve.wait_ge(mm_ready, 2)
            for g in range(G):
                last = TT(by_group(t0[:, :, :])[:, g], two_banks(2)[:, g], row4("bp1")[:, g], ALU.add)
            c0.link(last)
            variances(lambda q: t0[:, q, :], four)
            normalised(lambda q: n0[:, q, :], lambda q: t0[:, q, :], four, 4).then_inc(xh_ready, 1)
            dve.wait_ge(tr_ready, 3)
            TS(nT0[:, :, :], PS[:, 1, 0:2 * P].rearrange("p (c t) -> p c t", c=2), lnpH[:, 0:1], lnpH[:, 1:2],
               ALU.mult, ALU.add).then_inc(zh_ready, 1)
            dve.wait_ge(zh_ready, 1)
            dve.wait_ge(zt_ready, 1)
            STT(nT0[:, :, :], th0[:, :, :], 1.0, nT0[:, :, :], ALU.add, ALU.mult).then_inc(nt_ready, 1)
            dve.wait_ge(mm_ready, 3)
            for g in range(G):
                last = TT(by_group(HT[:, 0:4, :])[:, g], two_banks(3)[:, g], row4("bp2")[:, g], ALU.add)
            c0.link(last)
            variances(lambda q: HT[:, q, :], four)
            normalised(lambda q: XHD[:, q, 0, :], lambda q: HT[:, q, :], four, 5)
            normalised(lambda q: XHD[:, q, 1, :], lambda q: HT[:, q, :], four, 5).then_inc(xh_ready, 1)
            dve.wait_ge(tr_ready, 4)
            src = PS[:, 5:8, :].rearrange("p b n -> p (b n)").rearrange("p (q j c) -> p q j c", j=J, c=C)
            for u, q in ((0, 0), (1, 2), (2, 0), (3, 4), (4, 6), (5, 8)):
                last = V.tensor_copy(XT[0:D, u, :, :, :], src[0:D, q:q + 2, :, :])
            last.then_inc(xt_dve, 1)

            c1 = Chain(dve, dve1, 20)
            with dve.Fori(0, ROUNDS) as it:
                def bank(s, i):
                    return PS[:, 4 * s + i, :]

                def flat(t):
                    return t.rearrange("p g d -> p (g d)")

                kk, k2, kn, b2, bon = [0, 0], [0, 0], [0, 0], [0, 0], [0, 0]
                for s in range(2):
                    dve.wait_ge(rk_ready, 2 * it + (s + 1))
                    TT(ZA[s][:, :, :], RK[s][:, :, 3, :], row("b_a"), ALU.add).then_inc(za_ready, 1)
                    kk[s] = c1.mark(TT(KK[s][:, :, :], RK[s][:, :, 1, :], row("k_k"), ALU.mult))
                    TT(RR[s][:, :, :], RK[s][:, :, 0, :], row("r_k"), ALU.mult)
                    c1.wait(kk[s], it)
                    c1.link(TT(SQ[s][:, :, :], KK[s][:, :, :], KK[s][:, :, :], ALU.mult), it)
                    V.tensor_reduce(SS[s][:, :, :], SQ[s][:, :, :], AX.X, ALU.add).then_inc(ss_ready, 1)
                for s in range(2):
                    dve.wait_ge(tw_ready, 2 * it + (s + 1))
                    TS(LW[s][:, :, :], TWd[s][:, :, :], DECAY / 2, DECAY / 2, ALU.mult, ALU.add).then_inc(w_ready, 1)
                for s in range(2):
                    dve.wait_ge(ta_ready, 2 * it + (s + 1))
                    c1.link(STT(T1[s][:, :, :], TA[s][:, :, :], -1.0,
                                kaH[:, :].unsqueeze(1).to_broadcast([P, G, D]), ALU.add, ALU.mult), it)
                    k2[s] = c1.mark(STT(K2[s][:, :, :], T1[s][:, :, :], 1.0, RK[s][:, :, 1, :], ALU.add, ALU.mult))
                    dve.wait_ge(rn_ready, 2 * it + (s + 1))
                    kn[s] = c1.mark(TT(KN[s][:, :, :], KK[s][:, :, :], RN[s][:, :, :].to_broadcast([P, G, D]),
                                       ALU.mult))
                    c1.wait(k2[s], it)
                    mm = c1.mark(TT(MM[s][:, :, :], RR[s][:, :, :], K2[s][:, :, :], ALU.mult))
                    c1.wait(kn[s], it)
                    b2[s] = c1.mark(STT(B2[s][:, :, :], TA[s][:, :, :], 1.0, KN[s][:, :, :], ALU.add, ALU.mult))
                    c1.wait(mm, it)
                    bon[s] = c1.mark(V.tensor_reduce(BON[s][:, :, :], MM[s][:, :, :], AX.X, ALU.add))
                for s in range(2):
                    n = 2 * it + s
                    dve.wait_ge(ex_ready, 2 * it + (s + 1))
                    c1.wait(b2[s], it)
                    EXs = EX[s]
                    STT(HAT[s][:, 0, :, :], KN[s][:, :, :], -1.0, EXs[:, 1, :, :], ALU.mult, ALU.mult)
                    TT(HAT[s][:, 1, :, :], RK[s][:, :, 0, :], EXs[:, 0, :, :], ALU.mult)
                    STT(HAT[s][:, 2, :, :], B2[s][:, :, :], 0.5, NN[s][:, :, :], ALU.mult, ALU.mult)
                    TT(HAT[s][:, 3, :, :], K2[s][:, :, :], NN[s][:, :, :], ALU.mult).then_inc(hat_ready, 1)
                    TT(KP[s][:, :, :], K2[s][:, :, :], EXs[:, 2, :, :], ALU.mult).then_inc(kp_ready, 1)
                    STT(ARCH[:, at(n), ARC["Bp"]].rearrange("p u (g d) -> p (u g) d", g=G), B2[s][:, :, :], 0.5,
                        EXs[:, 2, :, :], ALU.mult, ALU.mult)
                for s in range(2):
                    n = 2 * it + s
                    dve.wait_ge(wg_ready, 2 * it + (s + 1))
                    gate = bank(s, 1)[:, 0:2 * G * D].rearrange("p (g w d) -> p g w d", g=G, w=2)[:, :, 1, :]
                    c1.wait(bon[s], it)
                    for g in range(G):
                        last = STT(VBN[s][:, g, :], RK[s][:, g, 2, :], BON[s][:, g, :], RW[:, ROWS["gn_b"]],
                                   ALU.mult, ALU.add)
                    vbn = c1.mark(last)
                    TT(ARCH[:, at(n), ARC["GW"]].rearrange("p u (g d) -> p (u g) d", g=G), gate, row("gn_w"), ALU.mult)
                    c1.wait(vbn, it)
                    TT(ARCH[:, at(n), ARC["GB"]].rearrange("p u (g d) -> p (u g) d", g=G), gate, VBN[s][:, :, :],
                       ALU.mult)
                for s in range(2):
                    n = 2 * it + s
                    masks = const("masks")
                    for g in range(G):
                        dve.wait_ge(l_ready, 4 * it + (2 * s + g + 1))
                        L = bank(s, 2 + g)
                        last = TT(AT[s][:, g, :], L[:, 0:P], masks[:, 0:P], ALU.mult)
                        TT(LKT[s][:, g, :, :].rearrange("p w t -> p (w t)"), L[:, 2 * P:4 * P],
                           masks[:, 2 * P:4 * P], ALU.mult)
                        lrb = ARC["LrbT"].start + g * P
                        arch = TT(ARCH[:, at(n), lrb:lrb + P], L[:, P:2 * P].unsqueeze(1),
                                  masks[:, P:2 * P].unsqueeze(1), ALU.mult)
                    arch.then_inc(arch_dve, 1)
                    dve.wait_ge(arch_dve, 2 * it + (s + 1))
                    c1.link(TT(flat(QA[s][:, :, :]), flat(AT[s][:, :, :]), const("m1"), ALU.mult), it)
                    TT(flat(QT[s][:, :, :]), flat(QA[s][:, :, :]), const("ident2"), ALU.add).then_inc(q_ready, 1)
                for li, size in enumerate(LEVELS):
                    for s in range(2):
                        dve.wait_ge(y_ready, level(it, li, s, 4))
                        TT(flat(YI[s][:, :, :]), bank(s, 2)[:, 0:G * P], const(f"m{size}"), ALU.mult)\
                            .then_inc(ysb_ready, 1)
                    for s in range(2):
                        if li < 3:
                            dve.wait_ge(pp_ready, level(it, li, s, 3))
                            TT(flat(PI[s][:, :, :]), flat(PI[s][:, :, :]), bank(s, 3)[:, 0:G * P], ALU.add)\
                                .then_inc(pu_ready, 1)
                        dve.wait_ge(qq_ready, level(it, li, s, 4))
                        TT(flat(QT[s][:, :, :]), flat(QT[s][:, :, :]), bank(s, 0)[:, 0:G * P], ALU.add)\
                            .then_inc(q_ready, 1)
            assert c1.n == c1.per, c1.n

            dve.sem_inc(hc_done, 2)
            dve.sem_inc(fin_done, 1)
            MARKS = 12
            m = Chain(dve, dve2)

            def expert(p, e, n):
                dve.wait_ge(relu_done, E * p + (e + 3))
                dve.wait_ge(c_ready, E * p + (e + 1))
                dve.wait_ge(y_done, E * p + (e + 1))
                TT(HC[e % 2][:, 0:n * G * P], RL[e % 2][:, 0:n * G * P], PS[:, 3 + 3 * (e % 2), 0:n * G * P],
                   ALU.mult).then_inc(hc_done, 1)

            def chunk(k, b, step):
                def mark(i, ins):
                    ins.then_inc(dve2, 1)
                    return i

                def wait(i):
                    dve.wait_ge(dve2, MARKS * k + i)

                dve.wait_ge(stg[b], loaded(k, b))
                dve.wait_ge(sap_ready, k + 1)
                TT(SA[:, :, :], PS[:, 0:2, 0:D], pairs(STG[b][:, ARC["U"]]), ALU.add).then_inc(sa_ready, 1)
                dve.wait_ge(sa_ready, k + 1)
                for g in range(G):
                    last = TT(SAB[:, g, :, :], SA[:, g, :].unsqueeze(1).to_broadcast([P, J, D]),
                              const("block").rearrange("p (j d) -> p j d", j=J), ALU.mult)
                last.then_inc(sab_ready, 1)
                step(0)
                dve.wait_ge(eh_ready, k + 1)
                dve.wait_ge(sps_ready, k + 1)
                TT(ST[1 - b][:, :], EHs[:, :], PS[:, 0, 3 * D:3 * D + J * D], ALU.add).then_inc(s_ready, 1)
                TT(OO[:, :, :], PS[:, 0:2, D:2 * D], pairs(STG[b][:, ARC["OV"]]), ALU.add).then_inc(oo_ready, 1)
                dve.wait_ge(oo_ready, k + 1)
                for g in range(G):
                    last = V.bn_stats(st2[:, g, :], OO[:, g, :])
                alone(dve, dve2, MARKS * k + mark(1, last))
                for g in range(G):
                    last = V.bn_aggr(mv2[:, g, :], st2[:, g, :])
                last.then_inc(mv2_ready, 1)
                step(1)
                dve.wait_ge(mv2_ready, k + 1)
                for g in range(G):
                    last = STT(X1[:, g, :], OO[:, g, :], mv2[:, g, 0:1], pairs(STG[b][:, ARC["GW"]])[:, g, :],
                               ALU.subtract, ALU.mult)
                wait(mark(2, last))
                dve.wait_ge(rs2_ready, k + 1)
                for g in range(G):
                    last = STT(OG[:, g, :], X1[:, g, :], rs2[:, g, :], pairs(STG[b][:, ARC["GB"]])[:, g, :],
                               ALU.mult, ALU.add)
                last.then_inc(og_ready, 1)
                step(2)
                dve.wait_ge(att_ready, k + 1)
                TT(H1[:, at(k), :], STH[b][:, :, :].rearrange("p g d -> p (g d)").unsqueeze(1),
                   PS[:, 2, P:2 * P].unsqueeze(1), ALU.add).then_inc(h1_ready, 1)
                alone(dve, h1_ready, k + 1)
                for g in range(G):
                    last = V.bn_stats(st3[:, g, :], H1[:, at(k), g * D:(g + 1) * D])
                alone(dve, dve2, MARKS * k + mark(3, last))
                for g in range(G):
                    last = V.bn_aggr(mv3[:, g, :], st3[:, g, :])
                last.then_inc(mv3_ready, 1)
                dve.wait_ge(mv3_ready, k + 1)
                dve.wait_ge(rs3_ready, k + 1)
                for g in range(G):
                    last = TS(XN[:, g:g + 1, :], H1[:, at(k), g * D:(g + 1) * D], mv3[:, g, 0:1], rs3[:, g, :],
                              ALU.subtract, ALU.mult)
                last.then_inc(xn_ready, 1)
                dve.wait_ge(xn_ready, k + 1)
                dve.wait_ge(xr_ready, k + 1)
                TT(XD[:, :, 1, :], XN[:, :, :], XD[:, :, 0, :].bitcast(F32), ALU.subtract).then_inc(xd_ready, 1)
                step(3)
                dve.wait_ge(lg_ready, k + 1)
                wait(mark(4, TT(LG[:, :, :], PS[:, 2, 0:G * E].rearrange("p (g e) -> p g e", g=G),
                                gbias[:, :].unsqueeze(1).to_broadcast([P, G, E]), ALU.add)))
                mark(5, V.tensor_reduce(M1[:, :, :], LG[:, :, :], AX.X, ALU.max))
                mark(6, TT(DD[:, :, :, :], LG[:, :, :].unsqueeze(2).to_broadcast([P, G, E, E]),
                           LG[:, :, :].unsqueeze(3).to_broadcast([P, G, E, E]), ALU.subtract))
                wait(5)
                TT(LS[:, :, :], LG[:, :, :], M1[:, :, :].to_broadcast([P, G, E]), ALU.subtract).then_inc(ls_ready, 1)
                wait(6)
                dd = DD[:, :, :, :].rearrange("p g e f -> p (g e f)")
                wait(mark(7, STT(D1[:, :], dd, 0.0, const("tri"), ALU.is_equal, ALU.mult)))
                wait(mark(8, STT(D2[:, :, :, :].rearrange("p g e f -> p (g e f)"), dd, 0.0, D1[:, :], ALU.is_gt,
                                 ALU.add)))
                wait(mark(9, V.tensor_reduce(RKs[:, :, :].unsqueeze(3), D2[:, :, :, :], AX.X, ALU.add)))
                dve.wait_ge(pex_ready, k + 1)
                wait(mark(10, STT(PM[:, :, :], RKs[:, :, :], 2.0, PX[:, :, :], ALU.is_lt, ALU.mult)))
                wait(mark(11, V.tensor_reduce(SM[:, :, :], PM[:, :, :], AX.X, ALU.add)))
                wait(mark(12, V.reciprocal(RC[:, :, :], SM[:, :, :])))
                TT(CF[:, :, :], PM[:, :, :], RC[:, :, :].to_broadcast([P, G, E]), ALU.mult).then_inc(cf_ready, 1)

            def finish(p, n):
                dve.wait_ge(fin_ready, p + 1)
                h = H1[:, at(2 * p, n), :]
                TT(h, h, PS[:, 7, 0:n * G * D].rearrange("p (k d) -> p k d", k=n), ALU.add).then_inc(fin_done, 1)

            phase2(dve, chunk, expert, finish)

        @block.tensor
        def _(pe):
            mm = nc.tensor.matmul

            def transpose(dst, src):
                return nc.tensor.transpose(dst, src, ident)

            pe.wait_ge(l_const, 16)
            pe.wait_ge(xh_ready, 1)
            for h in range(2):
                for q in range(4):
                    last = transpose(PS[0:PH, h, q * P:(q + 1) * P], xh0[:, q, h * PH:(h + 1) * PH])
            last.then_inc(tr_ready, 1)
            pe.wait_ge(l_attw, 16)
            mm(PS[:, 7, 0:D], AW[0:D, ATTW["A_aT"]], AW[0:D, ATTW["B_a"]], start=True, stop=True)\
                .then_inc(aab_ready, 1)
            pe.wait_ge(l_tokw, 16)
            pe.wait_ge(nt_ready, 1)
            for q in range(4):
                for h in range(2):
                    last = mm(PS[:, 2, q * D:(q + 1) * D], xT0[0:PH, h, q * P:(q + 1) * P],
                              TW[0:PH, TOKW["W1"]][:, h * D:(h + 1) * D], start=h == 0, stop=h == 1)
            last.then_inc(mm_ready, 1)
            for i, w in ((1, "Wp1"), (2, "Wp2")):
                pe.wait_ge(xh_ready, i + 1)
                for c in range(2):
                    last = transpose(PS[:, i - 1, c * P:(c + 1) * P],
                                     n0[:, 2 * c:2 * c + 2, :].rearrange("p g d -> p (g d)"))
                last.then_inc(tr_ready, 1)
                pe.wait_ge(nt_ready, i + 1)
                for g in range(G):
                    rows_g = slice(g * D, (g + 1) * D)
                    for c in range(2):
                        last = mm(PS[:, 1 + i + g, c * D:(c + 1) * D], nT0[rows_g, c, :], TW[rows_g, TOKW[w]],
                                  start=True, stop=True)
                last.then_inc(mm_ready, 1)
            pe.wait_ge(xh_ready, 4)
            pe.wait_ge(mix_ready, 1)
            for q in range(10):
                last = transpose(PS[:, 5 + q // 4, (q % 4) * P:(q % 4 + 1) * P],
                                 XHD[:, q, :, :].rearrange("p w d -> p (w d)"))
            last.then_inc(tr_ready, 1)

            pe.wait_ge(memsets, 1)
            masks = const("masks")
            with pe.Fori(0, ROUNDS) as it:
                def bank(s, i):
                    return PS[:, 4 * s + i, :]

                def tile(t, g):
                    return t[:, g * P:(g + 1) * P]

                for s in range(2):
                    pe.wait_ge(x_staged, 2 * it + (s + 1))
                    for g in range(G):
                        last = mm(bank(s, 0)[:, g * 4 * D:(g + 1) * 4 * D], tile(XS[s], g), Wproj[:, :],
                                  start=True, stop=True)
                    last.then_inc(proj_ready, 1)
                    mm(bank(s, 1)[0:D, 0:G * P], Wlora[:, 0:D], XS[s][:, :], start=True, stop=True)
                    mm(bank(s, 1)[:, G * P:2 * G * P], Wlora[:, D:D + P], XS[s][:, :], start=True, stop=True)\
                        .then_inc(hid_ready, 1)
                for s in range(2):
                    pe.wait_ge(th_ready, 2 * it + (s + 1))
                    pe.wait_ge(sg_ready, 2 * it + (s + 1))
                    for g in range(G):
                        o = bank(s, 1)[:, g * 2 * D:(g + 1) * 2 * D]
                        mm(o[:, 0:D], tile(TH[s], g), AW[0:D + 1, ATTW["B_w"]], start=True, stop=True)
                        last = mm(o[:, D:2 * D], tile(SG[s], g), AW[:, ATTW["B_g"]], start=True, stop=True)
                    last.then_inc(wg_ready, 1)
                for s in range(2):
                    pe.wait_ge(w_ready, 2 * it + (s + 1))
                    lw = LW[s][:, :, :].rearrange("p g d -> p (g d)")
                    for i, m in enumerate((masks[:, P:2 * P], masks[:, 0:P], const("suffix"))):
                        mm(bank(s, 2)[:, i * P:(i + 1) * P], m, lw, start=True, stop=True)
                    for g in range(G):
                        last = mm(bank(s, 2)[g * D:(g + 1) * D, 3 * P:3 * P + J], LW[s][:, g, :], const("seq"),
                                  start=True, stop=True)
                    last.then_inc(cum_ready, 1)
                for s in range(2):
                    pe.wait_ge(hat_ready, 2 * it + (s + 1))
                    for w in range(4):
                        last = transpose(bank(s, 0)[:, w * P:(w + 1) * P],
                                         HAT[s][:, w, :, :].rearrange("p g d -> p (g d)"))
                    last.then_inc(ft_ready, 1)
                for s in range(2):
                    pe.wait_ge(ftc_ready, 2 * it + (s + 1))
                    for g in range(G):
                        f = FT[s][g * D:(g + 1) * D, :, :]
                        ar = f[:, 0:2, :].rearrange("p w t -> p (w t)")
                        mm(bank(s, 2 + g)[:, 0:2 * P], f[:, 2, :], ar, start=True, stop=True)
                        mm(bank(s, 2 + g)[:, 2 * P:4 * P], f[:, 3, :], ar, start=True, stop=True).then_inc(l_ready, 1)
                for s in range(2):
                    pe.wait_ge(q_ready, level(it, 0, s, 5))
                    for g in range(G):
                        last = transpose(bank(s, 3)[:, g * P:(g + 1) * P], QT[s][:, g, :])
                    last.then_inc(p1t_ready, 1)
                for s in range(2):
                    pe.wait_ge(vb_ready, 2 * it + (s + 1))
                    pe.wait_ge(kp_ready, 2 * it + (s + 1))
                    for g in range(G):
                        mm(bank(s, 1)[:, g * D:(g + 1) * D], LKT[s][:, g, 0, :], RK[s][:, g, 2, :],
                           start=True, stop=True)
                        mm(bank(s, 1)[:, P + g * D:P + (g + 1) * D], LKT[s][:, g, 1, :], RK[s][:, g, 2, :],
                           start=True, stop=True)
                        last = mm(bank(s, 1)[g * D:(g + 1) * D, 2 * P:4 * P], KP[s][:, g, :],
                                  VB[s][:, g, :, :].rearrange("p j d -> p (j d)"), start=True, stop=True)
                    last.then_inc(lvov_ready, 1)
                for li in range(4):
                    for s in range(2):
                        if li == 0:
                            pe.wait_ge(p1_ready, 2 * it + (s + 1))
                        else:
                            pe.wait_ge(pu_ready, level(it, li - 1, s, 3))
                        for g in range(G):
                            last = mm(bank(s, 2)[:, g * P:(g + 1) * P], AT[s][:, g, :], PI[s][:, g, :],
                                      start=True, stop=True)
                        last.then_inc(y_ready, 1)
                    for s in range(2):
                        pe.wait_ge(q_ready, level(it, li, s, 5))
                        pe.wait_ge(ysb_ready, level(it, li, s, 4))
                        if li < 3:
                            for g in range(G):
                                last = mm(bank(s, 3)[:, g * P:(g + 1) * P], QT[s][:, g, :], YI[s][:, g, :],
                                          start=True, stop=True)
                            last.then_inc(pp_ready, 1)
                        for g in range(G):
                            last = mm(bank(s, 0)[:, g * P:(g + 1) * P], YI[s][:, g, :], QT[s][:, g, :],
                                      start=True, stop=True)
                        last.then_inc(qq_ready, 1)
                for s in range(2):
                    pe.wait_ge(lv_ready, 2 * it + (s + 1))
                    pe.wait_ge(q_ready, level(it, 4, s, 5))
                    for g in range(G):
                        mm(bank(s, 2)[:, g * D:(g + 1) * D], QT[s][:, g, :], LV[s][:, g, :], start=True, stop=True)
                        last = mm(bank(s, 2)[g * D:(g + 1) * D, P:2 * P], HAT[s][:, 0, g, :], QT[s][:, g, :],
                                  start=True, stop=True)
                    last.then_inc(uw_ready, 1)

            pe.sem_inc(y_done, 2)
            pe.wait_ge(arch_act, NU)

            def second(p, e, n):
                pe.wait_ge(hc_done, E * p + (e + 3))
                half = slice((e % 2) * D, (e % 2 + 1) * D)
                last = mm(PS[half, 7, 0:n * G * P], W2[:, e * D:(e + 1) * D],
                          HC[e % 2][:, 0:n * G * P], start=e < 2, stop=False)
                last.then_inc(y_done, 1)

            def expert(p, e, n):
                o = PS[:, 4 + e % 2, 0:n * G * P]
                pe.wait_ge(xhl_ready, 2 * p + n)
                pe.wait_ge(relu_done, E * p + (e + 1))
                mm(o, W1h[:, e * EH:(e + 1) * EH], XHL[:, at(2 * p, n), :], start=True, stop=False)
                mm(o, W1l[:, e * EH:(e + 1) * EH], XHL[:, at(2 * p, n), :], start=False, stop=True)\
                    .then_inc(z_ready, 1)
                pe.wait_ge(ctc_ready, 2 * p + n)
                alone(pe, hc_done, E * p + (e + 1))
                mm(PS[:, 3 + 3 * (e % 2), 0:n * G * P], pickB[:, e * P:(e + 1) * P], CTB[:, at(2 * p, n), :],
                   start=True, stop=True).then_inc(c_ready, 1)
                if e == 0:
                    pe.wait_ge(fin_done, p + 1)
                else:
                    second(p, e - 1, n)

            def chunk(k, b, step):
                def stage(name):
                    return STG[b][:, ARC[name]]

                pe.wait_ge(stg[b], loaded(k, b))
                if not (isinstance(k, int) and k == 0):
                    pe.wait_ge(s_ready, k)
                    alone(pe, oo_ready, k)
                for g in range(G):
                    rows_g = slice(g * D, (g + 1) * D)
                    for j in range(J):
                        last = mm(PS[j * C:(j + 1) * C, g, 0:D], stage("Wf")[rows_g, j * C:(j + 1) * C],
                                  ST[b][rows_g, j * D:(j + 1) * D], start=True, stop=True)
                last.then_inc(sap_ready, 1)
                step(0)
                alone(pe, sa_ready, k + 1)
                for g in range(G):
                    rows_g = slice(g * D, (g + 1) * D)
                    for j in range(J):
                        mm(PS[j * C:(j + 1) * C, g, D:2 * D], stage("Rf")[rows_g, j * C:(j + 1) * C],
                           ST[b][rows_g, j * D:(j + 1) * D], start=True, stop=False)
                    mm(PS[:, g, D:2 * D], stage("LrbT")[:, g * P:(g + 1) * P], SA[:, g, :], start=False, stop=True)
                pe.wait_ge(sab_ready, k + 1)
                for g in range(G):
                    last = mm(PS[g * D:(g + 1) * D, 0, 3 * D:3 * D + J * D], stage("Bp")[:, g * D:(g + 1) * D],
                              SAB[:, g, :, :].rearrange("p j d -> p (j d)"), start=True, stop=True)
                last.then_inc(sps_ready, 1)
                step(1)
                if not (isinstance(k, int) and k == 0):
                    pe.wait_ge(ctc_ready, k)
                pe.wait_ge(og_ready, k + 1)
                transpose(PS[:, 2, 0:P], OG[:, :, :].rearrange("p g d -> p (g d)")).then_inc(ogt_ready, 1)
                step(2)
                pe.wait_ge(ogtc_ready, k + 1)
                mm(PS[:, 2, P:2 * P], OGT[:, :], AW[:, ATTW["W_o"]], start=True, stop=True).then_inc(att_ready, 1)
                step(3)
                pe.wait_ge(xr_ready, k + 1)
                pe.wait_ge(xd_ready, k + 1)
                for g in range(G):
                    last = transpose(PS[:, 2, (2 + g) * P:(3 + g) * P],
                                     XD[:, g, :, :].rearrange("p w d -> p (w d)").bitcast(F32))
                last.then_inc(x2t_ready, 1)
                pe.wait_ge(x2s_ready, k + 1)
                for g in range(G):
                    last = mm(PS[:, 2, g * E:(g + 1) * E], X2S[:, g * P:(g + 1) * P], AW[:, ATTW["Wg"]],
                              start=True, stop=True)
                last.then_inc(lg_ready, 1)
                pe.wait_ge(cp_ready, k + 1)
                for g in range(G):
                    last = transpose(PS[0:24, 2, (1 + g) * P:(2 + g) * P],
                                     CP[:, g, :, :].rearrange("p w e -> p (w e)"))
                last.then_inc(ct_ready, 1)

            def finish(p, n):
                second(p, E - 1, n)
                mm(PS[:, 7, 0:n * G * P], AW[0:24, ATTW["b2"]], CTF[:, at(2 * p, n), :], start=False, stop=True)\
                    .then_inc(y_sum, 1)
                pe.wait_ge(ys_ready, p + 1)
                for i in range(n * G):
                    last = mm(PS[:, 7, i * D:(i + 1) * D], YS[:, i * P:(i + 1) * P], const("fold"),
                              start=True, stop=True)
                last.then_inc(fin_ready, 1)

            phase2(pe, chunk, expert, finish)


def kernel(**inputs):
    import numpy as _np
    import concourse.bacc as _bacc
    from concourse import mybir as _mybir
    from concourse.bass_utils import run_bass_kernel_spmd as _run

    w = {name.replace("L0_", ""): _np.asarray(a) for name, a in inputs.items()}

    def packed(height, layout, width, **parts):
        t = _np.zeros((height, width), _np.float32)
        for name, a in parts.items():
            t[:a.shape[0], layout[name]] = a
        return t

    def twice(a):
        return _np.concatenate([a, a], 0)

    side = IMG // 8
    patches = w["x"].reshape(BATCH, 3, side, 8, side, 8).transpose(0, 2, 4, 3, 5, 1).reshape(BATCH, IMG, PATCH)
    patches = patches.reshape(G, J, NIMG, C, PATCH).transpose(1, 3, 2, 0, 4).reshape(P, NIMG * G, PATCH)
    text = _np.zeros((BATCH, NTXT * C, D), _np.float32)
    text[:, :TXT] = w["txt"]
    text = text.reshape(G, J, NTXT, C, D).transpose(1, 3, 2, 0, 4).reshape(P, NTXT * G, D)

    rows = packed(1, ROWS, NROWS, b1=w["tok_b1"][None], bp1=w["tok_bp1"][None], bp2=w["tok_bp2"][None],
                  k_k=w["attn_k_k"][None], k_a=w["attn_k_a"][None], r_k=w["attn_r_k"][None],
                  gn_w=w["attn_gn_w"][None], gn_b=w["attn_gn_b"][None], b_a=w["attn_b_a"][None],
                  bg=w["ffn_bg"][None], bias=w["ffn_bias"][None])
    cols = packed(P, COLS, NCOLS, ln1_g=w["tok_ln1_g"].reshape(2, PH).T, ln1_b=w["tok_ln1_b"].reshape(2, PH).T,
                  ln2_g=twice(w["tok_ln2_g"][:, None]), ln2_b=twice(w["tok_ln2_b"][:, None]),
                  lnp_g=twice(w["tok_lnp_g"][:, None]), lnp_b=twice(w["tok_lnp_b"][:, None]),
                  mix=twice(w["attn_x_mix"].T), b1e=w["ffn_b1"].T)
    tokw = packed(P, TOKW, NTOKW, W1=w["tok_W1"].reshape(2, PH, D).transpose(1, 0, 2).reshape(PH, 2 * D),
                  Wp1=twice(w["tok_Wp1"]), Wp2=twice(w["tok_Wp2"]))
    W_o = _np.zeros((2, D, 2, D), _np.float32)
    W_o[0, :, 0] = W_o[1, :, 1] = w["attn_W_o"]
    b2 = _np.zeros((3, E, P), _np.float32)
    b2[:, :, :D] = w["ffn_b2"]
    attw = packed(P, ATTW, NATTW, rkv=twice(_np.concatenate([w["attn_W_r"], w["attn_W_k"], w["attn_W_v"]], 1)),
                  A_w=twice(w["attn_A_w"]), A_g=twice(w["attn_A_g"]),
                  A_aT=_np.concatenate([w["attn_A_a"].T] * 2, 1), B_a=w["attn_B_a"],
                  B_w=_np.concatenate([w["attn_B_w"], w["attn_b_w"][None]], 0), B_g=w["attn_B_g"],
                  W_o=W_o.reshape(P, P), Wg=twice(w["ffn_Wg"]), b2=b2.reshape(3 * E, P))
    w1 = twice(w["ffn_W1"].transpose(1, 0, 2).reshape(D, E * EH))
    w2 = w["ffn_W2"].transpose(1, 0, 2).reshape(EH, E * D)

    nc = _bacc.Bacc("TRN2", target_bir_lowering=False, num_devices=1)
    arrays, args = {}, []
    for name, a in (("patches", patches), ("text", text), ("consts", constants()), ("pick", picks()),
                    ("rows", rows), ("cols", cols), ("tokw", tokw), ("attw", attw), ("w1", w1), ("w2", w2)):
        a = _np.ascontiguousarray(a)
        arrays[f"in_{name}"] = a
        args.append(nc.dram_tensor(f"in_{name}", a.shape, _mybir.dt.from_np(a.dtype), kind="ExternalInput").ap())
    out = nc.dram_tensor("out_h", (P, NCH * G * D), F32, kind="ExternalOutput").ap()
    build(nc, *args, out)
    r = _run(nc, [arrays], core_ids=[0])
    got = r.results[0]["out_h"].reshape(J, C, NCH, G, D).transpose(3, 0, 2, 1, 4).reshape(BATCH, NCH * C, D)
    return got[:, :SEQ]
```

```python
from contextlib import ExitStack

import numpy as np
import concourse.bass as bass
from concourse import mybir

F32 = mybir.dt.float32
F32R = mybir.dt.float32r
BF16 = mybir.dt.bfloat16
ALU = mybir.AluOpType
ACT = mybir.ActivationFunctionType
AX = mybir.AxisListType

P = 128
D = 64
BATCH = 8
G = 2
J = 4
C = 32
IMG = 64
TXT = 77
SEQ = 3 * IMG + TXT
PATCH = 192
PH = PATCH // 2
NIMG = IMG // C
NTXT = -(-TXT // C)
NCH = 3 * NIMG + NTXT
NU = 1 + NIMG + NTXT
ROUNDS = NU // 2
E = 8
EH = 128
T = 3
GROUPS = NCH // T
Q = T * G
HALF = Q // 2
LEVELS = (2, 4, 8, 16)
EPS = 1e-5
GN_EPS = D * 1e-5
DECAY = -0.6065306597126334


def columns(*widths):
    at, out = 0, {}
    for name, width in widths:
        out[name] = slice(at, at + width)
        at += width
    return out, at


CONST, NCONST = columns(("ident", P), ("masks", 2 * P), ("suffix", P), ("m1", P),
                        *((f"m{l}", P) for l in LEVELS), ("seq", J), ("block", J * D),
                        ("tri", E * E), ("fold", D))
ROWS, NROWS = columns(("b1", D), ("bp1", D), ("bp2", D), ("k_k", D), ("k_a", D), ("r_k", D), ("gn_w", D),
                      ("gn_b", D), ("b_a", D), ("bg", E), ("bias", E))
COLS, NCOLS = columns(("ln1_g", 2), ("ln1_b", 2), ("ln2_g", 1), ("ln2_b", 1), ("lnp_g", 1), ("lnp_b", 1),
                      ("mix", 6), ("b1e", E))
TOKW, NTOKW = columns(("W1", 2 * D), ("Wp1", D), ("Wp2", D))
ATTW, NATTW = columns(("rkv", 3 * D), ("A_w", D), ("A_g", P), ("A_aT", P), ("B_a", D), ("B_w", D), ("B_g", D),
                      ("W_o", 2 * D), ("Wg", E), ("b2", P))
ARC, NARC = columns(("U", P), ("Wf", G * P), ("OV", P), ("H", 2 * P), ("GW", P), ("GB", P), ("Bp", G * J * D),
                    ("LrbT", 2 * P), ("Rf", G * P), ("E", J))


def constants():
    i = np.arange(P)
    same = (i[:, None] // C) == (i[None, :] // C)
    su = (same & (i[:, None] < i[None, :])).astype(np.float32)
    iu = (same & (i[:, None] <= i[None, :])).astype(np.float32)
    t = np.zeros((P, NCONST), np.float32)
    t[:, CONST["ident"]] = np.eye(P)
    t[:, CONST["masks"]] = np.concatenate([su, iu], 1)
    t[:, CONST["suffix"]] = su.T
    def merged(l):
        return ((i[:, None] // (2 * l) == i[None, :] // (2 * l)) & (i[:, None] % (2 * l) >= l)
                & (i[None, :] % (2 * l) < l)).astype(np.float32)
    t[:, CONST["m1"]] = merged(1).T
    for l in LEVELS:
        t[:, CONST[f"m{l}"]] = merged(l)
    seq = (i[:, None] // C == np.arange(J)[None, :]).astype(np.float32)
    t[:, CONST["seq"]] = seq
    t[:, CONST["block"]] = np.repeat(seq, D, 1)
    e = np.arange(E)
    t[:, CONST["tri"]] = (e[None, :] < e[:, None]).reshape(1, -1)
    t[:, CONST["fold"]] = np.tile(np.eye(D), (2, 1))
    return t


def picks():
    pick = np.zeros((2, E, E, P), np.float32)
    for e in range(E):
        pick[:, e, e] = 1.0
    return pick.reshape(2 * E, E * P)


def build(nc, patches, text, consts, pick, rows, cols, tokw, attw, w1, w2, out):
    ctx = ExitStack()
    with ctx:
        def sb(name, shape, dt=F32):
            return ctx.enter_context(nc.sbuf_tensor(name, shape, dt))

        def sem(name):
            return ctx.enter_context(nc.semaphore(name))

        PT = sb("PT", [P, 4, PATCH])
        KC = sb("KC", [P, NCONST])
        RW = sb("RW", [P, NROWS])
        CL = sb("CL", [P, NCOLS])
        TW = sb("TW", [P, NTOKW])
        AW = sb("AW", [P, NATTW])
        W2 = sb("W2", [P, E * D])

        def const(name):
            return KC[:, CONST[name]]

        def twice(ap):
            return ap.unsqueeze(1).to_broadcast([P, G, P])

        def row(name, n=2):
            v = RW[:, ROWS[name]]
            return v.unsqueeze(1).to_broadcast([P, n, v.shape[1]])

        def pairs(ap):
            return ap.rearrange("p (g d) -> p g d", g=2)

        ident = const("ident")
        Wproj = sb("Wproj", [P, 4 * D])
        Wlora = sb("Wlora", [P, D + P])
        mix = sb("mix", [P, 6])
        kaH = sb("kaH", [P, D])
        gbias = sb("gbias", [P, E])
        lnpH = sb("lnpH", [P, 2])
        PK = sb("PK", [2 * E, E * P], F32R)
        W1h = sb("W1h", [P, E * EH], F32R)
        W1l = sb("W1l", [P, E * EH], F32R)

        st0 = sb("st0", [P, 10, 6])
        mv0 = sb("mv0", [P, 10, 2])
        half = sb("half", [P, Q])
        rs0 = sb("rs0", [P, 10, 1])
        xh0 = sb("xh0", [P, 4, PATCH])
        xT0 = sb("xT0", [P, 2, 4 * P])
        P0 = sb("P0", [P, 4, 4 * D])
        t0, n0 = (P0[:, i, :].rearrange("p (q d) -> p q d", q=4) for i in range(2))
        nT0, th0 = (P0[:, i, :].rearrange("p (c t) -> p c t", c=2) for i in (2, 3))
        HT = sb("HT", [P, 10, D])
        XHD = sb("XHD", [P, 10, 2, D])
        XT = sb("XT", [P, NU + 2, G, J, C])

        def two(name, shape, dt=F32):
            return [sb(f"{name}{s}", shape, dt) for s in range(2)]

        XS = two("XS", [P, G * P])
        RK = two("RK", [P, G, 4, D])
        TH = two("TH", [P, G * P])
        SG = two("SG", [P, G * P])
        ZA = two("ZA", [P, G, D])
        TA = two("TA", [P, G, D])
        TWd = two("TWd", [P, G, D])
        LW = two("LW", [P, G, D])
        KK = two("KK", [P, G, D])
        SQ = two("SQ", [P, G, D])
        SS = two("SS", [P, G, 1])
        RN = two("RN", [P, G, 1])
        KN = two("KN", [P, G, D])
        RR = two("RR", [P, G, D])
        T1 = two("T1", [P, G, D])
        K2 = two("K2", [P, G, D])
        B2 = two("B2", [P, G, D])
        MM = SQ
        BON = two("BON", [P, G, 1])
        VBN = T1
        EX = two("EX", [P, 3, G, D])
        NN = two("NN", [P, G, D])
        HAT = two("HAT", [P, 4, G, D])
        BP = two("BP", [P, G, D])
        KP = two("KP", [P, G, D])
        FA = two("FA", [P, 2, P])
        FZ = two("FZ", [P, G, 2, P])
        AT = two("AT", [P, G, P])
        LKT = two("LKT", [P, G, 2, P])
        VB = two("VB", [P, G, J, D])
        QT = two("QT", [P, G, P])
        PI = two("PI", [P, G, P])
        YI = two("YI", [P, G, P])
        QA = YI
        LV = two("LV", [P, G, D])
        ARCH = sb("ARCH", [P, NU, NARC])
        W1raw = ARCH[:, 0, ARC["OV"].start:ARC["OV"].start + E * EH]
        pickraw = ARCH[0:2 * E, 1, ARC["OV"].start:ARC["OV"].start + E * P]

        ST = two("ST", [P, J * D])
        ES = sb("ES", [P, J * D])
        EHs = sb("EHs", [P, J * D])
        SA = sb("SA", [P, G, D])
        OO = sb("OO", [P, NCH * G, D])
        H1 = sb("H1", [P, NCH * G, D])
        XHL = [sb(f"XHL{i}", [P, Q, P], F32R) for i in range(GROUPS)]
        CF = sb("CF", [P, GROUPS * Q, E])
        st2 = sb("st2", [P, Q, 6])
        mv2 = sb("mv2", [P, Q, 2])
        rs2 = sb("rs2", [P, Q, 1])
        ve2 = sb("ve2", [P, Q, 1])
        st3, mv3, rs3, ve3 = (sb(n, [P, Q, w]) for n, w in (("st3", 6), ("mv3", 2), ("rs3", 1), ("ve3", 1)))
        OG = P0[:, :, :].rearrange("p i c -> p (i c)")[:, 0:Q * D].rearrange("p (q d) -> p q d", q=Q)
        OGT = P0[:, :, :].rearrange("p i c -> p (i c)")[:, Q * D:Q * D + T * P].rearrange("p (c t) -> p c t", c=T)
        XD = sb("XD", [P, Q, 2, D], F32R)
        LG = sb("LG", [P, Q, E])
        M1 = sb("M1", [P, Q, 1])
        LS = sb("LS", [P, Q, E])
        PX = sb("PX", [P, Q, E])
        D2 = sb("D2", [P, Q, E, E])
        RKs = sb("RKs", [P, Q, E])
        PM = sb("PM", [P, Q, E])
        SM = sb("SM", [P, Q, 1])
        RC = sb("RC", [P, Q, 1])
        CP = sb("CP", [P, Q, 2, E])
        CT = two("CT", [2 * E, Q * P], F32R)
        X1, XN = (PT[:, :, :].rearrange("p q d -> p (q d)")[:, i * Q * D:(i + 1) * Q * D].rearrange(
            "p (q d) -> p q d", q=Q) for i in range(2))
        DD, D1 = (xh0[:, :, :].rearrange("p q d -> p (q d)")[:, i * Q * E * E:(i + 1) * Q * E * E].rearrange(
            "p (q e f) -> p q e f", q=Q, e=E) for i in range(2))
        RL = [xT0[:, i, 0:HALF * P] for i in range(2)]
        HC = [sb(f"HC{i}", [P, HALF * P]) for i in range(4)]
        YS = sb("YS", [P, HALF * P])

        PS = ctx.enter_context(nc.psum_tensor("PS", [P, 8, 512], F32))

        def sems(names):
            return [sem(n) for n in names.split()]

        l_patch, l_text, l_ident, l_const, l_pick, l_rows, l_cols, l_tokw, l_attw, l_w1, l_w2 = sems(
            "l_patch l_text l_ident l_const l_pick l_rows l_cols l_tokw l_attw l_w1 l_w2")
        var_ready, rs_ready, xh_ready, tr_ready, nt_ready, mm_ready, zh_ready, zt_ready = sems(
            "var_ready rs_ready xh_ready tr_ready nt_ready mm_ready zh_ready zt_ready")
        dve0, pool0 = sems("dve0 pool0")
        memsets, xt_dve, xt_act, w_rounded, w_rest, pick_ready, mix_ready, aab_ready = sems(
            "memsets xt_dve xt_act w_rounded w_rest pick_ready mix_ready aab_ready")
        (x_staged, proj_ready, hid_ready, rk_ready, th_ready, sgt_ready, sg_ready, za_ready, ta_ready, wg_ready,
         tw_ready, w_ready, cum_ready, ex_ready, ss_ready, rn_ready, hat_ready, kp_ready, ft_ready, ftc_ready,
         l_ready, p1t_ready, p1_ready) = sems(
             "x_staged proj_ready hid_ready rk_ready th_ready sgt_ready sg_ready za_ready ta_ready wg_ready "
             "tw_ready w_ready cum_ready ex_ready ss_ready rn_ready hat_ready kp_ready ft_ready ftc_ready "
             "l_ready p1t_ready p1_ready")
        (y_ready, ysb_ready, pp_ready, pu_ready, qq_ready, q_ready, lvov_ready, lv_ready, uw_ready, vb_ready,
         arch_act, arch_dve, arch_pool, bp_ready, dve1, pool1) = sems(
             "y_ready ysb_ready pp_ready pu_ready qq_ready q_ready lvov_ready lv_ready uw_ready vb_ready "
             "arch_act arch_dve arch_pool bp_ready dve1 pool1")
        s_ready, sap_ready, sa_ready, ops_ready, sps_ready, eh_ready, es_ready, oo_ready = sems(
            "s_ready sap_ready sa_ready ops_ready sps_ready eh_ready es_ready oo_ready")
        (mv2_ready, rs2_ready, og_ready, ogt_ready, ogtc_ready, att_ready, mv3_ready, rs3_ready, xn_ready,
         x1_ready, rank_ready, xr_ready, xd_ready, x2t_ready, xhl_ready, lg_ready, ls_ready, pex_ready, cf_ready, cr_ready, cp_ready, ct_ready,
         ctc_ready) = sems(
             "mv2_ready rs2_ready og_ready ogt_ready ogtc_ready att_ready mv3_ready rs3_ready xn_ready "
             "x1_ready rank_ready xr_ready xd_ready x2t_ready xhl_ready lg_ready ls_ready pex_ready cf_ready cr_ready cp_ready "
             "ct_ready ctc_ready")
        z_ready, c_ready, relu_done, hc_done, y_done, y_sum, ys_ready, fin_ready, fin_done, stored = sems(
            "z_ready c_ready relu_done hc_done y_done y_sum ys_ready fin_ready fin_done stored")
        dve2, pool2, passed = sems("dve2 pool2 passed")

        block = ctx.enter_context(nc.Block())

        class Chain:

            def __init__(self, eng, s, per=0):
                self.eng, self.s, self.per, self.n = eng, s, per, 0

            def mark(self, ins):
                self.n += 1
                ins.then_inc(self.s, 1)
                return self.n

            def wait(self, n, r=0):
                self.eng.wait_ge(self.s, r * self.per + n)

            def link(self, ins, r=0):
                self.wait(self.mark(ins), r)

        def alone(eng, s, value):
            eng.wait_ge(s, value)
            if not isinstance(value, int):
                eng.sem_inc(passed, 1)

        SLOT = [0, 1, 2, 1, 2, 1] + list(range(NU - NTXT, NU))
        HQ = [2 * (k % NIMG) for k in range(3 * NIMG)] + [2 * NIMG + 2 * t for t in range(NTXT)]

        def at(k, n=1):
            return slice(k, k + n) if isinstance(k, int) else bass.ds(k, n)

        def skip(*_):
            pass

        def level(it, li, s, levels):
            return it * (2 * levels) + (2 * li + s + 1)

        OUT_BANK = (2, 7, 1)
        FFN_BANK = (2, 0, 1)

        def phase2(scan_a=skip, scan_b=skip, stats=skip, centre=skip, heads=skip, att=skip, split=skip, rest=skip,
                   feat=skip, rank=skip, choose=skip, parts=skip, weights=skip, experts=skip, total=skip, fold=skip):
            for k in range(T):
                scan_a(k)
                scan_b(k)
            scan_a(3)
            stats(0)
            scan_b(3)
            centre(0)
            scan_a(4)
            heads(0)
            scan_b(4)
            att(0)
            scan_a(5)
            scan_b(5)
            split(0)
            scan_a(6)
            stats(1)
            rest(0)
            scan_b(6)
            feat(0, 0)
            centre(1)
            scan_a(7)
            heads(1)
            feat(0, 1)
            scan_b(7)
            rank(0)
            att(1)
            scan_a(8)
            choose(0)
            scan_b(8)
            parts(0)
            split(1)
            weights(0, 0)
            weights(0, 1)
            stats(2)
            rest(1)
            experts(0, 0)
            centre(2)
            feat(1, 0)
            experts(0, 1)
            heads(2)
            feat(1, 1)
            experts(0, 2)
            rank(1)
            att(2)
            experts(0, 3)
            choose(1)
            experts(1, 0)
            total(0)
            split(2)
            parts(1)
            weights(1, 0)
            rest(2)
            fold(0)
            weights(1, 1)
            experts(1, 1)
            feat(2, 0)
            experts(1, 2)
            feat(2, 1)
            experts(1, 3)
            rank(2)
            experts(2, 0)
            total(1)
            choose(2)
            fold(1)
            experts(2, 1)
            parts(2)
            experts(2, 2)
            weights(2, 0)
            weights(2, 1)
            experts(2, 3)
            for u in range(3, 2 * GROUPS):
                experts(u, 0)
                total(u - 1)
                experts(u, 1)
                fold(u - 1)
                for v in range(2, E // 2):
                    experts(u, v)
            total(2 * GROUPS - 1)
            fold(2 * GROUPS - 1)

        @block.sync
        def _(sp):
            sp.dma_start(PT[:, :, :], patches).then_inc(l_patch, 16)
            sp.dma_start(KC[:, 0:P], consts[:, 0:P]).then_inc(l_ident, 16)
            sp.dma_start(KC[:, P:], consts[:, P:]).then_inc(l_const, 16)
            sp.dma_start(AW[:, :], attw).then_inc(l_attw, 16)
            sp.dma_start(W1raw, w1).then_inc(l_w1, 16)
            sp.dma_start(W2[:, :], w2).then_inc(l_w2, 16)
            width = HALF * D
            for u in range(2 * GROUPS):
                sp.wait_ge(fin_done, u + 1)
                sp.dma_start(out[:, u * width:(u + 1) * width],
                             H1[:, u * HALF:(u + 1) * HALF, :].rearrange("p q d -> p (q d)")).then_inc(stored, 16)
            sp.wait_ge(stored, 16 * 2 * GROUPS)

        @block.gpsimd
        def _(pool):
            c0 = Chain(pool, pool0)
            c0.link(nc.gpsimd.memset(half[:, :], -0.5))
            def clear():
                c0.link(nc.gpsimd.memset(XT[:, NU:, :, :, :], 0.0))
                c0.link(nc.gpsimd.memset(XT[D:P, 0, :, :, 0:1], 0.0))
                for s in range(2):
                    c0.link(nc.gpsimd.memset(TH[s][D:P, :], 0.0))
                    c0.link(nc.gpsimd.memset(TH[s][D:D + 1, :], 1.0))
                    c0.link(nc.gpsimd.memset(FZ[s][0:D, 1, :, :], 0.0))
                    c0.link(nc.gpsimd.memset(FZ[s][D:P, 0, :, :], 0.0))
                for name in ("Wf", "Rf"):
                    w = ARC[name]
                    c0.link(nc.gpsimd.memset(ARCH[0:D, :, w.start + P:w.stop], 0.0))
                    c0.link(nc.gpsimd.memset(ARCH[D:P, :, w.start:w.start + P], 0.0))
                nc.gpsimd.memset(ST[0][:, :], 0.0).then_inc(memsets, 1)
                pool.wait_ge(memsets, 1)

            for i, (a, b) in enumerate(((0, 4), (4, 10), (0, 4), (0, 4), (0, 4))):
                pool.wait_ge(var_ready, i + 1)
                c0.link(nc.gpsimd.tensor_scalar(rs0[:, a:b, :], mv0[:, a:b, 1:2], EPS, None, ALU.add))
                nc.gpsimd.tensor_tensor(rs0[:, a:b, :], rs0[:, a:b, :], half[:, 0:b - a].unsqueeze(2), ALU.pow)\
                    .then_inc(rs_ready, 1)
                if i == 0:
                    clear()
                if i == 1:
                    pool.wait_ge(w_rounded, 1)
                    nc.gpsimd.tensor_tensor(W1l[:, :], W1raw, W1h[:, :].bitcast(F32), ALU.subtract)\
                        .then_inc(w_rest, 1)

            def stage(n, s):
                nc.gpsimd.tensor_copy(XS[s][:, :].unsqueeze(1),
                                      XT[:, at(n), :, :, :].rearrange("p u g j c -> p u (g j c)"))\
                    .then_inc(x_staged, 1)

            pool.wait_ge(l_const, 16)
            pool.wait_ge(xt_dve, 1)
            pool.wait_ge(xt_act, 1)
            pool.wait_ge(memsets, 1)
            for s in range(2):
                stage(s, s)

            c1 = Chain(pool, pool1, 2)
            with pool.Fori(0, ROUNDS) as it:
                for s in range(2):
                    alone(pool, sgt_ready, 2 * it + (s + 1))
                    nc.gpsimd.tensor_scalar(SG[s][:, :], SG[s][:, :], 0.5, 0.5, ALU.mult, ALU.add)\
                        .then_inc(sg_ready, 1)
                for s in range(2):
                    alone(pool, ss_ready, 2 * it + (s + 1))
                    c1.link(nc.gpsimd.tensor_scalar(RN[s][:, :, :], SS[s][:, :, :], 1e-24, None, ALU.max), it)
                    nc.gpsimd.tensor_tensor(RN[s][:, :, :], RN[s][:, :, :], half[:, 0:G].unsqueeze(2), ALU.pow)\
                        .then_inc(rn_ready, 1)
                for s in range(2):
                    alone(pool, hid_ready, 2 * it + (s + 1))
                    stage(2 * it + (s + 2), s)
                for s in range(2):
                    pool.wait_ge(rk_ready, 2 * it + (s + 1))
                    for g in range(G):
                        last = nc.gpsimd.tensor_tensor(
                            VB[s][:, g, :, :], RK[s][:, g, 2:3, :].to_broadcast([P, J, D]),
                            const("block").rearrange("p (j d) -> p j d", j=J), ALU.mult)
                    last.then_inc(vb_ready, 1)
                for s in range(2):
                    pool.wait_ge(bp_ready, 2 * it + (s + 1))
                    for g in range(G):
                        w = ARC["Bp"].start + g * J * D
                        last = nc.gpsimd.tensor_tensor(
                            ARCH[:, at(2 * it + s), w:w + J * D].rearrange("p u (j d) -> p (u j) d", j=J),
                            BP[s][:, g:g + 1, :].to_broadcast([P, J, D]),
                            const("block").rearrange("p (j d) -> p j d", j=J), ALU.mult)
                    last.then_inc(arch_pool, 1)
            assert c1.n == c1.per

            c2 = Chain(pool, pool2)
            pool.wait_ge(arch_act, NU)
            pool.wait_ge(memsets, 1)

            def scan_a(k):
                if k:
                    pool.wait_ge(s_ready, k)
                u = SLOT[k]
                nc.gpsimd.tensor_tensor(ES[:, :].rearrange("p (j d) -> p j d", j=J),
                                        ST[k % 2][:, :].rearrange("p (j d) -> p j d", j=J),
                                        ARCH[:, u, ARC["E"]].unsqueeze(2).to_broadcast([P, J, D]), ALU.mult)\
                    .then_inc(es_ready, 1)
                pool.wait_ge(es_ready, k + 1)
                nc.gpsimd.tensor_tensor(EHs[:, :], ES[:, :], ARCH[:, u, ARC["H"]], ALU.add).then_inc(eh_ready, 1)

            def rsqrt(mv, ve, rs, eps, done):
                c2.link(nc.gpsimd.tensor_scalar(ve[:, :, :], mv[:, :, 1:2], eps, None, ALU.add))
                nc.gpsimd.tensor_tensor(rs[:, :, :], ve[:, :, :], half[:, 0:Q].unsqueeze(2), ALU.pow)\
                    .then_inc(done, 1)

            def stats(i):
                pool.wait_ge(mv2_ready, i + 1)
                rsqrt(mv2, ve2, rs2, GN_EPS, rs2_ready)

            def att(i):
                pool.wait_ge(mv3_ready, i + 1)
                rsqrt(mv3, ve3, rs3, EPS, rs3_ready)

            phase2(scan_a=scan_a, stats=stats, att=att)

        @block.scalar
        def _(act):
            copy = nc.scalar.copy
            act.dma_start(CL[:, :], cols).then_inc(l_cols, 16)
            act.dma_start(HT[:, 4:10, :], text).then_inc(l_text, 16)
            act.dma_start(RW[:, :], rows.partition_broadcast(P)).then_inc(l_rows, 16)
            act.dma_start(TW[:, :], tokw).then_inc(l_tokw, 16)
            act.dma_start(pickraw, pick).then_inc(l_pick, 16)
            act.wait_ge(l_pick, 16)
            copy(PK[:, :], pickraw).then_inc(pick_ready, 1)
            act.wait_ge(l_w1, 16)
            copy(W1h[:, :], W1raw).then_inc(w_rounded, 1)
            act.wait_ge(zh_ready, 1)
            nc.scalar.activation(th0[:, :, :], nT0[:, :, :], ACT.Tanh).then_inc(zt_ready, 1)
            act.wait_ge(tr_ready, 4)
            src = PS[:, 5:8, :].rearrange("p b n -> p (b n)").rearrange("p (q j c) -> p q j c", j=J, c=C)
            for u, q in ((0, 0), (1, 2), (2, 0), (3, 4), (4, 6), (5, 8)):
                copy(XT[D:P, u, :, :, 1:C], src[D:P, q:q + 2, :, 0:C - 1])
            for u, q in ((1, 0), (2, 2), (3, 2), (4, 4), (5, 6)):
                last = copy(XT[D:P, u, :, :, 0:1], src[D:P, q:q + 2, :, C - 1:C])
            last.then_inc(xt_act, 1)

            def by_tile(n, name, src):
                for g in range(G):
                    w, rows_g = ARC[name].start + g * P, slice(g * D, (g + 1) * D)
                    last = copy(ARCH[rows_g, at(n), w:w + P], src[rows_g].unsqueeze(1))
                return last

            act.wait_ge(w_rest, 1)
            with act.Fori(0, ROUNDS) as it:
                def bank(s, i):
                    return PS[:, 4 * s + i, :]

                for s in range(2):
                    n = 2 * it + s
                    act.wait_ge(proj_ready, 2 * it + (s + 1))
                    copy(RK[s][:, :, :, :].rearrange("p g w d -> p (g w d)"), bank(s, 0)).then_inc(rk_ready, 1)
                    act.wait_ge(hid_ready, 2 * it + (s + 1))
                    nc.scalar.activation(TH[s][0:D, :], bank(s, 1)[0:D, 0:G * P], ACT.Tanh).then_inc(th_ready, 1)
                    nc.scalar.activation(SG[s][:, :], bank(s, 1)[:, G * P:2 * G * P], ACT.Tanh, scale=0.5)\
                        .then_inc(sgt_ready, 1)
                for s in range(2):
                    act.wait_ge(za_ready, 2 * it + (s + 1))
                    nc.scalar.activation(TA[s][:, :, :], ZA[s][:, :, :], ACT.Tanh, scale=0.5).then_inc(ta_ready, 1)
                for s in range(2):
                    act.wait_ge(wg_ready, 2 * it + (s + 1))
                    nc.scalar.activation(TWd[s][:, :, :], bank(s, 1)[:, 0:2 * G * D].rearrange(
                        "p (g w d) -> p g w d", g=G, w=2)[:, :, 0, :], ACT.Tanh, scale=0.5).then_inc(tw_ready, 1)
                for s in range(2):
                    n = 2 * it + s
                    act.wait_ge(cum_ready, 2 * it + (s + 1))
                    nc.scalar.activation(EX[s][:, :, :, :].rearrange("p w g d -> p (w g d)"),
                                         bank(s, 2)[:, 0:3 * P], ACT.Exp)
                    nc.scalar.activation(ARCH[:, at(n), ARC["E"]], bank(s, 2)[:, 3 * P:3 * P + J].unsqueeze(1),
                                         ACT.Exp)
                    nc.scalar.activation(NN[s][:, :, :].rearrange("p g d -> p (g d)"), bank(s, 2)[:, 0:P],
                                         ACT.Exp, scale=-1.0).then_inc(ex_ready, 1)
                for s in range(2):
                    n = 2 * it + s
                    act.wait_ge(ft_ready, 2 * it + (s + 1))
                    copy(FA[s][:, :, :].rearrange("p w t -> p (w t)"), bank(s, 0)[:, 0:2 * P])
                    for g in range(G):
                        rows_g = slice(g * D, (g + 1) * D)
                        last = copy(FZ[s][rows_g, g, :, :].rearrange("p w t -> p (w t)"),
                                    bank(s, 0)[rows_g, 2 * P:4 * P])
                    last.then_inc(ftc_ready, 1)
                    by_tile(n, "Rf", bank(s, 0)[:, P:2 * P])
                for s in range(2):
                    act.wait_ge(p1t_ready, 2 * it + (s + 1))
                    copy(PI[s][:, :, :].rearrange("p g t -> p (g t)"), bank(s, 3)[:, 0:G * P]).then_inc(p1_ready, 1)
                for s in range(2):
                    n = 2 * it + s
                    act.wait_ge(lvov_ready, 2 * it + (s + 1))
                    copy(ARCH[:, at(n), ARC["OV"].start:ARC["H"].stop], bank(s, 1)[:, P:4 * P].unsqueeze(1))
                    copy(LV[s][:, :, :].rearrange("p g d -> p (g d)"), bank(s, 1)[:, 0:P]).then_inc(lv_ready, 1)
                for s in range(2):
                    n = 2 * it + s
                    act.wait_ge(uw_ready, 2 * it + (s + 1))
                    copy(ARCH[:, at(n), ARC["U"]], bank(s, 2)[:, 0:P].unsqueeze(1))
                    by_tile(n, "Wf", bank(s, 2)[:, P:2 * P]).then_inc(arch_act, 1)

            def heads(i):
                act.wait_ge(ogt_ready, i + 1)
                copy(OGT[:, :, :].rearrange("p c t -> p (c t)"), PS[:, OUT_BANK[i], 0:T * P]).then_inc(ogtc_ready, 1)

            def split(i):
                act.wait_ge(xn_ready, i + 1)
                copy(XD[:, :, 0, :], XN[:, :, :]).then_inc(xr_ready, 1)

            def feat(i, h):
                act.wait_ge(x2t_ready, 2 * i + h + 1)
                copy(XHL[i][:, h * HALF:(h + 1) * HALF, :].rearrange("p q t -> p (q t)"), PS[:, FFN_BANK[i], 0:HALF * P])\
                    .then_inc(xhl_ready, 1)

            def rank(i):
                act.wait_ge(ls_ready, i + 1)
                nc.scalar.activation(PX[:, :, :], LS[:, :, :], ACT.Exp).then_inc(pex_ready, 1)

            def parts(i):
                act.wait_ge(cf_ready, i + 1)
                copy(CP[:, :, 0, :].bitcast(F32R), CF[:, i * Q:(i + 1) * Q, :]).then_inc(cr_ready, 1)

            def weights(i, h):
                act.wait_ge(ct_ready, 2 * i + h + 1)
                copy(CT[i % 2][:, h * HALF * P:(h + 1) * HALF * P], PS[0:2 * E, FFN_BANK[i], 0:HALF * P])\
                    .then_inc(ctc_ready, 1)

            def experts(u, v):
                for e in (2 * v, 2 * v + 1):
                    x = E * u + e
                    act.wait_ge(z_ready, x + 1)
                    if x >= 2:
                        act.wait_ge(hc_done, x - 1)
                    nc.scalar.activation(RL[x % 2][:, :], PS[:, 3 + x % 2, 0:HALF * P], ACT.Relu,
                                         bias=CL[:, COLS["b1e"]][:, e:e + 1]).then_inc(relu_done, 1)

            def total(u):
                act.wait_ge(y_sum, u + 1)
                if u:
                    act.wait_ge(fin_ready, u)
                copy(YS[:, :], PS[:, 7, 0:HALF * P]).then_inc(ys_ready, 1)

            phase2(heads=heads, split=split, feat=feat, rank=rank, parts=parts, weights=weights, experts=experts,
                   total=total)

        @block.vector
        def _(dve):
            V = nc.vector
            TT, TS, STT = V.tensor_tensor, V.tensor_scalar, V.scalar_tensor_tensor
            c0 = Chain(dve, dve0)

            def variances(src, tiles):
                for q in tiles:
                    last = V.bn_stats(st0[:, q, :], src(q))
                c0.link(last)
                for q in tiles:
                    last = V.bn_aggr(mv0[:, q, :], st0[:, q, :])
                last.then_inc(var_ready, 1)

            def normalised(dst, src, tiles, count):
                dve.wait_ge(var_ready, count)
                dve.wait_ge(rs_ready, count)
                for q in tiles:
                    last = TS(dst(q), src(q), mv0[:, q, 0:1], rs0[:, q, 0:1], ALU.subtract, ALU.mult)
                return last

            four = range(4)
            dve.wait_ge(l_patch, 16)
            variances(lambda q: PT[:, q, :], four)
            normalised(lambda q: xh0[:, q, :], lambda q: PT[:, q, :], four, 1).then_inc(xh_ready, 1)
            dve.wait_ge(l_text, 16)
            variances(lambda q: HT[:, q, :], range(4, 10))

            def col(name):
                return CL[:, COLS[name]]

            dve.wait_ge(l_cols, 16)
            dve.wait_ge(l_rows, 16)
            TS(mix[0:D, :], col("mix")[0:D, :], -1.0, 1.0, ALU.mult, ALU.add)
            V.tensor_copy(mix[D:P, :], col("mix")[D:P, :])
            TS(kaH[:, :], RW[:, ROWS["k_a"]], 0.5, None, ALU.mult)
            TT(gbias[:, :], RW[:, ROWS["bg"]], RW[:, ROWS["bias"]], ALU.add)
            c0.link(TS(lnpH[:, :], CL[:, COLS["lnp_g"].start:COLS["lnp_b"].stop], 0.5, None, ALU.mult))
            dve.wait_ge(tr_ready, 1)
            for h in range(2):
                last = TS(xT0[0:PH, h, :], PS[0:PH, h, :], col("ln1_g")[0:PH, h:h + 1], col("ln1_b")[0:PH, h:h + 1],
                          ALU.mult, ALU.add)
            last.then_inc(nt_ready, 1)
            dve.wait_ge(l_attw, 16)
            for i, m in ((0, 0), (1, 2), (2, 3)):
                TS(Wproj[:, i * D:(i + 1) * D], AW[:, ATTW["rkv"]][:, i * D:(i + 1) * D], mix[:, m:m + 1], None,
                   ALU.mult)
            TS(Wlora[:, 0:D], AW[:, ATTW["A_w"]], mix[:, 1:2], None, ALU.mult)
            TS(Wlora[:, D:D + P], AW[:, ATTW["A_g"]], mix[:, 5:6], None, ALU.mult)
            dve.wait_ge(aab_ready, 1)
            TS(Wproj[:, 3 * D:4 * D], PS[:, 7, 0:D], mix[:, 4:5], None, ALU.mult).then_inc(mix_ready, 1)

            normalised(lambda q: XHD[:, q, 0, :], lambda q: HT[:, q, :], range(4, 10), 2)
            normalised(lambda q: XHD[:, q, 1, :], lambda q: HT[:, q, :], range(4, 10), 2)
            dve.wait_ge(mm_ready, 1)
            c0.link(TT(t0[:, :, :], PS[:, 2, 0:4 * D].rearrange("p (q d) -> p q d", q=4), row("b1", 4), ALU.add))
            variances(lambda q: t0[:, q, :], four)
            normalised(lambda q: n0[:, q, :], lambda q: t0[:, q, :], four, 3).then_inc(xh_ready, 1)
            dve.wait_ge(tr_ready, 2)
            TS(nT0[:, :, :], PS[:, 0, 0:2 * P].rearrange("p (c t) -> p c t", c=2), col("ln2_g"), col("ln2_b"),
               ALU.mult, ALU.add).then_inc(nt_ready, 1)

            def by_group(ap):
                return ap.rearrange("p (c g) d -> p g c d", g=G)

            def two_banks(b):
                return PS[:, b:b + 2, 0:2 * D].rearrange("p g (c d) -> p g c d", c=2)

            def row4(name):
                return RW[:, ROWS[name]].unsqueeze(1).unsqueeze(1).to_broadcast([P, G, 2, D])

            dve.wait_ge(mm_ready, 2)
            for g in range(G):
                last = TT(by_group(t0[:, :, :])[:, g], two_banks(2)[:, g], row4("bp1")[:, g], ALU.add)
            c0.link(last)
            variances(lambda q: t0[:, q, :], four)
            normalised(lambda q: n0[:, q, :], lambda q: t0[:, q, :], four, 4).then_inc(xh_ready, 1)
            dve.wait_ge(tr_ready, 3)
            TS(nT0[:, :, :], PS[:, 1, 0:2 * P].rearrange("p (c t) -> p c t", c=2), lnpH[:, 0:1], lnpH[:, 1:2],
               ALU.mult, ALU.add).then_inc(zh_ready, 1)
            dve.wait_ge(zh_ready, 1)
            dve.wait_ge(zt_ready, 1)
            STT(nT0[:, :, :], th0[:, :, :], 1.0, nT0[:, :, :], ALU.add, ALU.mult).then_inc(nt_ready, 1)
            dve.wait_ge(mm_ready, 3)
            for g in range(G):
                last = TT(by_group(HT[:, 0:4, :])[:, g], two_banks(3)[:, g], row4("bp2")[:, g], ALU.add)
            c0.link(last)
            variances(lambda q: HT[:, q, :], four)
            normalised(lambda q: XHD[:, q, 0, :], lambda q: HT[:, q, :], four, 5)
            normalised(lambda q: XHD[:, q, 1, :], lambda q: HT[:, q, :], four, 5).then_inc(xh_ready, 1)
            dve.wait_ge(tr_ready, 4)
            src = PS[:, 5:8, :].rearrange("p b n -> p (b n)").rearrange("p (q j c) -> p q j c", j=J, c=C)
            for u, q in ((0, 0), (1, 2), (2, 0), (3, 4), (4, 6), (5, 8)):
                last = V.tensor_copy(XT[0:D, u, :, :, :], src[0:D, q:q + 2, :, :])
            last.then_inc(xt_dve, 1)

            dve.wait_ge(l_const, 16)
            dve.wait_ge(l_ident, 16)
            c1 = Chain(dve, dve1, 20)
            with dve.Fori(0, ROUNDS) as it:
                def bank(s, i):
                    return PS[:, 4 * s + i, :]

                def flat(t):
                    return t.rearrange("p g d -> p (g d)")

                kk, k2, kn, b2, bon = [0, 0], [0, 0], [0, 0], [0, 0], [0, 0]
                for s in range(2):
                    dve.wait_ge(rk_ready, 2 * it + (s + 1))
                    TT(ZA[s][:, :, :], RK[s][:, :, 3, :], row("b_a"), ALU.add).then_inc(za_ready, 1)
                    kk[s] = c1.mark(TT(KK[s][:, :, :], RK[s][:, :, 1, :], row("k_k"), ALU.mult))
                    TT(RR[s][:, :, :], RK[s][:, :, 0, :], row("r_k"), ALU.mult)
                    c1.wait(kk[s], it)
                    c1.link(TT(SQ[s][:, :, :], KK[s][:, :, :], KK[s][:, :, :], ALU.mult), it)
                    V.tensor_reduce(SS[s][:, :, :], SQ[s][:, :, :], AX.X, ALU.add).then_inc(ss_ready, 1)
                for s in range(2):
                    dve.wait_ge(tw_ready, 2 * it + (s + 1))
                    TS(LW[s][:, :, :], TWd[s][:, :, :], DECAY / 2, DECAY / 2, ALU.mult, ALU.add).then_inc(w_ready, 1)
                for s in range(2):
                    dve.wait_ge(ta_ready, 2 * it + (s + 1))
                    c1.link(STT(T1[s][:, :, :], TA[s][:, :, :], -1.0,
                                kaH[:, :].unsqueeze(1).to_broadcast([P, G, D]), ALU.add, ALU.mult), it)
                    k2[s] = c1.mark(STT(K2[s][:, :, :], T1[s][:, :, :], 1.0, RK[s][:, :, 1, :], ALU.add, ALU.mult))
                    dve.wait_ge(rn_ready, 2 * it + (s + 1))
                    kn[s] = c1.mark(TT(KN[s][:, :, :], KK[s][:, :, :], RN[s][:, :, :].to_broadcast([P, G, D]),
                                       ALU.mult))
                    c1.wait(k2[s], it)
                    mm = c1.mark(TT(MM[s][:, :, :], RR[s][:, :, :], K2[s][:, :, :], ALU.mult))
                    c1.wait(kn[s], it)
                    b2[s] = c1.mark(STT(B2[s][:, :, :], TA[s][:, :, :], 1.0, KN[s][:, :, :], ALU.add, ALU.mult))
                    c1.wait(mm, it)
                    bon[s] = c1.mark(V.tensor_reduce(BON[s][:, :, :], MM[s][:, :, :], AX.X, ALU.add))
                for s in range(2):
                    n = 2 * it + s
                    dve.wait_ge(ex_ready, 2 * it + (s + 1))
                    c1.wait(b2[s], it)
                    EXs = EX[s]
                    STT(HAT[s][:, 0, :, :], KN[s][:, :, :], -1.0, EXs[:, 1, :, :], ALU.mult, ALU.mult)
                    TT(HAT[s][:, 1, :, :], RK[s][:, :, 0, :], EXs[:, 0, :, :], ALU.mult)
                    STT(HAT[s][:, 2, :, :], B2[s][:, :, :], 0.5, NN[s][:, :, :], ALU.mult, ALU.mult)
                    TT(HAT[s][:, 3, :, :], K2[s][:, :, :], NN[s][:, :, :], ALU.mult).then_inc(hat_ready, 1)
                    TT(KP[s][:, :, :], K2[s][:, :, :], EXs[:, 2, :, :], ALU.mult).then_inc(kp_ready, 1)
                    STT(BP[s][:, :, :], B2[s][:, :, :], 0.5, EXs[:, 2, :, :], ALU.mult, ALU.mult)\
                        .then_inc(bp_ready, 1)
                for s in range(2):
                    n = 2 * it + s
                    dve.wait_ge(wg_ready, 2 * it + (s + 1))
                    gate = bank(s, 1)[:, 0:2 * G * D].rearrange("p (g w d) -> p g w d", g=G, w=2)[:, :, 1, :]
                    c1.wait(bon[s], it)
                    for g in range(G):
                        last = STT(VBN[s][:, g, :], RK[s][:, g, 2, :], BON[s][:, g, :], RW[:, ROWS["gn_b"]],
                                   ALU.mult, ALU.add)
                    vbn = c1.mark(last)
                    TT(ARCH[:, at(n), ARC["GW"]].rearrange("p u (g d) -> p (u g) d", g=G), gate, row("gn_w"), ALU.mult)
                    c1.wait(vbn, it)
                    TT(ARCH[:, at(n), ARC["GB"]].rearrange("p u (g d) -> p (u g) d", g=G), gate, VBN[s][:, :, :],
                       ALU.mult)
                for s in range(2):
                    n = 2 * it + s
                    masks = const("masks")
                    for g in range(G):
                        dve.wait_ge(l_ready, 4 * it + (2 * s + g + 1))
                        L = bank(s, 2 + g)
                        last = TT(AT[s][:, g, :], L[:, 0:P], masks[:, 0:P], ALU.mult)
                        TT(LKT[s][:, g, :, :].rearrange("p w t -> p (w t)"), L[:, 2 * P:4 * P], masks, ALU.mult)
                        lrb = ARC["LrbT"].start + g * P
                        arch = TT(ARCH[:, at(n), lrb:lrb + P], L[:, P:2 * P].unsqueeze(1),
                                  masks[:, P:2 * P].unsqueeze(1), ALU.mult)
                    arch.then_inc(arch_dve, 1)
                    dve.wait_ge(arch_dve, 2 * it + (s + 1))
                    c1.link(TT(QA[s][:, :, :], AT[s][:, :, :], twice(const("m1")), ALU.mult), it)
                    TT(QT[s][:, :, :], QA[s][:, :, :], twice(ident), ALU.add).then_inc(q_ready, 1)
                for li, size in enumerate(LEVELS):
                    for s in range(2):
                        dve.wait_ge(y_ready, level(it, li, s, 4))
                        TT(YI[s][:, :, :], pairs(bank(s, 2)[:, 0:G * P]), twice(const(f"m{size}")), ALU.mult)\
                            .then_inc(ysb_ready, 1)
                    for s in range(2):
                        if li < 3:
                            dve.wait_ge(pp_ready, level(it, li, s, 3))
                            TT(flat(PI[s][:, :, :]), flat(PI[s][:, :, :]), bank(s, 3)[:, 0:G * P], ALU.add)\
                                .then_inc(pu_ready, 1)
                        dve.wait_ge(qq_ready, level(it, li, s, 4))
                        TT(flat(QT[s][:, :, :]), flat(QT[s][:, :, :]), bank(s, 0)[:, 0:G * P], ALU.add)\
                            .then_inc(q_ready, 1)
            assert c1.n == c1.per, c1.n

            m = Chain(dve, dve2)
            dve.wait_ge(arch_act, NU)

            def scan_a(k):
                dve.wait_ge(sap_ready, k + 1)
                TT(SA[:, :, :], pairs(PS[:, k % 2, 0:P]), pairs(ARCH[:, SLOT[k], ARC["U"]]), ALU.add)\
                    .then_inc(sa_ready, 1)

            def scan_b(k):
                dve.wait_ge(eh_ready, k + 1)
                dve.wait_ge(sps_ready, k + 1)
                TT(ST[1 - k % 2][:, :], EHs[:, :], PS[:, 1 - k % 2, 0:J * D], ALU.add).then_inc(s_ready, 1)
                dve.wait_ge(ops_ready, k + 1)
                TT(OO[:, G * k:G * (k + 1), :], pairs(PS[:, k % 2, P:2 * P]), pairs(ARCH[:, SLOT[k], ARC["OV"]]),
                   ALU.add).then_inc(oo_ready, 1)

            def variances_of(src, st, mv, done):
                for q in range(Q):
                    last = V.bn_stats(st[:, q, :], src(q))
                m.link(last)
                for q in range(Q):
                    last = V.bn_aggr(mv[:, q, :], st[:, q, :])
                last.then_inc(done, 1)

            def arch(i, q, name):
                return pairs(ARCH[:, SLOT[i * T + q // G], ARC[name]])[:, q % G, :]

            def stats(i):
                dve.wait_ge(oo_ready, (i + 1) * T)
                variances_of(lambda q: OO[:, i * Q + q, :], st2, mv2, mv2_ready)

            def centre(i):
                dve.wait_ge(mv2_ready, i + 1)
                for q in range(Q):
                    last = STT(X1[:, q, :], OO[:, i * Q + q, :], mv2[:, q, 0:1], arch(i, q, "GW"),
                               ALU.subtract, ALU.mult)
                last.then_inc(x1_ready, 1)

            def heads(i):
                dve.wait_ge(x1_ready, i + 1)
                dve.wait_ge(rs2_ready, i + 1)
                for q in range(Q):
                    last = STT(OG[:, q, :], X1[:, q, :], rs2[:, q, :], arch(i, q, "GB"), ALU.mult, ALU.add)
                last.then_inc(og_ready, 1)

            def att(i):
                dve.wait_ge(att_ready, i + 1)
                for c in range(T):
                    h = HQ[i * T + c]
                    last = TT(H1[:, i * Q + G * c:i * Q + G * (c + 1), :], HT[:, h:h + G, :],
                              pairs(PS[:, OUT_BANK[i], c * P:(c + 1) * P]), ALU.add)
                m.link(last)
                variances_of(lambda q: H1[:, i * Q + q, :], st3, mv3, mv3_ready)

            def split(i):
                dve.wait_ge(mv3_ready, i + 1)
                dve.wait_ge(rs3_ready, i + 1)
                for q in range(Q):
                    last = TS(XN[:, q, :], H1[:, i * Q + q, :], mv3[:, q, 0:1], rs3[:, q, :],
                              ALU.subtract, ALU.mult)
                last.then_inc(xn_ready, 1)

            def rest(i):
                dve.wait_ge(xn_ready, i + 1)
                dve.wait_ge(xr_ready, i + 1)
                TT(XD[:, :, 1, :], XN[:, :, :], XD[:, :, 0, :].bitcast(F32), ALU.subtract).then_inc(xd_ready, 1)

            def per_tile(ap):
                return ap.to_broadcast([P, Q, E])

            def rank(i):
                dve.wait_ge(lg_ready, i + 1)
                m.link(TT(LG[:, :, :], PS[:, FFN_BANK[i], 0:Q * E].rearrange("p (q e) -> p q e", q=Q),
                          per_tile(gbias[:, :].unsqueeze(1)), ALU.add))
                largest = m.mark(V.tensor_reduce(M1[:, :, :], LG[:, :, :], AX.X, ALU.max))
                differences = m.mark(TT(DD[:, :, :, :], LG[:, :, :].unsqueeze(2).to_broadcast([P, Q, E, E]),
                                        LG[:, :, :].unsqueeze(3).to_broadcast([P, Q, E, E]), ALU.subtract))
                m.wait(largest)
                TT(LS[:, :, :], LG[:, :, :], per_tile(M1[:, :, :]), ALU.subtract).then_inc(ls_ready, 1)
                m.wait(differences)

                def square(t):
                    return t[:, :, :, :].rearrange("p q e f -> p q (e f)")
                m.link(STT(square(D1), square(DD), 0.0, const("tri").unsqueeze(1).to_broadcast([P, Q, E * E]),
                           ALU.is_equal, ALU.mult))
                m.link(STT(square(D2), square(DD), 0.0, square(D1), ALU.is_gt, ALU.add))
                V.tensor_reduce(RKs[:, :, :].unsqueeze(3), D2[:, :, :, :], AX.X, ALU.add).then_inc(rank_ready, 1)

            def choose(i):
                dve.wait_ge(rank_ready, i + 1)
                dve.wait_ge(pex_ready, i + 1)
                m.link(STT(PM[:, :, :], RKs[:, :, :], 2.0, PX[:, :, :], ALU.is_lt, ALU.mult))
                m.link(V.tensor_reduce(SM[:, :, :], PM[:, :, :], AX.X, ALU.add))
                m.link(V.reciprocal(RC[:, :, :], SM[:, :, :]))
                TT(CF[:, i * Q:(i + 1) * Q, :], PM[:, :, :], per_tile(RC[:, :, :]), ALU.mult).then_inc(cf_ready, 1)

            def parts(i):
                dve.wait_ge(cf_ready, i + 1)
                dve.wait_ge(cr_ready, i + 1)
                TT(CP[:, :, 1, :].bitcast(F32R), CF[:, i * Q:(i + 1) * Q, :], CP[:, :, 0, :], ALU.subtract)\
                    .then_inc(cp_ready, 1)

            def experts(u, v):
                for e in (2 * v, 2 * v + 1):
                    x = E * u + e
                    dve.wait_ge(relu_done, x + 1)
                    dve.wait_ge(c_ready, x + 1)
                    if x >= 4:
                        dve.wait_ge(y_done, x - 3)
                    TT(HC[x % 4][:, :], RL[x % 2][:, :], PS[:, 5 + x % 2, 0:HALF * P], ALU.mult)\
                        .then_inc(hc_done, 1)

            def fold(u):
                dve.wait_ge(fin_ready, u + 1)
                h = H1[:, u * HALF:(u + 1) * HALF, :]
                TT(h, h, PS[:, 2, 0:HALF * D].rearrange("p (q d) -> p q d", q=HALF), ALU.add).then_inc(fin_done, 1)

            phase2(scan_a=scan_a, scan_b=scan_b, stats=stats, centre=centre, heads=heads, att=att, split=split,
                   rest=rest, rank=rank, choose=choose, parts=parts, experts=experts, fold=fold)

        @block.tensor
        def _(pe):
            mm = nc.tensor.matmul

            def transpose(dst, src):
                return nc.tensor.transpose(dst, src, ident)

            pe.wait_ge(l_ident, 16)
            pe.wait_ge(xh_ready, 1)
            for h in range(2):
                for q in range(4):
                    last = transpose(PS[0:PH, h, q * P:(q + 1) * P], xh0[:, q, h * PH:(h + 1) * PH])
            last.then_inc(tr_ready, 1)
            pe.wait_ge(l_attw, 16)
            mm(PS[:, 7, 0:D], AW[0:D, ATTW["A_aT"]], AW[0:D, ATTW["B_a"]], start=True, stop=True)\
                .then_inc(aab_ready, 1)
            pe.wait_ge(l_tokw, 16)
            pe.wait_ge(nt_ready, 1)
            for q in range(4):
                for h in range(2):
                    last = mm(PS[:, 2, q * D:(q + 1) * D], xT0[0:PH, h, q * P:(q + 1) * P],
                              TW[0:PH, TOKW["W1"]][:, h * D:(h + 1) * D], start=h == 0, stop=h == 1)
            last.then_inc(mm_ready, 1)
            for i, w in ((1, "Wp1"), (2, "Wp2")):
                pe.wait_ge(xh_ready, i + 1)
                for c in range(2):
                    last = transpose(PS[:, i - 1, c * P:(c + 1) * P],
                                     n0[:, 2 * c:2 * c + 2, :].rearrange("p g d -> p (g d)"))
                last.then_inc(tr_ready, 1)
                pe.wait_ge(nt_ready, i + 1)
                for g in range(G):
                    rows_g = slice(g * D, (g + 1) * D)
                    for c in range(2):
                        last = mm(PS[:, 1 + i + g, c * D:(c + 1) * D], nT0[rows_g, c, :], TW[rows_g, TOKW[w]],
                                  start=True, stop=True)
                last.then_inc(mm_ready, 1)
            pe.wait_ge(xh_ready, 4)
            pe.wait_ge(mix_ready, 1)
            for q in range(10):
                last = transpose(PS[:, 5 + q // 4, (q % 4) * P:(q % 4 + 1) * P],
                                 XHD[:, q, :, :].rearrange("p w d -> p (w d)"))
            last.then_inc(tr_ready, 1)

            pe.wait_ge(memsets, 1)
            pe.wait_ge(l_const, 16)
            masks = const("masks")
            with pe.Fori(0, ROUNDS) as it:
                def bank(s, i):
                    return PS[:, 4 * s + i, :]

                def tile(t, g):
                    return t[:, g * P:(g + 1) * P]

                for s in range(2):
                    pe.wait_ge(x_staged, 2 * it + (s + 1))
                    for g in range(G):
                        last = mm(bank(s, 0)[:, g * 4 * D:(g + 1) * 4 * D], tile(XS[s], g), Wproj[:, :],
                                  start=True, stop=True)
                    last.then_inc(proj_ready, 1)
                    mm(bank(s, 1)[0:D, 0:G * P], Wlora[:, 0:D], XS[s][:, :], start=True, stop=True)
                    mm(bank(s, 1)[:, G * P:2 * G * P], Wlora[:, D:D + P], XS[s][:, :], start=True, stop=True)\
                        .then_inc(hid_ready, 1)
                for s in range(2):
                    pe.wait_ge(th_ready, 2 * it + (s + 1))
                    pe.wait_ge(sg_ready, 2 * it + (s + 1))
                    for g in range(G):
                        o = bank(s, 1)[:, g * 2 * D:(g + 1) * 2 * D]
                        mm(o[:, 0:D], tile(TH[s], g), AW[:, ATTW["B_w"]], start=True, stop=True)
                        last = mm(o[:, D:2 * D], tile(SG[s], g), AW[:, ATTW["B_g"]], start=True, stop=True)
                    last.then_inc(wg_ready, 1)
                for s in range(2):
                    pe.wait_ge(w_ready, 2 * it + (s + 1))
                    lw = LW[s][:, :, :].rearrange("p g d -> p (g d)")
                    for i, m in enumerate((masks[:, P:2 * P], masks[:, 0:P], const("suffix"))):
                        mm(bank(s, 2)[:, i * P:(i + 1) * P], m, lw, start=True, stop=True)
                    for g in range(G):
                        last = mm(bank(s, 2)[g * D:(g + 1) * D, 3 * P:3 * P + J], LW[s][:, g, :], const("seq"),
                                  start=True, stop=True)
                    last.then_inc(cum_ready, 1)
                for s in range(2):
                    pe.wait_ge(hat_ready, 2 * it + (s + 1))
                    for w in range(4):
                        last = transpose(bank(s, 0)[:, w * P:(w + 1) * P],
                                         HAT[s][:, w, :, :].rearrange("p g d -> p (g d)"))
                    last.then_inc(ft_ready, 1)
                for s in range(2):
                    pe.wait_ge(ftc_ready, 2 * it + (s + 1))
                    for g in range(G):
                        ar = FA[s][:, :, :].rearrange("p w t -> p (w t)")
                        mm(bank(s, 2 + g)[:, 0:2 * P], FZ[s][:, g, 0, :], ar, start=True, stop=True)
                        mm(bank(s, 2 + g)[:, 2 * P:4 * P], FZ[s][:, g, 1, :], ar, start=True, stop=True)\
                            .then_inc(l_ready, 1)
                for s in range(2):
                    pe.wait_ge(q_ready, level(it, 0, s, 5))
                    for g in range(G):
                        last = transpose(bank(s, 3)[:, g * P:(g + 1) * P], QT[s][:, g, :])
                    last.then_inc(p1t_ready, 1)
                for s in range(2):
                    pe.wait_ge(vb_ready, 2 * it + (s + 1))
                    pe.wait_ge(kp_ready, 2 * it + (s + 1))
                    for g in range(G):
                        mm(bank(s, 1)[:, g * D:(g + 1) * D], LKT[s][:, g, 0, :], RK[s][:, g, 2, :],
                           start=True, stop=True)
                        mm(bank(s, 1)[:, P + g * D:P + (g + 1) * D], LKT[s][:, g, 1, :], RK[s][:, g, 2, :],
                           start=True, stop=True)
                        last = mm(bank(s, 1)[g * D:(g + 1) * D, 2 * P:4 * P], KP[s][:, g, :],
                                  VB[s][:, g, :, :].rearrange("p j d -> p (j d)"), start=True, stop=True)
                    last.then_inc(lvov_ready, 1)
                for li in range(4):
                    for s in range(2):
                        if li == 0:
                            pe.wait_ge(p1_ready, 2 * it + (s + 1))
                        else:
                            pe.wait_ge(pu_ready, level(it, li - 1, s, 3))
                        for g in range(G):
                            last = mm(bank(s, 2)[:, g * P:(g + 1) * P], AT[s][:, g, :], PI[s][:, g, :],
                                      start=True, stop=True)
                        last.then_inc(y_ready, 1)
                    for s in range(2):
                        pe.wait_ge(q_ready, level(it, li, s, 5))
                        pe.wait_ge(ysb_ready, level(it, li, s, 4))
                        if li < 3:
                            for g in range(G):
                                last = mm(bank(s, 3)[:, g * P:(g + 1) * P], QT[s][:, g, :], YI[s][:, g, :],
                                          start=True, stop=True)
                            last.then_inc(pp_ready, 1)
                        for g in range(G):
                            last = mm(bank(s, 0)[:, g * P:(g + 1) * P], YI[s][:, g, :], QT[s][:, g, :],
                                      start=True, stop=True)
                        last.then_inc(qq_ready, 1)
                for s in range(2):
                    pe.wait_ge(lv_ready, 2 * it + (s + 1))
                    pe.wait_ge(q_ready, level(it, 4, s, 5))
                    for g in range(G):
                        mm(bank(s, 2)[:, g * D:(g + 1) * D], QT[s][:, g, :], LV[s][:, g, :], start=True, stop=True)
                        last = mm(bank(s, 2)[g * D:(g + 1) * D, P:2 * P], HAT[s][:, 0, g, :], QT[s][:, g, :],
                                  start=True, stop=True)
                    last.then_inc(uw_ready, 1)

            pe.wait_ge(arch_act, NU)
            pe.wait_ge(arch_dve, NU)
            pe.wait_ge(arch_pool, NU)

            def scan_a(k):
                if k:
                    pe.wait_ge(s_ready, k)
                if k >= 2:
                    pe.wait_ge(oo_ready, k - 1)
                wf = ARCH[:, SLOT[k], ARC["Wf"]]
                for g in range(G):
                    for j in range(J):
                        last = mm(PS[j * C:(j + 1) * C, k % 2, g * D:(g + 1) * D],
                                  wf[:, g * P + j * C:g * P + (j + 1) * C], ST[k % 2][:, j * D:(j + 1) * D],
                                  start=True, stop=True)
                last.then_inc(sap_ready, 1)

            def scan_b(k):
                u = SLOT[k]
                pe.wait_ge(sa_ready, k + 1)
                if k:
                    pe.wait_ge(oo_ready, k)
                for j in range(J):
                    for g in range(G):
                        bp = ARC["Bp"].start + (g * J + j) * D
                        last = mm(PS[g * D:(g + 1) * D, 1 - k % 2, j * D:(j + 1) * D], ARCH[:, u, bp:bp + D],
                                  SA[:, g, :], start=True, stop=True)
                last.then_inc(sps_ready, 1)
                for g in range(G):
                    o = slice(P + g * D, P + (g + 1) * D)
                    for j in range(J):
                        mm(PS[j * C:(j + 1) * C, k % 2, o],
                           ARCH[:, u, ARC["Rf"]][:, g * P + j * C:g * P + (j + 1) * C],
                           ST[k % 2][:, j * D:(j + 1) * D], start=True, stop=False)
                    last = mm(PS[:, k % 2, o], ARCH[:, u, ARC["LrbT"]][:, g * P:(g + 1) * P], SA[:, g, :],
                              start=False, stop=True)
                last.then_inc(ops_ready, 1)

            def heads(i):
                pe.wait_ge(og_ready, i + 1)
                for c in range(T):
                    last = transpose(PS[:, OUT_BANK[i], c * P:(c + 1) * P],
                                     OG[:, G * c:G * (c + 1), :].rearrange("p g d -> p (g d)"))
                last.then_inc(ogt_ready, 1)

            def att(i):
                pe.wait_ge(ogtc_ready, i + 1)
                for c in range(T):
                    last = mm(PS[:, OUT_BANK[i], c * P:(c + 1) * P], OGT[:, c, :], AW[:, ATTW["W_o"]], start=True, stop=True)
                last.then_inc(att_ready, 1)

            def feat(i, h):
                if h:
                    pe.wait_ge(xhl_ready, 2 * i + h)
                else:
                    pe.wait_ge(xr_ready, i + 1)
                    pe.wait_ge(xd_ready, i + 1)
                for t in range(HALF):
                    last = transpose(PS[:, FFN_BANK[i], t * P:(t + 1) * P],
                                     XD[:, h * HALF + t, :, :].rearrange("p w d -> p (w d)").bitcast(F32))
                last.then_inc(x2t_ready, 1)

            def rank(i):
                pe.wait_ge(xhl_ready, 2 * i + 2)
                for q in range(Q):
                    last = mm(PS[:, FFN_BANK[i], q * E:(q + 1) * E], XHL[i][:, q, :].bitcast(F32), AW[:, ATTW["Wg"]],
                              start=True, stop=True)
                last.then_inc(lg_ready, 1)

            def weights(i, h):
                if h:
                    pe.wait_ge(ctc_ready, 2 * i + h)
                else:
                    pe.wait_ge(cp_ready, i + 1)
                for t in range(HALF):
                    last = transpose(PS[0:2 * E, FFN_BANK[i], t * P:(t + 1) * P],
                                     CP[:, h * HALF + t, :, :].rearrange("p w e -> p (w e)"))
                last.then_inc(ct_ready, 1)

            def second(u, v):
                for e in (2 * v, 2 * v + 1):
                    pe.wait_ge(hc_done, E * u + e + 1)
                    mm(PS[(e % 2) * D:(e % 2 + 1) * D, 7, 0:HALF * P], W2[:, e * D:(e + 1) * D],
                       HC[e % 4][:, :], start=v == 0, stop=False).then_inc(y_done, 1)

            def experts(u, v):
                if u == 0 and v == 0:
                    pe.wait_ge(w_rounded, 1)
                    pe.wait_ge(w_rest, 1)
                    pe.wait_ge(pick_ready, 1)
                    pe.wait_ge(l_w2, 16)
                if v == 0:
                    pe.wait_ge(xhl_ready, u + 1)
                    pe.wait_ge(ctc_ready, u + 1)
                half = slice(u % 2 * HALF, (u % 2 + 1) * HALF)
                xhl = XHL[u // 2][:, half, :].rearrange("p q t -> p (q t)")
                for e in (2 * v, 2 * v + 1):
                    x = E * u + e
                    if x >= 2:
                        pe.wait_ge(relu_done, x - 1)
                    z = PS[:, 3 + x % 2, 0:HALF * P]
                    mm(z, W1h[:, e * EH:(e + 1) * EH], xhl, start=True, stop=False)
                    mm(z, W1l[:, e * EH:(e + 1) * EH], xhl, start=False, stop=True).then_inc(z_ready, 1)
                ct = CT[u // 2 % 2][:, u % 2 * HALF * P:(u % 2 + 1) * HALF * P]
                for e in (2 * v, 2 * v + 1):
                    x = E * u + e
                    if x >= 2:
                        pe.wait_ge(hc_done, x - 1)
                    mm(PS[:, 5 + x % 2, 0:HALF * P], PK[:, e * P:(e + 1) * P], ct, start=True, stop=True)\
                        .then_inc(c_ready, 1)
                if v == 1 and u:
                    pe.wait_ge(ys_ready, u)
                if u == 0 and v == 1:
                    pe.wait_ge(mv3_ready, 2)
                if v:
                    second(u, v - 1)

            def total(u):
                second(u, E // 2 - 1)
                mm(PS[:, 7, 0:HALF * P], AW[0:2 * E, ATTW["b2"]],
                   CT[u // 2 % 2][:, u % 2 * HALF * P:(u % 2 + 1) * HALF * P].bitcast(F32), start=False, stop=True)\
                    .then_inc(y_sum, 1)

            def fold(u):
                pe.wait_ge(ys_ready, u + 1)
                if u:
                    pe.wait_ge(fin_done, u)
                for t in range(HALF):
                    last = mm(PS[:, 2, t * D:(t + 1) * D], YS[:, t * P:(t + 1) * P], const("fold"),
                              start=True, stop=True)
                last.then_inc(fin_ready, 1)

            phase2(scan_a=scan_a, scan_b=scan_b, heads=heads, att=att, feat=feat, rank=rank, weights=weights,
                   experts=experts, total=total, fold=fold)


def kernel(**inputs):
    import numpy as _np
    import concourse.bacc as _bacc
    from concourse import mybir as _mybir
    from concourse.bass_utils import run_bass_kernel_spmd as _run

    w = {name.replace("L0_", ""): _np.asarray(a) for name, a in inputs.items()}

    def packed(height, layout, width, **parts):
        t = _np.zeros((height, width), _np.float32)
        for name, a in parts.items():
            t[:a.shape[0], layout[name]] = a
        return t

    def twice(a):
        return _np.concatenate([a, a], 0)

    side = IMG // 8
    patches = w["x"].reshape(BATCH, 3, side, 8, side, 8).transpose(0, 2, 4, 3, 5, 1).reshape(BATCH, IMG, PATCH)
    patches = patches.reshape(G, J, NIMG, C, PATCH).transpose(1, 3, 2, 0, 4).reshape(P, NIMG * G, PATCH)
    text = _np.zeros((BATCH, NTXT * C, D), _np.float32)
    text[:, :TXT] = w["txt"]
    text = text.reshape(G, J, NTXT, C, D).transpose(1, 3, 2, 0, 4).reshape(P, NTXT * G, D)

    rows = packed(1, ROWS, NROWS, b1=w["tok_b1"][None], bp1=w["tok_bp1"][None], bp2=w["tok_bp2"][None],
                  k_k=w["attn_k_k"][None], k_a=w["attn_k_a"][None], r_k=w["attn_r_k"][None],
                  gn_w=w["attn_gn_w"][None], gn_b=w["attn_gn_b"][None], b_a=w["attn_b_a"][None],
                  bg=w["ffn_bg"][None], bias=w["ffn_bias"][None])
    cols = packed(P, COLS, NCOLS, ln1_g=w["tok_ln1_g"].reshape(2, PH).T, ln1_b=w["tok_ln1_b"].reshape(2, PH).T,
                  ln2_g=twice(w["tok_ln2_g"][:, None]), ln2_b=twice(w["tok_ln2_b"][:, None]),
                  lnp_g=twice(w["tok_lnp_g"][:, None]), lnp_b=twice(w["tok_lnp_b"][:, None]),
                  mix=twice(w["attn_x_mix"].T), b1e=w["ffn_b1"].T)
    tokw = packed(P, TOKW, NTOKW, W1=w["tok_W1"].reshape(2, PH, D).transpose(1, 0, 2).reshape(PH, 2 * D),
                  Wp1=twice(w["tok_Wp1"]), Wp2=twice(w["tok_Wp2"]))
    W_o = _np.zeros((2, D, 2, D), _np.float32)
    W_o[0, :, 0] = W_o[1, :, 1] = w["attn_W_o"]
    b2 = _np.zeros((2, E, P), _np.float32)
    b2[:, :, :D] = w["ffn_b2"]
    attw = packed(P, ATTW, NATTW, rkv=twice(_np.concatenate([w["attn_W_r"], w["attn_W_k"], w["attn_W_v"]], 1)),
                  A_w=twice(w["attn_A_w"]), A_g=twice(w["attn_A_g"]),
                  A_aT=_np.concatenate([w["attn_A_a"].T] * 2, 1), B_a=w["attn_B_a"],
                  B_w=_np.concatenate([w["attn_B_w"], w["attn_b_w"][None]], 0), B_g=w["attn_B_g"],
                  W_o=W_o.reshape(P, P), Wg=twice(w["ffn_Wg"]), b2=b2.reshape(2 * E, P))
    w1 = twice(w["ffn_W1"].transpose(1, 0, 2).reshape(D, E * EH))
    w2 = w["ffn_W2"].transpose(1, 0, 2).reshape(EH, E * D)

    nc = _bacc.Bacc("TRN2", target_bir_lowering=False, num_devices=1)
    arrays, args = {}, []
    for name, a in (("patches", patches), ("text", text), ("consts", constants()), ("pick", picks()),
                    ("rows", rows), ("cols", cols), ("tokw", tokw), ("attw", attw), ("w1", w1), ("w2", w2)):
        a = _np.ascontiguousarray(a)
        arrays[f"in_{name}"] = a
        args.append(nc.dram_tensor(f"in_{name}", a.shape, _mybir.dt.from_np(a.dtype), kind="ExternalInput").ap())
    out = nc.dram_tensor("out_h", (P, NCH * G * D), F32, kind="ExternalOutput").ap()
    build(nc, *args, out)
    r = _run(nc, [arrays], core_ids=[0])
    got = r.results[0]["out_h"].reshape(J, C, NCH, G, D).transpose(3, 0, 2, 1, 4).reshape(BATCH, NCH * C, D)
    return got[:, :SEQ]
```

```python
from contextlib import ExitStack

import numpy as np
import concourse.bass as bass
from concourse import mybir

F32 = mybir.dt.float32
F32R = mybir.dt.float32r
ALU = mybir.AluOpType
ACT = mybir.ActivationFunctionType
AX = mybir.AxisListType

P = 128
D = 64
BATCH = 8
G = 2
J = 4
C = 32
IMG = 64
TXT = 77
SEQ = 3 * IMG + TXT
PATCH = 192
PH = PATCH // 2
NIMG = IMG // C
NTXT = -(-TXT // C)
NCH = 3 * NIMG + NTXT
NU = 1 + NIMG + NTXT
E = 8
EH = 128
T = 3
GROUPS = NCH // T
Q = T * G
HALF = Q // 2
LEVELS = (2, 4, 8, 16)
EPS = 1e-5
GN_EPS = D * 1e-5
DECAY = -0.6065306597126334


def columns(*widths):
    at, out = 0, {}
    for name, width in widths:
        out[name] = slice(at, at + width)
        at += width
    return out, at


CONST, NCONST = columns(("ident", P), ("masks", 2 * P), ("suffix", P), ("m1", P),
                        *((f"m{l}", P) for l in LEVELS), ("seq", J), ("block", J * D),
                        ("tri", E * E), ("fold", D))
ROWS, NROWS = columns(("b1", D), ("bp1", D), ("bp2", D), ("k_k", D), ("k_a", D), ("r_k", D), ("gn_w", D),
                      ("gn_b", D), ("b_a", D), ("bg", E), ("bias", E))
COLS, NCOLS = columns(("ln1_g", 2), ("ln1_b", 2), ("ln2_g", 1), ("ln2_b", 1), ("lnp_g", 1), ("lnp_b", 1),
                      ("mix", 6), ("b1e", E))
TOKW, NTOKW = columns(("W1", 2 * D), ("Wp1", P), ("Wp2", P))
ATTW, NATTW = columns(("rkv", 3 * D), ("A_w", D), ("A_g", P), ("A_aT", P), ("B_a", D), ("B_w", D), ("B_g", D),
                      ("W_o", 2 * D), ("Wg", E), ("b2", P))
ARC, NARC = columns(("U", P), ("Wf", G * P), ("OV", P), ("H", 2 * P), ("GW", P), ("GB", P), ("Bp", G * J * D),
                    ("LrbT", 2 * P), ("Rf", G * P), ("E", J))


def constants():
    i = np.arange(P)
    same = (i[:, None] // C) == (i[None, :] // C)
    su = (same & (i[:, None] < i[None, :])).astype(np.float32)
    iu = (same & (i[:, None] <= i[None, :])).astype(np.float32)
    t = np.zeros((P, NCONST), np.float32)
    t[:, CONST["ident"]] = np.eye(P)
    t[:, CONST["masks"]] = np.concatenate([su, iu], 1)
    t[:, CONST["suffix"]] = su.T
    def merged(l):
        return ((i[:, None] // (2 * l) == i[None, :] // (2 * l)) & (i[:, None] % (2 * l) >= l)
                & (i[None, :] % (2 * l) < l)).astype(np.float32)
    t[:, CONST["m1"]] = merged(1).T
    for l in LEVELS:
        t[:, CONST[f"m{l}"]] = merged(l)
    seq = (i[:, None] // C == np.arange(J)[None, :]).astype(np.float32)
    t[:, CONST["seq"]] = seq
    t[:, CONST["block"]] = np.repeat(seq, D, 1)
    e = np.arange(E)
    t[:, CONST["tri"]] = (e[None, :] < e[:, None]).reshape(1, -1)
    t[:, CONST["fold"]] = np.tile(np.eye(D), (2, 1))
    return t


def picks():
    pick = np.zeros((2, E, E, P), np.float32)
    for e in range(E):
        pick[:, e, e] = 1.0
    return pick.reshape(2 * E, E * P)


def build(nc, patches, text, consts, pick, rows, cols, tokw, attw, w1, w2, out):
    ctx = ExitStack()
    with ctx:
        def sb(name, shape, dt=F32):
            return ctx.enter_context(nc.sbuf_tensor(name, shape, dt))

        def sem(name):
            return ctx.enter_context(nc.semaphore(name))

        PT = sb("PT", [P, 4, PATCH])
        KC = sb("KC", [P, NCONST])
        RW = sb("RW", [P, NROWS])
        CL = sb("CL", [P, NCOLS])
        TW = sb("TW", [P, NTOKW])
        AW = sb("AW", [P, NATTW])
        W2 = sb("W2", [P, E * D])

        def const(name):
            return KC[:, CONST[name]]

        def twice(ap):
            return ap.unsqueeze(1).to_broadcast([P, G, P])

        def row(name, n=2):
            v = RW[:, ROWS[name]]
            return v.unsqueeze(1).to_broadcast([P, n, v.shape[1]])

        def pairs(ap):
            return ap.rearrange("p (g d) -> p g d", g=2)

        ident = const("ident")
        Wproj = sb("Wproj", [P, 4 * D])
        Wlora = sb("Wlora", [P, D + P])
        mix = sb("mix", [P, 6])
        kaH = sb("kaH", [P, D])
        gbias = sb("gbias", [P, E])
        lnpH = sb("lnpH", [P, 2])
        PK = sb("PK", [2 * E, E * P], F32R)
        W1h = sb("W1h", [P, E * EH], F32R)
        W1l = sb("W1l", [P, E * EH], F32R)

        st0 = sb("st0", [P, 10, 6])
        mv0 = sb("mv0", [P, 10, 2])
        half = sb("half", [P, Q])
        rs0 = sb("rs0", [P, 10, 1])
        xh0 = sb("xh0", [P, 4, PATCH])
        xT0 = sb("xT0", [P, 2, 4 * P])
        P0 = sb("P0", [P, 4, 4 * D])
        t0, n0 = (P0[:, i, :].rearrange("p (q d) -> p q d", q=4) for i in range(2))
        nT0, th0 = (P0[:, i, :].rearrange("p (c t) -> p c t", c=2) for i in (2, 3))
        HT = sb("HT", [P, 10, D])
        XHD = sb("XHD", [P, 10, 2, D])
        XT = sb("XT", [P, NU, G, J, C])

        def two(name, shape, dt=F32):
            return [sb(f"{name}{s}", shape, dt) for s in range(2)]

        RK = two("RK", [P, G, 4, D])
        TH = two("TH", [P, G * P])
        SG = two("SG", [P, G * P])
        ZA = two("ZA", [P, G, D])
        TA = two("TA", [P, G, D])
        TWd = two("TWd", [P, G, D])
        LW = two("LW", [P, G, D])
        KK = two("KK", [P, G, D])
        SQ = two("SQ", [P, G, D])
        SS = two("SS", [P, G, 1])
        RN = two("RN", [P, G, 1])
        KN = two("KN", [P, G, D])
        RR = two("RR", [P, G, D])
        T1 = two("T1", [P, G, D])
        K2 = two("K2", [P, G, D])
        B2 = two("B2", [P, G, D])
        MM = SQ
        BON = two("BON", [P, G, 1])
        VBN = T1
        EX = two("EX", [P, 3, G, D])
        NN = two("NN", [P, G, D])
        HA = [two(f"HA{i}_", [P, G, D]) for i in range(2)]
        HAT = two("HAT", [P, 3, G, D])
        BP = two("BP", [P, G, D])
        KP = two("KP", [P, G, D])
        FA = two("FA", [P, 2, P])
        FZ = two("FZ", [P, G, 2, P])
        AT = two("AT", [P, G, P])
        LKT = two("LKT", [P, G, 2, P])
        VB = two("VB", [P, G, J, D])
        QT = two("QT", [P, G, P])
        PI = two("PI", [P, G, P])
        YI = two("YI", [P, G, P])
        QA = YI
        LV = two("LV", [P, G, D])
        ARCH = sb("ARCH", [P, NU, NARC])
        W1raw = ARCH[:, 0, ARC["OV"].start:ARC["OV"].start + E * EH]
        pickraw = ARCH[0:2 * E, 1, ARC["OV"].start:ARC["OV"].start + E * P]

        ST = two("ST", [P, J * D])
        ES = sb("ES", [P, J * D])
        EHs = sb("EHs", [P, J * D])
        SA = sb("SA", [P, G, D])
        OO = sb("OO", [P, NCH * G, D])
        H1 = sb("H1", [P, NCH * G, D])
        XHL = [sb(f"XHL{i}", [P, Q, P], F32R) for i in range(GROUPS)]
        CF = sb("CF", [P, GROUPS * Q, E])
        st2 = sb("st2", [P, Q, 6])
        mv2 = sb("mv2", [P, Q, 2])
        rs2 = sb("rs2", [P, Q, 1])
        ve2 = sb("ve2", [P, Q, 1])
        st3, mv3, rs3, ve3 = (sb(n, [P, Q, w]) for n, w in (("st3", 6), ("mv3", 2), ("rs3", 1), ("ve3", 1)))
        OG = P0[:, :, :].rearrange("p i c -> p (i c)")[:, 0:Q * D].rearrange("p (q d) -> p q d", q=Q)
        OGT = P0[:, :, :].rearrange("p i c -> p (i c)")[:, Q * D:Q * D + T * P].rearrange("p (c t) -> p c t", c=T)
        XD = sb("XD", [P, Q, 2, D], F32R)
        LG = sb("LG", [P, Q, E])
        M1 = sb("M1", [P, Q, 1])
        LS = sb("LS", [P, Q, E])
        PX = sb("PX", [P, Q, E])
        D2 = sb("D2", [P, Q, E, E])
        RKs = sb("RKs", [P, Q, E])
        PM = sb("PM", [P, Q, E])
        SM = sb("SM", [P, Q, 1])
        RC = sb("RC", [P, Q, 1])
        CP = sb("CP", [P, Q, 2, E])
        CT = two("CT", [2 * E, Q * P], F32R)
        X1, XN = (PT[:, :, :].rearrange("p q d -> p (q d)")[:, i * Q * D:(i + 1) * Q * D].rearrange(
            "p (q d) -> p q d", q=Q) for i in range(2))
        DD, D1 = (xh0[:, :, :].rearrange("p q d -> p (q d)")[:, i * Q * E * E:(i + 1) * Q * E * E].rearrange(
            "p (q e f) -> p q e f", q=Q, e=E) for i in range(2))
        RL = [xT0[:, i, 0:HALF * P] for i in range(2)]
        HC = [sb(f"HC{i}", [P, HALF * P]) for i in range(4)]
        YS = sb("YS", [P, HALF * P])

        PS = ctx.enter_context(nc.psum_tensor("PS", [P, 8, 512], F32))

        def sems(names):
            return [sem(n) for n in names.split()]

        l_patch, l_text, l_ident, l_const, l_pick, l_rows, l_cols, l_tokw, l_attw, l_w1, l_w2 = sems(
            "l_patch l_text l_ident l_const l_pick l_rows l_cols l_tokw l_attw l_w1 l_w2")
        var_ready, rs_ready, xh_ready, tr_ready, nt_ready, mm_ready, zh_ready, zt_ready = sems(
            "var_ready rs_ready xh_ready tr_ready nt_ready mm_ready zh_ready zt_ready")
        dve0, pool0 = sems("dve0 pool0")
        memsets, xtr_ready, xt_dve, xt_act, w_rounded, w_rest, pick_ready, mix_ready, aab_ready, xhd_ready = sems(
            "memsets xtr_ready xt_dve xt_act w_rounded w_rest pick_ready mix_ready aab_ready xhd_ready")
        (proj_ready, hid_ready, rk_ready, th_ready, sgt_ready, sg_ready, za_ready, ta_ready, wg_ready,
         tw_ready, w_ready, cum_ready, ex_ready, ss_ready, rn_ready, hat_ready, kp_ready, ft_ready, ftc_ready,
         l_ready, p1t_ready, p1_ready) = sems(
             "proj_ready hid_ready rk_ready th_ready sgt_ready sg_ready za_ready ta_ready wg_ready "
             "tw_ready w_ready cum_ready ex_ready ss_ready rn_ready hat_ready kp_ready ft_ready ftc_ready "
             "l_ready p1t_ready p1_ready")
        (lvov_ready, lv_ready, uw_ready, vb_ready,
         arch_act, arch_dve, arch_pool, bp_ready, rr_ready, k2_ready, rf_ready, gb_ready, dve1, pool1) = sems(
             "lvov_ready lv_ready uw_ready vb_ready "
             "arch_act arch_dve arch_pool bp_ready rr_ready k2_ready rf_ready gb_ready dve1 pool1")
        y_ready, ysb_ready, pp_ready, pu_ready, qq_ready, q_ready = (
            sems(f"{n}0 {n}1") for n in ("y_ready", "ysb_ready", "pp_ready", "pu_ready", "qq_ready", "q_ready"))
        s_ready, sap_ready, sa_ready, ops_ready, sps_ready, eh_ready, es_ready, oo_ready = sems(
            "s_ready sap_ready sa_ready ops_ready sps_ready eh_ready es_ready oo_ready")
        (mv2_ready, rs2_ready, og_ready, ogt_ready, ogtc_ready, att_ready, mv3_ready, rs3_ready, xn_ready,
         x1_ready, rank_ready, xr_ready, xd_ready, x2t_ready, xhl_ready, lg_ready, ls_ready, pex_ready,
         cf_ready, cr_ready, cp_ready, ct_ready, ctc_ready) = sems(
             "mv2_ready rs2_ready og_ready ogt_ready ogtc_ready att_ready mv3_ready rs3_ready xn_ready "
             "x1_ready rank_ready xr_ready xd_ready x2t_ready xhl_ready lg_ready ls_ready pex_ready "
             "cf_ready cr_ready cp_ready ct_ready ctc_ready")
        z_ready, c_ready, relu_done, hc_done, y_done, y_sum, ys_ready, fin_ready, fin_done, stored = sems(
            "z_ready c_ready relu_done hc_done y_done y_sum ys_ready fin_ready fin_done stored")
        dve2, pool2 = sems("dve2 pool2")

        block = ctx.enter_context(nc.Block())

        class Chain:

            def __init__(self, eng, s):
                self.eng, self.s, self.n = eng, s, 0

            def mark(self, ins):
                self.n += 1
                ins.then_inc(self.s, 1)
                return self.n

            def wait(self, n):
                self.eng.wait_ge(self.s, n)

            def link(self, ins):
                self.wait(self.mark(ins))

        SLOT = [0, 1, 2, 1, 2, 1] + list(range(NU - NTXT, NU))
        HQ = [2 * (k % NIMG) for k in range(3 * NIMG)] + [2 * NIMG + 2 * t for t in range(NTXT)]

        def skip(*_):
            pass

        def level(r, li, levels):
            return r * levels + li + 1

        SLOTS = ((NU - 2, NU - 1), (0, 1), (2, 3))

        def bank(s, i):
            return PS[:, 3 * s + i, :]

        def wide(r, s):
            return PS[:, 6 + s, :] if r else bank(s, 1)

        DONE = {u: 2 * r + s + 1 for r, us in enumerate(SLOTS) for s, u in enumerate(us)}
        IMAGE, TEXT = range(4), range(4, 10)

        SCAN_BANK, Z_BANK, C_BANK, Y_BANK, FIN_BANK = (6, 7), (3, 4), (5, 0), 1, 2
        OUT_BANK = (2, 1, 7)
        FFN_BANK = (2, 6, 7)

        def run(patch=skip, texts=skip, factors=skip, image=skip, proj=skip, lora=skip, cum=skip, hats=skip,
                gates=skip, products=skip, keep=skip, turn=skip, apply=skip, lt=skip, tlt=skip, out=skip,
                scan_a=skip, scan_b=skip, stats=skip, centre=skip, heads=skip, att=skip, split=skip, rest=skip,
                feat=skip, rank=skip, choose=skip, parts=skip, weights=skip, experts=skip, total=skip, fold=skip):
            patch()
            texts()
            factors()
            image(0)
            proj(0, 0)
            image(1)
            proj(0, 1)
            lora(0, 0)
            lora(0, 1)
            cum(0, 0)
            cum(0, 1)
            image(2)
            hats(0, 0)
            gates(0, 0)
            hats(0, 1)
            image(3)
            gates(0, 1)
            products(0, 0)
            products(0, 1)
            turn(0, 0)
            keep(0, 0)
            keep(0, 1)
            turn(0, 1)
            image(4)
            apply(0, 0)
            lt(0, 0, 0)
            lt(0, 0, 1)
            apply(0, 1)
            image(5)
            tlt(0, 0, 0)
            tlt(0, 0, 1)
            lt(0, 1, 0)
            lt(0, 1, 1)
            tlt(0, 1, 0)
            tlt(0, 1, 1)
            proj(1, 0)
            lt(0, 2, 0)
            proj(1, 1)
            lt(0, 2, 1)
            tlt(0, 2, 0)
            lora(1, 0)
            tlt(0, 2, 1)
            cum(1, 0)
            lora(1, 1)
            lt(0, 3, 0)
            lt(0, 3, 1)
            cum(1, 1)
            tlt(0, 3, 1)
            tlt(0, 3, 0)
            out(0, 0)
            hats(1, 0)
            out(0, 1)
            hats(1, 1)
            products(1, 0)
            products(1, 1)
            turn(1, 0)
            keep(1, 0)
            gates(1, 0)
            keep(1, 1)
            turn(1, 1)
            apply(1, 0)
            gates(1, 1)
            proj(2, 0)
            apply(1, 1)
            lt(1, 0, 0)
            proj(2, 1)
            lt(1, 0, 1)
            tlt(1, 0, 0)
            tlt(1, 0, 1)
            lt(1, 1, 0)
            lt(1, 1, 1)
            lora(2, 0)
            tlt(1, 1, 0)
            tlt(1, 1, 1)
            cum(2, 0)
            lora(2, 1)
            lt(1, 2, 0)
            lt(1, 2, 1)
            cum(2, 1)
            tlt(1, 2, 0)
            tlt(1, 2, 1)
            lt(1, 3, 0)
            lt(1, 3, 1)
            tlt(1, 3, 0)
            tlt(1, 3, 1)
            out(1, 0)
            hats(2, 0)
            hats(2, 1)
            gates(2, 0)
            gates(2, 1)
            out(1, 1)
            products(2, 0)
            products(2, 1)
            turn(2, 0)
            turn(2, 1)
            keep(2, 0)
            scan_a(0)
            keep(2, 1)
            apply(2, 0)
            lt(2, 0, 0)
            apply(2, 1)
            scan_b(0)
            lt(2, 0, 1)
            tlt(2, 0, 0)
            scan_a(1)
            tlt(2, 0, 1)
            lt(2, 1, 0)
            scan_b(1)
            lt(2, 1, 1)
            tlt(2, 1, 0)
            tlt(2, 1, 1)
            lt(2, 2, 0)
            lt(2, 2, 1)
            tlt(2, 2, 0)
            tlt(2, 2, 1)
            lt(2, 3, 0)
            tlt(2, 3, 0)
            lt(2, 3, 1)
            out(2, 0)
            tlt(2, 3, 1)
            scan_a(2)
            out(2, 1)
            scan_b(2)
            scan_a(3)
            scan_b(3)
            scan_a(4)
            stats(0)
            centre(0)
            scan_b(4)
            heads(0)
            scan_a(5)
            att(0)
            scan_b(5)
            scan_a(6)
            split(0)
            stats(1)
            rest(0)
            scan_b(6)
            feat(0, 0)
            centre(1)
            scan_a(7)
            feat(0, 1)
            heads(1)
            rank(0)
            scan_b(7)
            choose(0)
            att(1)
            scan_a(8)
            split(1)
            parts(0)
            scan_b(8)
            weights(0, 0)
            stats(2)
            rest(1)
            centre(2)
            experts(0, 0)
            experts(0, 1)
            feat(1, 0)
            feat(1, 1)
            heads(2)
            experts(0, 2)
            att(2)
            rank(1)
            experts(0, 3)
            choose(1)
            weights(0, 1)
            experts(1, 0)
            parts(1)
            total(0)
            split(2)
            rest(2)
            experts(1, 1)
            fold(0)
            weights(1, 0)
            feat(2, 0)
            experts(1, 2)
            feat(2, 1)
            experts(1, 3)
            rank(2)
            total(1)
            experts(2, 0)
            fold(1)
            weights(1, 1)
            experts(2, 1)
            experts(2, 2)
            experts(2, 3)
            choose(2)
            experts(3, 0)
            parts(2)
            total(2)
            experts(3, 1)
            weights(2, 0)
            experts(3, 2)
            weights(2, 1)
            experts(3, 3)
            fold(2)
            experts(4, 0)
            total(3)
            experts(4, 1)
            experts(4, 2)
            experts(4, 3)
            fold(3)
            experts(5, 0)
            total(4)
            experts(5, 1)
            experts(5, 2)
            experts(5, 3)
            fold(4)
            total(5)
            fold(5)

        @block.sync
        def _(sp):
            sp.dma_start(PT[:, :, :], patches).then_inc(l_patch, 16)
            sp.dma_start(KC[:, 0:P], consts[:, 0:P]).then_inc(l_ident, 16)
            sp.dma_start(KC[:, P:], consts[:, P:]).then_inc(l_const, 16)
            sp.dma_start(AW[:, :], attw).then_inc(l_attw, 16)
            sp.dma_start(W1raw, w1).then_inc(l_w1, 16)
            sp.dma_start(W2[:, :], w2).then_inc(l_w2, 16)
            width = HALF * D
            for u in range(2 * GROUPS):
                sp.wait_ge(fin_done, u + 1)
                sp.dma_start(out[:, u * width:(u + 1) * width],
                             H1[:, u * HALF:(u + 1) * HALF, :].rearrange("p q d -> p (q d)")).then_inc(stored, 16)
            sp.wait_ge(stored, 16 * 2 * GROUPS)

        @block.gpsimd
        def _(pool):
            c0 = Chain(pool, pool0)
            c0.link(nc.gpsimd.memset(half[:, :], -0.5))
            c0.link(nc.gpsimd.memset(XT[D:P, 0, :, :, 0:1], 0.0))
            for s in range(2):
                c0.link(nc.gpsimd.memset(TH[s][D:P, :], 0.0))
                c0.link(nc.gpsimd.memset(TH[s][D:D + 1, :], 1.0))
                c0.link(nc.gpsimd.memset(FZ[s][0:D, 1, :, :], 0.0))
                last = nc.gpsimd.memset(FZ[s][D:P, 0, :, :], 0.0)
                if s == 0:
                    c0.link(last)
            last.then_inc(memsets, 1)
            pool.wait_ge(memsets, 1)

            def rsqrt0(i, tiles):
                t = slice(tiles.start, tiles.stop)
                pool.wait_ge(var_ready, i + 1)
                c0.link(nc.gpsimd.tensor_scalar(rs0[:, t, :], mv0[:, t, 1:2], EPS, None, ALU.add))
                nc.gpsimd.tensor_tensor(rs0[:, t, :], rs0[:, t, :], half[:, 0:len(tiles)].unsqueeze(2), ALU.pow)\
                    .then_inc(rs_ready, 1)

            def patch():
                rsqrt0(0, IMAGE)

            def texts():
                rsqrt0(1, TEXT)
                for name in ("Wf", "Rf"):
                    w = ARC[name]
                    c0.link(nc.gpsimd.memset(ARCH[0:D, :, w.start + P:w.stop], 0.0))
                    c0.link(nc.gpsimd.memset(ARCH[D:P, :, w.start:w.start + P], 0.0))
                nc.gpsimd.memset(ST[0][:, :], 0.0).then_inc(memsets, 1)
                pool.wait_ge(memsets, 2)

            def factors():
                pool.wait_ge(w_rounded, 1)
                nc.gpsimd.tensor_tensor(W1l[:, :], W1raw, W1h[:, :].bitcast(F32), ALU.subtract).then_inc(w_rest, 1)

            def image(i):
                if i % 2 == 0:
                    rsqrt0(2 + i // 2, IMAGE)

            c1 = Chain(pool, pool1)

            def block(dst, src):
                return nc.gpsimd.tensor_tensor(dst, src.to_broadcast([P, J, D]),
                                               const("block").rearrange("p (j d) -> p j d", j=J), ALU.mult)

            def proj(r, s):
                pool.wait_ge(sgt_ready, 2 * r + (s + 1))
                nc.gpsimd.tensor_scalar(SG[s][:, :], SG[s][:, :], 0.5, 0.5, ALU.mult, ALU.add)\
                    .then_inc(sg_ready, 1)

            def lora(r, s):
                pool.wait_ge(ss_ready, 2 * r + (s + 1))
                c1.link(nc.gpsimd.tensor_scalar(RN[s][:, :, :], SS[s][:, :, :], 1e-24, None, ALU.max))
                nc.gpsimd.tensor_tensor(RN[s][:, :, :], RN[s][:, :, :], half[:, 0:G].unsqueeze(2), ALU.pow)\
                    .then_inc(rn_ready, 1)
                pool.wait_ge(rk_ready, 2 * r + (s + 1))
                pool.wait_ge(l_rows, 16)
                nc.gpsimd.tensor_tensor(RR[s][:, :, :], RK[s][:, :, 0, :], row("r_k"), ALU.mult)\
                    .then_inc(rr_ready, 1)

            def cum(r, s):
                pool.wait_ge(l_const, 16)
                pool.wait_ge(rk_ready, 2 * r + (s + 1))
                for g in range(G):
                    last = block(VB[s][:, g, :, :], RK[s][:, g, 2:3, :])
                last.then_inc(vb_ready, 1)

            def gates(r, s):
                pool.wait_ge(k2_ready, 2 * r + (s + 1))
                pool.wait_ge(ex_ready, 2 * r + (s + 1))
                nc.gpsimd.tensor_tensor(KP[s][:, :, :], K2[s][:, :, :], EX[s][:, 2, :, :], ALU.mult)\
                    .then_inc(kp_ready, 1)
                pool.wait_ge(bp_ready, 2 * r + (s + 1))
                for g in range(G):
                    w = ARC["Bp"].start + g * J * D
                    last = block(ARCH[:, SLOTS[r][s], w:w + J * D].rearrange("p (j d) -> p j d", j=J),
                                 BP[s][:, g:g + 1, :])
                last.then_inc(arch_pool, 1)

            c2 = Chain(pool, pool2)

            def scan_a(k):
                if k:
                    pool.wait_ge(s_ready, k)
                u = SLOT[k]
                pool.wait_ge(arch_act, DONE[u])
                nc.gpsimd.tensor_tensor(ES[:, :].rearrange("p (j d) -> p j d", j=J),
                                        ST[k % 2][:, :].rearrange("p (j d) -> p j d", j=J),
                                        ARCH[:, u, ARC["E"]].unsqueeze(2).to_broadcast([P, J, D]), ALU.mult)\
                    .then_inc(es_ready, 1)
                pool.wait_ge(es_ready, k + 1)
                nc.gpsimd.tensor_tensor(EHs[:, :], ES[:, :], ARCH[:, u, ARC["H"]], ALU.add).then_inc(eh_ready, 1)

            def rsqrt(mv, ve, rs, eps, done):
                c2.link(nc.gpsimd.tensor_scalar(ve[:, :, :], mv[:, :, 1:2], eps, None, ALU.add))
                nc.gpsimd.tensor_tensor(rs[:, :, :], ve[:, :, :], half[:, 0:Q].unsqueeze(2), ALU.pow)\
                    .then_inc(done, 1)

            def stats(i):
                pool.wait_ge(mv2_ready, i + 1)
                rsqrt(mv2, ve2, rs2, GN_EPS, rs2_ready)

            def att(i):
                pool.wait_ge(mv3_ready, i + 1)
                rsqrt(mv3, ve3, rs3, EPS, rs3_ready)

            run(patch=patch, texts=texts, factors=factors, image=image, proj=proj, lora=lora, cum=cum, gates=gates,
                scan_a=scan_a, stats=stats, att=att)

        @block.scalar
        def _(act):
            copy = nc.scalar.copy
            act.dma_start(HT[:, 4:10, :], text).then_inc(l_text, 16)
            act.dma_start(CL[:, :], cols).then_inc(l_cols, 16)
            act.dma_start(RW[:, :], rows.partition_broadcast(P)).then_inc(l_rows, 16)
            act.dma_start(TW[:, :], tokw).then_inc(l_tokw, 16)
            act.dma_start(pickraw, pick).then_inc(l_pick, 16)

            def texts():
                act.wait_ge(xtr_ready, 1)
                src = PS[:, 0:2, :].rearrange("p b n -> p (b n)").rearrange("p (q j c) -> p q j c", j=J, c=C)
                for u, q in ((3, 0), (4, 2), (5, 4)):
                    copy(XT[D:P, u, :, :, 1:C], src[D:P, q:q + 2, :, 0:C - 1])
                for u, q in ((4, 0), (5, 2)):
                    last = copy(XT[D:P, u, :, :, 0:1], src[D:P, q:q + 2, :, C - 1:C])
                last.then_inc(xt_act, 1)

            def factors():
                act.wait_ge(l_pick, 16)
                copy(PK[:, :], pickraw).then_inc(pick_ready, 1)
                act.wait_ge(l_w1, 16)
                copy(W1h[:, :], W1raw).then_inc(w_rounded, 1)

            def image(i):
                if i == 3:
                    act.wait_ge(zh_ready, 1)
                    nc.scalar.activation(th0[:, :, :], nT0[:, :, :], ACT.Tanh).then_inc(zt_ready, 1)
                if i == 5:
                    act.wait_ge(tr_ready, 4)
                    act.wait_ge(memsets, 1)
                    src = PS[:, 7, :].rearrange("p (q j c) -> p q j c", j=J, c=C)
                    for u, q in ((0, 0), (1, 2), (2, 0)):
                        copy(XT[D:P, u, :, :, 1:C], src[D:P, q:q + 2, :, 0:C - 1])
                    for u, q in ((1, 0), (2, 2), (3, 2)):
                        last = copy(XT[D:P, u, :, :, 0:1], src[D:P, q:q + 2, :, C - 1:C])
                    last.then_inc(xt_act, 1)

            def by_tile(n, name, src):
                for g in range(G):
                    w, rows_g = ARC[name].start + g * P, slice(g * D, (g + 1) * D)
                    last = copy(ARCH[rows_g, n, w:w + P], src[rows_g])
                return last

            def proj(r, s):
                if r == 1:
                    act.wait_ge(w_rest, 1)
                act.wait_ge(proj_ready, 2 * r + (s + 1))
                copy(RK[s][:, :, :, :].rearrange("p g w d -> p (g w d)"), bank(s, 0)).then_inc(rk_ready, 1)
                act.wait_ge(hid_ready, 2 * r + (s + 1))
                act.wait_ge(memsets, 1)
                nc.scalar.activation(TH[s][0:D, :], wide(r, s)[0:D, 0:G * P], ACT.Tanh).then_inc(th_ready, 1)
                nc.scalar.activation(SG[s][:, :], wide(r, s)[:, G * P:2 * G * P], ACT.Tanh, scale=0.5)\
                    .then_inc(sgt_ready, 1)

            def lora(r, s):
                act.wait_ge(za_ready, 2 * r + (s + 1))
                nc.scalar.activation(TA[s][:, :, :], ZA[s][:, :, :], ACT.Tanh, scale=0.5).then_inc(ta_ready, 1)
                act.wait_ge(wg_ready, 2 * r + (s + 1))
                nc.scalar.activation(TWd[s][:, :, :], wide(r, s)[:, 0:2 * G * D].rearrange(
                    "p (g w d) -> p g w d", g=G, w=2)[:, :, 0, :], ACT.Tanh, scale=0.5).then_inc(tw_ready, 1)

            def cum(r, s):
                act.wait_ge(cum_ready, 2 * r + (s + 1))
                if r:
                    act.wait_ge(kp_ready, 2 * (r - 1) + (s + 1))
                nc.scalar.activation(EX[s][:, :, :, :].rearrange("p w g d -> p (w g d)"),
                                     bank(s, 0)[:, 0:3 * P], ACT.Exp)
                nc.scalar.activation(ARCH[:, SLOTS[r][s], ARC["E"]], bank(s, 0)[:, 3 * P:3 * P + J], ACT.Exp)
                nc.scalar.activation(NN[s][:, :, :].rearrange("p g d -> p (g d)"), bank(s, 0)[:, 0:P],
                                     ACT.Exp, scale=-1.0).then_inc(ex_ready, 1)

            def hats(r, s):
                act.wait_ge(ft_ready, 2 * r + (s + 1))
                copy(FA[s][:, :, :].rearrange("p w t -> p (w t)"), bank(s, 0)[:, 0:2 * P])
                for g in range(G):
                    rows_g = slice(g * D, (g + 1) * D)
                    last = copy(FZ[s][rows_g, g, :, :].rearrange("p w t -> p (w t)"),
                                bank(s, 0)[rows_g, 2 * P:4 * P])
                last.then_inc(ftc_ready, 1)
                by_tile(SLOTS[r][s], "Rf", bank(s, 0)[:, P:2 * P]).then_inc(rf_ready, 1)

            def turn(r, s):
                act.wait_ge(p1t_ready, 2 * r + (s + 1))
                copy(PI[s][:, :, :].rearrange("p g t -> p (g t)"), bank(s, 0)[:, 0:G * P]).then_inc(p1_ready, 1)

            def apply(r, s):
                act.wait_ge(lvov_ready, 2 * r + (s + 1))
                copy(ARCH[:, SLOTS[r][s], ARC["OV"].start:ARC["H"].stop], bank(s, 1)[:, P:4 * P])
                copy(LV[s][:, :, :].rearrange("p g d -> p (g d)"), bank(s, 1)[:, 0:P]).then_inc(lv_ready, 1)

            def out(r, s):
                act.wait_ge(uw_ready, 2 * r + (s + 1))
                copy(ARCH[:, SLOTS[r][s], ARC["U"]], bank(s, 2)[:, 0:P])
                by_tile(SLOTS[r][s], "Wf", bank(s, 2)[:, P:2 * P]).then_inc(arch_act, 1)

            def heads(i):
                act.wait_ge(ogt_ready, i + 1)
                copy(OGT[:, :, :].rearrange("p c t -> p (c t)"), PS[:, OUT_BANK[i], 0:T * P]).then_inc(ogtc_ready, 1)

            def split(i):
                act.wait_ge(xn_ready, i + 1)
                copy(XD[:, :, 0, :], XN[:, :, :]).then_inc(xr_ready, 1)

            def feat(i, h):
                act.wait_ge(x2t_ready, 2 * i + h + 1)
                copy(XHL[i][:, h * HALF:(h + 1) * HALF, :].rearrange("p q t -> p (q t)"),
                     PS[:, FFN_BANK[i], 0:HALF * P])\
                    .then_inc(xhl_ready, 1)

            def rank(i):
                act.wait_ge(ls_ready, i + 1)
                nc.scalar.activation(PX[:, :, :], LS[:, :, :], ACT.Exp).then_inc(pex_ready, 1)

            def parts(i):
                act.wait_ge(cf_ready, i + 1)
                copy(CP[:, :, 0, :].bitcast(F32R), CF[:, i * Q:(i + 1) * Q, :]).then_inc(cr_ready, 1)

            def weights(i, h):
                act.wait_ge(ct_ready, 2 * i + h + 1)
                copy(CT[i % 2][:, h * HALF * P:(h + 1) * HALF * P], PS[0:2 * E, FFN_BANK[i], 0:HALF * P])\
                    .then_inc(ctc_ready, 1)

            def experts(u, v):
                for e in (2 * v, 2 * v + 1):
                    x = E * u + e
                    act.wait_ge(z_ready, x + 1)
                    if x >= 2:
                        act.wait_ge(hc_done, x - 1)
                    nc.scalar.activation(RL[x % 2][:, :], PS[:, Z_BANK[x % 2], 0:HALF * P], ACT.Relu,
                                         bias=CL[:, COLS["b1e"]][:, e:e + 1]).then_inc(relu_done, 1)

            def total(u):
                act.wait_ge(y_sum, u + 1)
                if u:
                    act.wait_ge(fin_ready, u)
                copy(YS[:, :], PS[:, Y_BANK, 0:HALF * P]).then_inc(ys_ready, 1)

            run(texts=texts, factors=factors, image=image, proj=proj, lora=lora, cum=cum, hats=hats, turn=turn,
                apply=apply, out=out, heads=heads, split=split, feat=feat, rank=rank, parts=parts, weights=weights,
                experts=experts, total=total)

        @block.vector
        def _(dve):
            V = nc.vector
            TT, TS, STT = V.tensor_tensor, V.tensor_scalar, V.scalar_tensor_tensor
            c0 = Chain(dve, dve0)

            def variances(src, tiles):
                for q in tiles:
                    last = V.bn_stats(st0[:, q, :], src(q))
                c0.link(last)
                for q in tiles:
                    last = V.bn_aggr(mv0[:, q, :], st0[:, q, :])
                last.then_inc(var_ready, 1)

            def normalised(dst, src, tiles, count):
                dve.wait_ge(var_ready, count)
                dve.wait_ge(rs_ready, count)
                for q in tiles:
                    last = TS(dst(q), src(q), mv0[:, q, 0:1], rs0[:, q, 0:1], ALU.subtract, ALU.mult)
                return last

            def side_by_side(tiles, centred, count):
                t, n = slice(tiles.start, tiles.stop), len(tiles)
                dve.wait_ge(var_ready, count)
                c0.link(TT(centred, HT[:, t, :], mv0[:, t, 0:1].to_broadcast([P, n, D]), ALU.subtract))
                dve.wait_ge(rs_ready, count)
                return TT(XHD[:, t, :, :], centred.unsqueeze(2).to_broadcast([P, n, 2, D]),
                          rs0[:, t, :].unsqueeze(3).to_broadcast([P, n, 2, D]), ALU.mult)

            def col(name):
                return CL[:, COLS[name]]

            def patch():
                dve.wait_ge(l_patch, 16)
                variances(lambda q: PT[:, q, :], IMAGE)
                dve.wait_ge(l_text, 16)
                variances(lambda q: HT[:, q, :], TEXT)
                normalised(lambda q: xh0[:, q, :], lambda q: PT[:, q, :], IMAGE, 1).then_inc(xh_ready, 1)

            def texts():
                side_by_side(TEXT, YS[:, :].rearrange("p (q d) -> p q d", q=Q), 2).then_inc(xhd_ready, 1)
                dve.wait_ge(l_cols, 16)
                dve.wait_ge(l_rows, 16)
                TS(mix[0:D, :], col("mix")[0:D, :], -1.0, 1.0, ALU.mult, ALU.add)
                V.tensor_copy(mix[D:P, :], col("mix")[D:P, :])
                TS(kaH[:, :], RW[:, ROWS["k_a"]], 0.5, None, ALU.mult)
                TT(gbias[:, :], RW[:, ROWS["bg"]], RW[:, ROWS["bias"]], ALU.add)
                c0.link(TS(lnpH[:, :], CL[:, COLS["lnp_g"].start:COLS["lnp_b"].stop], 0.5, None, ALU.mult))
                dve.wait_ge(tr_ready, 1)
                for h in range(2):
                    last = TS(xT0[0:PH, h, :], PS[0:PH, 6 + h, :], col("ln1_g")[0:PH, h:h + 1],
                              col("ln1_b")[0:PH, h:h + 1], ALU.mult, ALU.add)
                last.then_inc(nt_ready, 1)

            def factors():
                dve.wait_ge(l_attw, 16)
                for i, m in ((0, 0), (1, 2), (2, 3)):
                    TS(Wproj[:, i * D:(i + 1) * D], AW[:, ATTW["rkv"]][:, i * D:(i + 1) * D], mix[:, m:m + 1], None,
                       ALU.mult)
                TS(Wlora[:, 0:D], AW[:, ATTW["A_w"]], mix[:, 1:2], None, ALU.mult)
                TS(Wlora[:, D:D + P], AW[:, ATTW["A_g"]], mix[:, 5:6], None, ALU.mult)
                dve.wait_ge(xtr_ready, 1)
                src = PS[:, 0:2, :].rearrange("p b n -> p (b n)").rearrange("p (q j c) -> p q j c", j=J, c=C)
                for u, q in ((3, 0), (4, 2), (5, 4)):
                    last = V.tensor_copy(XT[0:D, u, :, :, :], src[0:D, q:q + 2, :, :])
                last.then_inc(xt_dve, 1)
                dve.wait_ge(aab_ready, 1)
                TS(Wproj[:, 3 * D:4 * D], PS[:, 2, 0:D], mix[:, 4:5], None, ALU.mult).then_inc(mix_ready, 1)

            def by_group(ap):
                return ap.rearrange("p (c g) d -> p c g d", g=G)

            def product():
                return PS[:, 6, 0:4 * D].rearrange("p (c g d) -> p c g d", g=G, c=2)

            def row4(name):
                return RW[:, ROWS[name]].unsqueeze(1).unsqueeze(1).to_broadcast([P, 2, G, D])

            def image(i):
                if i < 4 and i % 2 == 0:
                    dve.wait_ge(mm_ready, i // 2 + 1)
                    c0.link(TT(by_group(t0[:, :, :]), product(), row4(("b1", "bp1")[i // 2]), ALU.add))
                    variances(lambda q: t0[:, q, :], IMAGE)
                if i in (1, 3):
                    normalised(lambda q: n0[:, q, :], lambda q: t0[:, q, :], IMAGE, 3 + i // 2)\
                        .then_inc(xh_ready, 1)
                    dve.wait_ge(tr_ready, 2 + i // 2)
                features = PS[:, 7, 0:2 * P].rearrange("p (c t) -> p c t", c=2)
                if i == 1:
                    TS(nT0[:, :, :], features, col("ln2_g"), col("ln2_b"), ALU.mult, ALU.add).then_inc(nt_ready, 1)
                if i == 3:
                    TS(nT0[:, :, :], features, lnpH[:, 0:1], lnpH[:, 1:2], ALU.mult, ALU.add).then_inc(zh_ready, 1)
                    dve.wait_ge(zh_ready, 1)
                    dve.wait_ge(zt_ready, 1)
                    STT(nT0[:, :, :], th0[:, :, :], 1.0, nT0[:, :, :], ALU.add, ALU.mult).then_inc(nt_ready, 1)
                if i == 4:
                    dve.wait_ge(mm_ready, 3)
                    c0.link(TT(by_group(HT[:, 0:4, :]), product(), row4("bp2"), ALU.add))
                    variances(lambda q: HT[:, q, :], IMAGE)
                if i == 5:
                    side_by_side(IMAGE, n0, 5).then_inc(xh_ready, 1)
                    dve.wait_ge(tr_ready, 4)
                    src = PS[:, 7, :].rearrange("p (q j c) -> p q j c", j=J, c=C)
                    for u, q in ((0, 0), (1, 2), (2, 0)):
                        last = V.tensor_copy(XT[0:D, u, :, :, :], src[0:D, q:q + 2, :, :])
                    last.then_inc(xt_dve, 1)

            c1 = Chain(dve, dve1)

            def flat(t):
                return t.rearrange("p g d -> p (g d)")

            kk, kn, b2, bon = [0, 0], [0, 0], [0, 0], [0, 0]

            def proj(r, s):
                dve.wait_ge(rk_ready, 2 * r + (s + 1))
                TT(ZA[s][:, :, :], RK[s][:, :, 3, :], row("b_a"), ALU.add).then_inc(za_ready, 1)
                kk[s] = c1.mark(TT(KK[s][:, :, :], RK[s][:, :, 1, :], row("k_k"), ALU.mult))
                c1.wait(kk[s])
                c1.link(TT(SQ[s][:, :, :], KK[s][:, :, :], KK[s][:, :, :], ALU.mult))
                V.tensor_reduce(SS[s][:, :, :], SQ[s][:, :, :], AX.X, ALU.add).then_inc(ss_ready, 1)

            def lora(r, s):
                dve.wait_ge(tw_ready, 2 * r + (s + 1))
                TS(LW[s][:, :, :], TWd[s][:, :, :], DECAY / 2, DECAY / 2, ALU.mult, ALU.add).then_inc(w_ready, 1)

            def cum(r, s):
                dve.wait_ge(ta_ready, 2 * r + (s + 1))
                if r:
                    dve.wait_ge(kp_ready, 2 * (r - 1) + (s + 1))
                c1.link(STT(T1[s][:, :, :], TA[s][:, :, :], -1.0,
                            kaH[:, :].unsqueeze(1).to_broadcast([P, G, D]), ALU.add, ALU.mult))
                STT(K2[s][:, :, :], T1[s][:, :, :], 1.0, RK[s][:, :, 1, :], ALU.add, ALU.mult)\
                    .then_inc(k2_ready, 1)
                dve.wait_ge(rn_ready, 2 * r + (s + 1))
                kn[s] = c1.mark(TT(KN[s][:, :, :], KK[s][:, :, :], RN[s][:, :, :].to_broadcast([P, G, D]),
                                   ALU.mult))
                dve.wait_ge(k2_ready, 2 * r + (s + 1))
                dve.wait_ge(rr_ready, 2 * r + (s + 1))
                mm = c1.mark(TT(MM[s][:, :, :], RR[s][:, :, :], K2[s][:, :, :], ALU.mult))
                c1.wait(kn[s])
                b2[s] = c1.mark(STT(B2[s][:, :, :], TA[s][:, :, :], 1.0, KN[s][:, :, :], ALU.add, ALU.mult))
                c1.wait(mm)
                bon[s] = c1.mark(V.tensor_reduce(BON[s][:, :, :], MM[s][:, :, :], AX.X, ALU.add))

            def hats(r, s):
                if r == 1:
                    dve.wait_ge(w_rest, 1)
                dve.wait_ge(ex_ready, 2 * r + (s + 1))
                c1.wait(b2[s])
                if r:
                    dve.wait_ge(arch_pool, 2 * (r - 1) + (s + 1))
                EXs = EX[s]
                STT(HA[r % 2][s][:, :, :], KN[s][:, :, :], -1.0, EXs[:, 1, :, :], ALU.mult, ALU.mult)
                TT(HAT[s][:, 0, :, :], RK[s][:, :, 0, :], EXs[:, 0, :, :], ALU.mult)
                STT(HAT[s][:, 1, :, :], B2[s][:, :, :], 0.5, NN[s][:, :, :], ALU.mult, ALU.mult)
                TT(HAT[s][:, 2, :, :], K2[s][:, :, :], NN[s][:, :, :], ALU.mult).then_inc(hat_ready, 1)
                STT(BP[s][:, :, :], B2[s][:, :, :], 0.5, EXs[:, 2, :, :], ALU.mult, ALU.mult)\
                    .then_inc(bp_ready, 1)

            def gates(r, s):
                kept = ARCH[:, SLOTS[r][s]:SLOTS[r][s] + 1, :]
                dve.wait_ge(wg_ready, 2 * r + (s + 1))
                gate = wide(r, s)[:, 0:2 * G * D].rearrange("p (g w d) -> p g w d", g=G, w=2)[:, :, 1, :]
                c1.wait(bon[s])
                for g in range(G):
                    last = STT(VBN[s][:, g, :], RK[s][:, g, 2, :], BON[s][:, g, :], RW[:, ROWS["gn_b"]],
                               ALU.mult, ALU.add)
                vbn = c1.mark(last)
                TT(kept[:, :, ARC["GW"]].rearrange("p u (g d) -> p (u g) d", g=G), gate, row("gn_w"), ALU.mult)
                c1.wait(vbn)
                TT(kept[:, :, ARC["GB"]].rearrange("p u (g d) -> p (u g) d", g=G), gate, VBN[s][:, :, :],
                   ALU.mult).then_inc(gb_ready, 1)

            def products(r, s):
                dve.wait_ge(l_const, 16)
                dve.wait_ge(l_ident, 16)
                masks = const("masks")
                for g in range(G):
                    dve.wait_ge(l_ready, 4 * r + (2 * s + g + 1))
                    last = TT(AT[s][:, g, :], bank(s, 2 - g)[:, 0:P], masks[:, 0:P], ALU.mult)
                c1.link(last)
                c1.link(TT(QA[s][:, :, :], AT[s][:, :, :], twice(const("m1")), ALU.mult))
                TT(QT[s][:, :, :], QA[s][:, :, :], twice(ident), ALU.add).then_inc(q_ready[s], 1)

            def keep(r, s):
                masks = const("masks")
                for g in range(G):
                    L = bank(s, 2 - g)
                    TT(LKT[s][:, g, :, :].rearrange("p w t -> p (w t)"), L[:, 2 * P:4 * P], masks, ALU.mult)
                    lrb = ARC["LrbT"].start + g * P
                    last = TT(ARCH[:, SLOTS[r][s], lrb:lrb + P], L[:, P:2 * P], masks[:, P:2 * P], ALU.mult)
                last.then_inc(arch_dve, 1)

            def lt(r, li, s):
                dve.wait_ge(y_ready[s], level(r, li, 4))
                TT(YI[s][:, :, :], pairs(bank(s, 2)[:, 0:G * P]), twice(const(f"m{LEVELS[li]}")), ALU.mult)\
                    .then_inc(ysb_ready[s], 1)

            def tlt(r, li, s):
                if li < 3:
                    dve.wait_ge(pp_ready[s], level(r, li, 3))
                    TT(flat(PI[s][:, :, :]), flat(PI[s][:, :, :]), bank(s, 2)[:, 0:G * P], ALU.add)\
                        .then_inc(pu_ready[s], 1)
                dve.wait_ge(qq_ready[s], level(r, li, 4))
                TT(flat(QT[s][:, :, :]), flat(QT[s][:, :, :]), bank(s, 1)[:, 0:G * P], ALU.add)\
                    .then_inc(q_ready[s], 1)

            m = Chain(dve, dve2)

            def scan_a(k):
                dve.wait_ge(arch_act, DONE[SLOT[k]])
                dve.wait_ge(sap_ready, k + 1)
                TT(SA[:, :, :], pairs(PS[:, SCAN_BANK[k % 2], 0:P]), pairs(ARCH[:, SLOT[k], ARC["U"]]), ALU.add)\
                    .then_inc(sa_ready, 1)

            def scan_b(k):
                dve.wait_ge(eh_ready, k + 1)
                dve.wait_ge(sps_ready, k + 1)
                TT(ST[1 - k % 2][:, :], EHs[:, :], PS[:, SCAN_BANK[1 - k % 2], 0:J * D], ALU.add).then_inc(s_ready, 1)
                dve.wait_ge(ops_ready, k + 1)
                TT(OO[:, G * k:G * (k + 1), :], pairs(PS[:, SCAN_BANK[k % 2], P:2 * P]),
                   pairs(ARCH[:, SLOT[k], ARC["OV"]]), ALU.add).then_inc(oo_ready, 1)

            def variances_of(src, st, mv, done):
                for q in range(Q):
                    last = V.bn_stats(st[:, q, :], src(q))
                m.link(last)
                for q in range(Q):
                    last = V.bn_aggr(mv[:, q, :], st[:, q, :])
                last.then_inc(done, 1)

            def arch(i, q, name):
                return pairs(ARCH[:, SLOT[i * T + q // G], ARC[name]])[:, q % G, :]

            def stats(i):
                dve.wait_ge(oo_ready, (i + 1) * T)
                variances_of(lambda q: OO[:, i * Q + q, :], st2, mv2, mv2_ready)

            def centre(i):
                dve.wait_ge(mv2_ready, i + 1)
                for q in range(Q):
                    last = STT(X1[:, q, :], OO[:, i * Q + q, :], mv2[:, q, 0:1], arch(i, q, "GW"),
                               ALU.subtract, ALU.mult)
                last.then_inc(x1_ready, 1)

            def heads(i):
                dve.wait_ge(x1_ready, i + 1)
                dve.wait_ge(rs2_ready, i + 1)
                for q in range(Q):
                    last = STT(OG[:, q, :], X1[:, q, :], rs2[:, q, :], arch(i, q, "GB"), ALU.mult, ALU.add)
                last.then_inc(og_ready, 1)

            def att(i):
                dve.wait_ge(att_ready, i + 1)
                for c in range(T):
                    h = HQ[i * T + c]
                    last = TT(H1[:, i * Q + G * c:i * Q + G * (c + 1), :], HT[:, h:h + G, :],
                              pairs(PS[:, OUT_BANK[i], c * P:(c + 1) * P]), ALU.add)
                m.link(last)
                variances_of(lambda q: H1[:, i * Q + q, :], st3, mv3, mv3_ready)

            def split(i):
                dve.wait_ge(mv3_ready, i + 1)
                m.link(TT(XN[:, :, :], H1[:, i * Q:(i + 1) * Q, :], mv3[:, :, 0:1].to_broadcast([P, Q, D]),
                          ALU.subtract))
                dve.wait_ge(rs3_ready, i + 1)
                TT(XN[:, :, :], XN[:, :, :], rs3[:, :, :].to_broadcast([P, Q, D]), ALU.mult).then_inc(xn_ready, 1)

            def rest(i):
                dve.wait_ge(xn_ready, i + 1)
                dve.wait_ge(xr_ready, i + 1)
                TT(XD[:, :, 1, :], XN[:, :, :], XD[:, :, 0, :].bitcast(F32), ALU.subtract).then_inc(xd_ready, 1)

            def per_tile(ap):
                return ap.to_broadcast([P, Q, E])

            def rank(i):
                dve.wait_ge(lg_ready, i + 1)
                m.link(TT(LG[:, :, :], PS[:, FFN_BANK[i], 0:Q * E].rearrange("p (q e) -> p q e", q=Q),
                          per_tile(gbias[:, :].unsqueeze(1)), ALU.add))
                largest = m.mark(V.tensor_reduce(M1[:, :, :], LG[:, :, :], AX.X, ALU.max))
                differences = m.mark(TT(DD[:, :, :, :], LG[:, :, :].unsqueeze(2).to_broadcast([P, Q, E, E]),
                                        LG[:, :, :].unsqueeze(3).to_broadcast([P, Q, E, E]), ALU.subtract))
                m.wait(largest)
                TT(LS[:, :, :], LG[:, :, :], per_tile(M1[:, :, :]), ALU.subtract).then_inc(ls_ready, 1)
                m.wait(differences)

                def square(t):
                    return t[:, :, :, :].rearrange("p q e f -> p q (e f)")
                m.link(STT(square(D1), square(DD), 0.0, const("tri").unsqueeze(1).to_broadcast([P, Q, E * E]),
                           ALU.is_equal, ALU.mult))
                m.link(STT(square(D2), square(DD), 0.0, square(D1), ALU.is_gt, ALU.add))
                V.tensor_reduce(RKs[:, :, :].unsqueeze(3), D2[:, :, :, :], AX.X, ALU.add).then_inc(rank_ready, 1)

            def choose(i):
                dve.wait_ge(rank_ready, i + 1)
                dve.wait_ge(pex_ready, i + 1)
                m.link(STT(PM[:, :, :], RKs[:, :, :], 2.0, PX[:, :, :], ALU.is_lt, ALU.mult))
                m.link(V.tensor_reduce(SM[:, :, :], PM[:, :, :], AX.X, ALU.add))
                m.link(V.reciprocal(RC[:, :, :], SM[:, :, :]))
                TT(CF[:, i * Q:(i + 1) * Q, :], PM[:, :, :], per_tile(RC[:, :, :]), ALU.mult).then_inc(cf_ready, 1)

            def parts(i):
                dve.wait_ge(cf_ready, i + 1)
                dve.wait_ge(cr_ready, i + 1)
                TT(CP[:, :, 1, :].bitcast(F32R), CF[:, i * Q:(i + 1) * Q, :], CP[:, :, 0, :], ALU.subtract)\
                    .then_inc(cp_ready, 1)

            def experts(u, v):
                for e in (2 * v, 2 * v + 1):
                    x = E * u + e
                    dve.wait_ge(relu_done, x + 1)
                    dve.wait_ge(c_ready, x + 1)
                    if x >= 4:
                        dve.wait_ge(y_done, x - 3)
                    TT(HC[x % 4][:, :], RL[x % 2][:, :], PS[:, C_BANK[x % 2], 0:HALF * P], ALU.mult)\
                        .then_inc(hc_done, 1)

            def fold(u):
                dve.wait_ge(fin_ready, u + 1)
                h = H1[:, u * HALF:(u + 1) * HALF, :]
                TT(h, h, PS[:, FIN_BANK, 0:HALF * D].rearrange("p (q d) -> p q d", q=HALF), ALU.add)\
                    .then_inc(fin_done, 1)

            run(patch=patch, texts=texts, factors=factors, image=image, proj=proj, lora=lora, cum=cum, hats=hats,
                gates=gates, products=products, keep=keep, lt=lt, tlt=tlt, scan_a=scan_a, scan_b=scan_b,
                stats=stats, centre=centre, heads=heads, att=att, split=split, rest=rest, rank=rank, choose=choose,
                parts=parts, experts=experts, fold=fold)

        @block.tensor
        def _(pe):
            mm = nc.tensor.matmul

            def transpose(dst, src):
                return nc.tensor.transpose(dst, src, ident)

            def patch():
                pe.wait_ge(l_ident, 16)
                pe.wait_ge(xh_ready, 1)
                for h in range(2):
                    for q in range(4):
                        last = transpose(PS[0:PH, 6 + h, q * P:(q + 1) * P], xh0[:, q, h * PH:(h + 1) * PH])
                last.then_inc(tr_ready, 1)

            def doubled(dst, q):
                return transpose(dst, XHD[:, q, :, :].rearrange("p w d -> p (w d)"))

            def texts():
                pe.wait_ge(xhd_ready, 1)
                for i, q in enumerate(TEXT):
                    last = doubled(PS[:, i // 4, (i % 4) * P:(i % 4 + 1) * P], q)
                last.then_inc(xtr_ready, 1)
                pe.wait_ge(l_attw, 16)
                mm(PS[:, 2, 0:D], AW[0:D, ATTW["A_aT"]], AW[0:D, ATTW["B_a"]], start=True, stop=True)\
                    .then_inc(aab_ready, 1)

            def image(i):
                if i == 0:
                    pe.wait_ge(l_tokw, 16)
                    pe.wait_ge(nt_ready, 1)
                    for q in IMAGE:
                        for h in range(2):
                            last = mm(PS[:, 6, q * D:(q + 1) * D], xT0[0:PH, h, q * P:(q + 1) * P],
                                      TW[0:PH, TOKW["W1"]][:, h * D:(h + 1) * D], start=h == 0, stop=h == 1)
                    last.then_inc(mm_ready, 1)
                if i in (2, 4):
                    pe.wait_ge(nt_ready, i // 2 + 1)
                    for c in range(2):
                        last = mm(PS[:, 6, c * P:(c + 1) * P], nT0[:, c, :], TW[:, TOKW[("Wp1", "Wp2")[i // 2 - 1]]],
                                  start=True, stop=True)
                    last.then_inc(mm_ready, 1)
                if i in (1, 3):
                    pe.wait_ge(xh_ready, i // 2 + 2)
                    for c in range(2):
                        last = transpose(PS[:, 7, c * P:(c + 1) * P],
                                         n0[:, 2 * c:2 * c + 2, :].rearrange("p g d -> p (g d)"))
                    last.then_inc(tr_ready, 1)
                if i == 5:
                    pe.wait_ge(xh_ready, 4)
                    for q in IMAGE:
                        last = doubled(PS[:, 7, q * P:(q + 1) * P], q)
                    last.then_inc(tr_ready, 1)

            masks = const("masks")

            def tile(t, g):
                return t[:, g * P:(g + 1) * P]

            def proj(r, s):
                if r == 0:
                    pe.wait_ge(mix_ready, 1)
                    pe.wait_ge(memsets, 1)
                if r < 2:
                    pe.wait_ge(xt_dve, r + 1)
                    pe.wait_ge(xt_act, r + 1)
                if r:
                    pe.wait_ge(p1_ready, 2 * (r - 1) + (s + 1))
                    pe.wait_ge(gb_ready, 2 * (r - 1) + (s + 1))
                x = XT[:, SLOTS[r][s], :, :, :].rearrange("p g j c -> p (g j c)")
                for g in range(G):
                    last = mm(bank(s, 0)[:, g * 4 * D:(g + 1) * 4 * D], tile(x, g), Wproj[:, :],
                              start=True, stop=True)
                last.then_inc(proj_ready, 1)
                mm(wide(r, s)[0:D, 0:G * P], Wlora[:, 0:D], x, start=True, stop=True)
                mm(wide(r, s)[:, G * P:2 * G * P], Wlora[:, D:D + P], x, start=True, stop=True)\
                    .then_inc(hid_ready, 1)

            def lora(r, s):
                pe.wait_ge(th_ready, 2 * r + (s + 1))
                pe.wait_ge(sg_ready, 2 * r + (s + 1))
                for g in range(G):
                    o = wide(r, s)[:, g * 2 * D:(g + 1) * 2 * D]
                    mm(o[:, 0:D], tile(TH[s], g), AW[:, ATTW["B_w"]], start=True, stop=True)
                    last = mm(o[:, D:2 * D], tile(SG[s], g), AW[:, ATTW["B_g"]], start=True, stop=True)
                last.then_inc(wg_ready, 1)

            def cum(r, s):
                pe.wait_ge(l_const, 16)
                pe.wait_ge(w_ready, 2 * r + (s + 1))
                lw = LW[s][:, :, :].rearrange("p g d -> p (g d)")
                for i, m in enumerate((masks[:, P:2 * P], masks[:, 0:P], const("suffix"))):
                    mm(bank(s, 0)[:, i * P:(i + 1) * P], m, lw, start=True, stop=True)
                for g in range(G):
                    last = mm(bank(s, 0)[g * D:(g + 1) * D, 3 * P:3 * P + J], LW[s][:, g, :], const("seq"),
                              start=True, stop=True)
                last.then_inc(cum_ready, 1)

            def hats(r, s):
                pe.wait_ge(hat_ready, 2 * r + (s + 1))
                for w, hat in enumerate((HA[r % 2][s], *(HAT[s][:, w, :, :] for w in range(3)))):
                    last = transpose(bank(s, 0)[:, w * P:(w + 1) * P], hat.rearrange("p g d -> p (g d)"))
                last.then_inc(ft_ready, 1)

            def products(r, s):
                pe.wait_ge(ftc_ready, 2 * r + (s + 1))
                if r:
                    pe.wait_ge(q_ready[s], level(r - 1, 4, 5))
                    pe.wait_ge(arch_act, 2 * (r - 1) + (s + 1))
                for g in range(G):
                    if g and r == 0:
                        pe.wait_ge(gb_ready, 2 * r + (s + 1))
                    ar = FA[s][:, :, :].rearrange("p w t -> p (w t)")
                    mm(bank(s, 2 - g)[:, 0:2 * P], FZ[s][:, g, 0, :], ar, start=True, stop=True)
                    mm(bank(s, 2 - g)[:, 2 * P:4 * P], FZ[s][:, g, 1, :], ar, start=True, stop=True)\
                        .then_inc(l_ready, 1)

            def turn(r, s):
                pe.wait_ge(q_ready[s], level(r, 0, 5))
                pe.wait_ge(rf_ready, 2 * r + (s + 1))
                for g in range(G):
                    last = transpose(bank(s, 0)[:, g * P:(g + 1) * P], QT[s][:, g, :])
                last.then_inc(p1t_ready, 1)

            def apply(r, s):
                pe.wait_ge(vb_ready, 2 * r + (s + 1))
                pe.wait_ge(kp_ready, 2 * r + (s + 1))
                pe.wait_ge(arch_dve, 2 * r + (s + 1))
                for g in range(G):
                    mm(bank(s, 1)[:, g * D:(g + 1) * D], LKT[s][:, g, 0, :], RK[s][:, g, 2, :],
                       start=True, stop=True)
                    mm(bank(s, 1)[:, P + g * D:P + (g + 1) * D], LKT[s][:, g, 1, :], RK[s][:, g, 2, :],
                       start=True, stop=True)
                    last = mm(bank(s, 1)[g * D:(g + 1) * D, 2 * P:4 * P], KP[s][:, g, :],
                              VB[s][:, g, :, :].rearrange("p j d -> p (j d)"), start=True, stop=True)
                last.then_inc(lvov_ready, 1)

            def lt(r, li, s):
                if li == 0:
                    pe.wait_ge(p1_ready, 2 * r + (s + 1))
                    pe.wait_ge(arch_dve, 2 * r + (s + 1))
                else:
                    pe.wait_ge(pu_ready[s], level(r, li - 1, 3))
                for g in range(G):
                    last = mm(bank(s, 2)[:, g * P:(g + 1) * P], AT[s][:, g, :], PI[s][:, g, :],
                              start=True, stop=True)
                last.then_inc(y_ready[s], 1)

            def tlt(r, li, s):
                pe.wait_ge(q_ready[s], level(r, li, 5))
                pe.wait_ge(ysb_ready[s], level(r, li, 4))
                if li == 0:
                    pe.wait_ge(lv_ready, 2 * r + (s + 1))
                if li < 3:
                    for g in range(G):
                        last = mm(bank(s, 2)[:, g * P:(g + 1) * P], QT[s][:, g, :], YI[s][:, g, :],
                                  start=True, stop=True)
                    last.then_inc(pp_ready[s], 1)
                for g in range(G):
                    last = mm(bank(s, 1)[:, g * P:(g + 1) * P], YI[s][:, g, :], QT[s][:, g, :],
                              start=True, stop=True)
                last.then_inc(qq_ready[s], 1)

            def out(r, s):
                pe.wait_ge(lv_ready, 2 * r + (s + 1))
                pe.wait_ge(q_ready[s], level(r, 4, 5))
                for g in range(G):
                    mm(bank(s, 2)[:, g * D:(g + 1) * D], QT[s][:, g, :], LV[s][:, g, :], start=True, stop=True)
                    last = mm(bank(s, 2)[g * D:(g + 1) * D, P:2 * P], HA[r % 2][s][:, g, :], QT[s][:, g, :],
                              start=True, stop=True)
                last.then_inc(uw_ready, 1)

            def scan_a(k):
                done = DONE[SLOT[k]]
                pe.wait_ge(arch_act, done)
                pe.wait_ge(arch_dve, done)
                pe.wait_ge(arch_pool, done)
                if k == 0:
                    pe.wait_ge(memsets, 2)
                    pe.wait_ge(gb_ready, NU)
                if k:
                    pe.wait_ge(s_ready, k)
                if k >= 2:
                    pe.wait_ge(oo_ready, k - 1)
                wf = ARCH[:, SLOT[k], ARC["Wf"]]
                for g in range(G):
                    for j in range(J):
                        last = mm(PS[j * C:(j + 1) * C, SCAN_BANK[k % 2], g * D:(g + 1) * D],
                                  wf[:, g * P + j * C:g * P + (j + 1) * C], ST[k % 2][:, j * D:(j + 1) * D],
                                  start=True, stop=True)
                last.then_inc(sap_ready, 1)

            def scan_b(k):
                u = SLOT[k]
                pe.wait_ge(sa_ready, k + 1)
                if k:
                    pe.wait_ge(oo_ready, k)
                for j in range(J):
                    for g in range(G):
                        bp = ARC["Bp"].start + (g * J + j) * D
                        last = mm(PS[g * D:(g + 1) * D, SCAN_BANK[1 - k % 2], j * D:(j + 1) * D],
                                  ARCH[:, u, bp:bp + D], SA[:, g, :], start=True, stop=True)
                last.then_inc(sps_ready, 1)
                for g in range(G):
                    o = slice(P + g * D, P + (g + 1) * D)
                    for j in range(J):
                        mm(PS[j * C:(j + 1) * C, SCAN_BANK[k % 2], o],
                           ARCH[:, u, ARC["Rf"]][:, g * P + j * C:g * P + (j + 1) * C],
                           ST[k % 2][:, j * D:(j + 1) * D], start=True, stop=False)
                    last = mm(PS[:, SCAN_BANK[k % 2], o], ARCH[:, u, ARC["LrbT"]][:, g * P:(g + 1) * P], SA[:, g, :],
                              start=False, stop=True)
                last.then_inc(ops_ready, 1)

            def heads(i):
                if i == 0:
                    pe.wait_ge(arch_act, NU)
                pe.wait_ge(og_ready, i + 1)
                for c in range(T):
                    last = transpose(PS[:, OUT_BANK[i], c * P:(c + 1) * P],
                                     OG[:, G * c:G * (c + 1), :].rearrange("p g d -> p (g d)"))
                last.then_inc(ogt_ready, 1)

            def att(i):
                pe.wait_ge(ogtc_ready, i + 1)
                for c in range(T):
                    last = mm(PS[:, OUT_BANK[i], c * P:(c + 1) * P], OGT[:, c, :], AW[:, ATTW["W_o"]],
                              start=True, stop=True)
                last.then_inc(att_ready, 1)

            def feat(i, h):
                if h:
                    pe.wait_ge(xhl_ready, 2 * i + h)
                else:
                    pe.wait_ge(xr_ready, i + 1)
                    pe.wait_ge(xd_ready, i + 1)
                for t in range(HALF):
                    last = transpose(PS[:, FFN_BANK[i], t * P:(t + 1) * P],
                                     XD[:, h * HALF + t, :, :].rearrange("p w d -> p (w d)").bitcast(F32))
                last.then_inc(x2t_ready, 1)

            def rank(i):
                pe.wait_ge(xhl_ready, 2 * i + 2)
                for q in range(Q):
                    last = mm(PS[:, FFN_BANK[i], q * E:(q + 1) * E], XHL[i][:, q, :].bitcast(F32), AW[:, ATTW["Wg"]],
                              start=True, stop=True)
                last.then_inc(lg_ready, 1)

            def weights(i, h):
                if h:
                    pe.wait_ge(ctc_ready, 2 * i + h)
                else:
                    pe.wait_ge(cp_ready, i + 1)
                for t in range(HALF):
                    last = transpose(PS[0:2 * E, FFN_BANK[i], t * P:(t + 1) * P],
                                     CP[:, h * HALF + t, :, :].rearrange("p w e -> p (w e)"))
                last.then_inc(ct_ready, 1)

            def second(u, v):
                for e in (2 * v, 2 * v + 1):
                    pe.wait_ge(hc_done, E * u + e + 1)
                    mm(PS[(e % 2) * D:(e % 2 + 1) * D, Y_BANK, 0:HALF * P], W2[:, e * D:(e + 1) * D],
                       HC[e % 4][:, :], start=v == 0, stop=False).then_inc(y_done, 1)

            def experts(u, v):
                if u == 0 and v == 0:
                    pe.wait_ge(w_rounded, 1)
                    pe.wait_ge(w_rest, 1)
                    pe.wait_ge(pick_ready, 1)
                    pe.wait_ge(l_w2, 16)
                if v == 0:
                    pe.wait_ge(xhl_ready, u + 1)
                    pe.wait_ge(ctc_ready, u + 1)
                half = slice(u % 2 * HALF, (u % 2 + 1) * HALF)
                xhl = XHL[u // 2][:, half, :].rearrange("p q t -> p (q t)")
                for e in (2 * v, 2 * v + 1):
                    x = E * u + e
                    if x >= 2:
                        pe.wait_ge(relu_done, x - 1)
                    z = PS[:, Z_BANK[x % 2], 0:HALF * P]
                    mm(z, W1h[:, e * EH:(e + 1) * EH], xhl, start=True, stop=False)
                    mm(z, W1l[:, e * EH:(e + 1) * EH], xhl, start=False, stop=True).then_inc(z_ready, 1)
                ct = CT[u // 2 % 2][:, u % 2 * HALF * P:(u % 2 + 1) * HALF * P]
                for e in (2 * v, 2 * v + 1):
                    x = E * u + e
                    if x >= 2:
                        pe.wait_ge(hc_done, x - 1)
                    mm(PS[:, C_BANK[x % 2], 0:HALF * P], PK[:, e * P:(e + 1) * P], ct, start=True, stop=True)\
                        .then_inc(c_ready, 1)
                if v == 1 and u:
                    pe.wait_ge(ys_ready, u)
                if u == 0 and v == 1:
                    pe.wait_ge(mv3_ready, 2)
                if v:
                    second(u, v - 1)

            def total(u):
                second(u, E // 2 - 1)
                mm(PS[:, Y_BANK, 0:HALF * P], AW[0:2 * E, ATTW["b2"]],
                   CT[u // 2 % 2][:, u % 2 * HALF * P:(u % 2 + 1) * HALF * P].bitcast(F32), start=False, stop=True)\
                    .then_inc(y_sum, 1)

            def fold(u):
                pe.wait_ge(ys_ready, u + 1)
                if u:
                    pe.wait_ge(fin_done, u)
                for t in range(HALF):
                    last = mm(PS[:, FIN_BANK, t * D:(t + 1) * D], YS[:, t * P:(t + 1) * P], const("fold"),
                              start=True, stop=True)
                last.then_inc(fin_ready, 1)

            run(patch=patch, texts=texts, image=image, proj=proj, lora=lora, cum=cum, hats=hats, products=products,
                turn=turn, apply=apply, lt=lt, tlt=tlt, out=out, scan_a=scan_a, scan_b=scan_b, heads=heads, att=att,
                feat=feat, rank=rank, weights=weights, experts=experts, total=total, fold=fold)


def kernel(**inputs):
    import numpy as _np
    import concourse.bacc as _bacc
    from concourse import mybir as _mybir
    from concourse.bass_utils import run_bass_kernel_spmd as _run

    w = {name.replace("L0_", ""): _np.asarray(a) for name, a in inputs.items()}

    def packed(height, layout, width, **parts):
        t = _np.zeros((height, width), _np.float32)
        for name, a in parts.items():
            t[:a.shape[0], layout[name]] = a
        return t

    def twice(a):
        return _np.concatenate([a, a], 0)

    def diagonal(a):
        t = _np.zeros((2, D, 2, D), _np.float32)
        t[0, :, 0] = t[1, :, 1] = a
        return t.reshape(P, P)

    side = IMG // 8
    patches = w["x"].reshape(BATCH, 3, side, 8, side, 8).transpose(0, 2, 4, 3, 5, 1).reshape(BATCH, IMG, PATCH)
    patches = patches.reshape(G, J, NIMG, C, PATCH).transpose(1, 3, 2, 0, 4).reshape(P, NIMG * G, PATCH)
    text = _np.zeros((BATCH, NTXT * C, D), _np.float32)
    text[:, :TXT] = w["txt"]
    text = text.reshape(G, J, NTXT, C, D).transpose(1, 3, 2, 0, 4).reshape(P, NTXT * G, D)

    rows = packed(1, ROWS, NROWS, b1=w["tok_b1"][None], bp1=w["tok_bp1"][None], bp2=w["tok_bp2"][None],
                  k_k=w["attn_k_k"][None], k_a=w["attn_k_a"][None], r_k=w["attn_r_k"][None],
                  gn_w=w["attn_gn_w"][None], gn_b=w["attn_gn_b"][None], b_a=w["attn_b_a"][None],
                  bg=w["ffn_bg"][None], bias=w["ffn_bias"][None])
    cols = packed(P, COLS, NCOLS, ln1_g=w["tok_ln1_g"].reshape(2, PH).T, ln1_b=w["tok_ln1_b"].reshape(2, PH).T,
                  ln2_g=twice(w["tok_ln2_g"][:, None]), ln2_b=twice(w["tok_ln2_b"][:, None]),
                  lnp_g=twice(w["tok_lnp_g"][:, None]), lnp_b=twice(w["tok_lnp_b"][:, None]),
                  mix=twice(w["attn_x_mix"].T), b1e=w["ffn_b1"].T)
    tokw = packed(P, TOKW, NTOKW, W1=w["tok_W1"].reshape(2, PH, D).transpose(1, 0, 2).reshape(PH, 2 * D),
                  Wp1=diagonal(w["tok_Wp1"]), Wp2=diagonal(w["tok_Wp2"]))
    b2 = _np.zeros((2, E, P), _np.float32)
    b2[:, :, :D] = w["ffn_b2"]
    attw = packed(P, ATTW, NATTW, rkv=twice(_np.concatenate([w["attn_W_r"], w["attn_W_k"], w["attn_W_v"]], 1)),
                  A_w=twice(w["attn_A_w"]), A_g=twice(w["attn_A_g"]),
                  A_aT=_np.concatenate([w["attn_A_a"].T] * 2, 1), B_a=w["attn_B_a"],
                  B_w=_np.concatenate([w["attn_B_w"], w["attn_b_w"][None]], 0), B_g=w["attn_B_g"],
                  W_o=diagonal(w["attn_W_o"]), Wg=twice(w["ffn_Wg"]), b2=b2.reshape(2 * E, P))
    w1 = twice(w["ffn_W1"].transpose(1, 0, 2).reshape(D, E * EH))
    w2 = w["ffn_W2"].transpose(1, 0, 2).reshape(EH, E * D)

    nc = _bacc.Bacc("TRN2", target_bir_lowering=False, num_devices=1)
    arrays, args = {}, []
    for name, a in (("patches", patches), ("text", text), ("consts", constants()), ("pick", picks()),
                    ("rows", rows), ("cols", cols), ("tokw", tokw), ("attw", attw), ("w1", w1), ("w2", w2)):
        a = _np.ascontiguousarray(a)
        arrays[f"in_{name}"] = a
        args.append(nc.dram_tensor(f"in_{name}", a.shape, _mybir.dt.from_np(a.dtype), kind="ExternalInput").ap())
    out = nc.dram_tensor("out_h", (P, NCH * G * D), F32, kind="ExternalOutput").ap()
    build(nc, *args, out)
    r = _run(nc, [arrays], core_ids=[0])
    got = r.results[0]["out_h"].reshape(J, C, NCH, G, D).transpose(3, 0, 2, 1, 4).reshape(BATCH, NCH * C, D)
    return got[:, :SEQ]
```
